# Optimizing a Trainium2 kernel written in Bass

```python
import numpy as np
import jax
import jax.numpy as jnp

def _softmax(x, axis=-1):
    return jax.nn.softmax(x, axis=axis)

def _gelu(x):
    return jax.nn.gelu(x, approximate=True)

def _silu(x):
    return jax.nn.silu(x)

def _sigmoid(x):
    return jax.nn.sigmoid(x)

def _layernorm(x, axis=-1, eps=1e-05):
    m = jnp.mean(x, axis=axis, keepdims=True)
    v = jnp.var(x, axis=axis, keepdims=True)
    return (x - m) / jnp.sqrt(v + eps)

def _scatter_add(tgt, idx, src, axis=0):
    return tgt.at[idx].add(src)

def _segment_sum(src, seg, n):
    return jax.ops.segment_sum(src, seg, n)
kernel_name = 'mk_xattn_ffn_d1_seqx_r4_22b2cf'

def setup_inputs(seed: int=0):
    np.random.seed(seed)
    _w = jnp.asarray

    def _rec_inputs():
        import jax
        import jax.numpy as jnp
        _rk = jax.random.key(seed)
        x = 7.22e-05 + 1 * jax.random.normal(jax.random.fold_in(_rk, 1), (16, 256, 256), jnp.float32)
        _lenS = 256 - jax.random.randint(jax.random.fold_in(_rk, 7), (16,), 0, max(1, 256 // 4) + 1, jnp.int32)
        _lenS2 = 120 - jax.random.randint(jax.random.fold_in(_rk, 8), (16,), 0, max(1, 120 // 4) + 1, jnp.int32)
        _ctx_1024P = jax.random.normal(jax.random.fold_in(_rk, 11), (16, 16, 256), jnp.float32)
        _ctx_1024c = jax.random.dirichlet(jax.random.fold_in(_rk, 511), 0.3 * jnp.ones((16,), jnp.float32), (16, 120))
        _ctx_1024t = jnp.einsum('bsk,bkd->bsd', _ctx_1024c, _ctx_1024P)
        _ctx_1024t = _ctx_1024t * jax.lax.rsqrt(jnp.mean(jnp.square(_ctx_1024t)) + 1e-12) * 0.953939
        ctx_1024 = 4.13588e-05 + 0.999923 * (_ctx_1024t + 0.3 * jax.random.normal(jax.random.fold_in(_rk, 611), (16, 120, 256), jnp.float32))
        return (x, ctx_1024)
    x, ctx_1024 = _rec_inputs()

    def _L0_xattn_setup():
        import jax, jax.numpy as jnp
        import numpy as np
        import math
        B, SQ, SK, D = (4, 512, 512, 256)
        key = jax.random.key(seed)
        ks = jax.random.split(key, 9)
        s = 1.0 / math.sqrt(D)
        return {'q': jax.random.normal(ks[0], (B, SQ, D), jnp.float32), 'k': jax.random.normal(ks[1], (B, SK, D), jnp.float32), 'v': jax.random.normal(ks[2], (B, SK, D), jnp.float32), 'Wq': jax.random.normal(ks[3], (D, D), jnp.float32) * s, 'bq': jax.random.normal(ks[4], (D,), jnp.float32) * s, 'Wk': jax.random.normal(ks[5], (D, D), jnp.float32) * s, 'bk': jax.random.normal(ks[6], (D,), jnp.float32) * s, 'Wv': jax.random.normal(ks[7], (D, D), jnp.float32) * s, 'bv': jax.random.normal(ks[8], (D,), jnp.float32) * s}
    _L0_xattn_all = _L0_xattn_setup()
    _L0_xattn_in = {k: v for k, v in _L0_xattn_all.items() if k in ('Wq', 'bq', 'Wk', 'bk', 'Wv', 'bv')}
    del _L0_xattn_all

    def _L0_ffn_setup():
        import jax, jax.numpy as jnp
        import numpy as np
        E = 8
        TOP_K = 2
        H = 256
        F = 1024
        LN_EPS = 1e-12
        key = jax.random.key(seed)
        ks = jax.random.split(key, 9)
        s = lambda k, shape, scale: jax.random.normal(k, shape, dtype=jnp.float32) * scale
        return {'hidden_states': s(ks[0], (4, 512, H), 1.0), 'Wr': s(ks[1], (E, H), 0.02), 'br': jnp.zeros((E,), jnp.float32), 'W1': s(ks[2], (E, F, H), 0.02), 'b1': jnp.zeros((E, F), jnp.float32), 'W2': s(ks[3], (E, H, F), 0.02), 'b2': jnp.zeros((E, H), jnp.float32), 'ln_w': jnp.ones((H,), jnp.float32), 'ln_b': jnp.zeros((H,), jnp.float32)}
    _L0_ffn_all = _L0_ffn_setup()
    _L0_ffn_in = {k: v for k, v in _L0_ffn_all.items() if k in ('Wr', 'br', 'W1', 'b1', 'W2', 'b2', 'ln_w', 'ln_b')}
    del _L0_ffn_all
    return {'x': x, 'ctx_1024': ctx_1024, 'L0_xattn_Wq': _L0_xattn_in['Wq'], 'L0_xattn_bq': _L0_xattn_in['bq'], 'L0_xattn_Wk': _L0_xattn_in['Wk'], 'L0_xattn_bk': _L0_xattn_in['bk'], 'L0_xattn_Wv': _L0_xattn_in['Wv'], 'L0_xattn_bv': _L0_xattn_in['bv'], 'L0_ffn_Wr': _L0_ffn_in['Wr'], 'L0_ffn_br': _L0_ffn_in['br'], 'L0_ffn_W1': _L0_ffn_in['W1'], 'L0_ffn_b1': _L0_ffn_in['b1'], 'L0_ffn_W2': _L0_ffn_in['W2'], 'L0_ffn_b2': _L0_ffn_in['b2'], 'L0_ffn_ln_w': _L0_ffn_in['ln_w'], 'L0_ffn_ln_b': _L0_ffn_in['ln_b']}

def reference(x, ctx_1024, L0_xattn_Wq, L0_xattn_bq, L0_xattn_Wk, L0_xattn_bk, L0_xattn_Wv, L0_xattn_bv, L0_ffn_Wr, L0_ffn_br, L0_ffn_W1, L0_ffn_b1, L0_ffn_W2, L0_ffn_b2, L0_ffn_ln_w, L0_ffn_ln_b):
    import jax
    import jax.numpy as jnp

    def _L0_xattn_ref(q, k, v, Wq, bq, Wk, bk, Wv, bv):
        import jax, jax.numpy as jnp
        import numpy as np
        import math
        B, SQ, SK, D = (4, 512, 512, 256)
        qp = jnp.einsum('bsd,ed->bse', q, Wq) + bq
        kp = jnp.einsum('bsd,ed->bse', k, Wk) + bk
        vp = jnp.einsum('bsd,ed->bse', v, Wv) + bv
        scale = 1.0 / jnp.sqrt(jnp.asarray(kp.shape[-1], qp.dtype))
        scores = jnp.einsum('bqd,bkd->bqk', qp, kp) * scale
        attn = jax.nn.softmax(scores, axis=-1)
        return jnp.einsum('bqk,bkd->bqd', attn, vp)

    def _L0_ffn_ref(hidden_states, Wr, br, W1, b1, W2, b2, ln_w, ln_b):
        import jax, jax.numpy as jnp
        import numpy as np
        E = 8
        TOP_K = 2
        H = 256
        F = 1024
        LN_EPS = 1e-12
        bsz, seqlen, h = hidden_states.shape
        x = hidden_states.reshape(-1, h)
        logits = x @ Wr.T + br
        topk_vals, topk_idx = jax.lax.top_k(logits, TOP_K)
        topk_w = jax.nn.softmax(topk_vals, axis=-1)
        out = jnp.zeros_like(x)
        for e in range(E):
            cw = jnp.sum(topk_w * (topk_idx == e), axis=-1)
            y = jax.nn.gelu(x @ W1[e].T + b1[e], approximate=False) @ W2[e].T + b2[e]
            out = out + cw[:, None] * y
        z = out + x
        mu = jnp.mean(z, axis=-1, keepdims=True)
        var = jnp.mean(jnp.square(z - mu), axis=-1, keepdims=True)
        z = (z - mu) * jax.lax.rsqrt(var + LN_EPS) * ln_w + ln_b
        return z.reshape(bsz, seqlen, h)
    x = x + _L0_xattn_ref(_layernorm(x, axis=-1), ctx_1024, ctx_1024, L0_xattn_Wq, L0_xattn_bq, L0_xattn_Wk, L0_xattn_bk, L0_xattn_Wv, L0_xattn_bv)
    x = x + _L0_ffn_ref(_layernorm(x, axis=-1), L0_ffn_Wr, L0_ffn_br, L0_ffn_W1, L0_ffn_b1, L0_ffn_W2, L0_ffn_b2, L0_ffn_ln_w, L0_ffn_ln_b)
    return x

_drawn_inputs = setup_inputs


def setup_inputs(seed=0):
    import zlib

    import numpy as np

    out = dict(_drawn_inputs(seed))
    spreads = {'L0_ffn_br': (0.0, 0.1),
     'L0_ffn_b1': (0.0, 0.676),
     'L0_ffn_b2': (0.0, 0.1),
     'L0_ffn_ln_w': (1.0, 0.2),
     'L0_ffn_ln_b': (0.0, 0.1)}
    factors = {'L0_xattn_bq': 4.64, 'L0_xattn_bk': 8.0}
    for name, (base, spread) in spreads.items():
        noise = np.random.default_rng([zlib.crc32(name.encode()), seed]).standard_normal(out[name].shape)
        drawn = base * np.exp(spread * noise) if base else spread * noise
        out[name] = jnp.asarray(drawn.astype(out[name].dtype))
    for name, factor in factors.items():
        out[name] = (out[name] * factor).astype(out[name].dtype)
    return out
```

```python
from contextlib import ExitStack

import concourse.bass as bass
from concourse import mybir

F32 = mybir.dt.float32
F16 = mybir.dt.float16
BF16 = mybir.dt.bfloat16
I32 = mybir.dt.int32
U32 = mybir.dt.uint32
ALU = mybir.AluOpType
ACT = mybir.ActivationFunctionType
AX = mybir.AxisListType

P = 128
EPS_LN = 1e-5
EPS_FFN = 1e-12
W_SCALE = 64.0


def at_least(eng, sem, n):
    if not (isinstance(n, int) and n <= 0):
        eng.wait_ge(sem, n)


def alone(eng, sem, n, tally):
    if not (isinstance(n, int) and n <= 0):
        eng.wait_ge(sem, n)
        eng.sem_inc(tally, 1)


def build(nc, x, ctx_in, Wq, bq, Wk, bk, Wv, bv, Wr, br, W1, b1, W2, b2, ln_w, ln_b, out):
    NB, SQ, D = x.shape
    SK = ctx_in.shape[1]
    E, FF, _ = W1.shape
    KD = D // P
    KF = FF // P
    TJ = SQ // P
    NT = NB * TJ
    TOK = NB * SQ
    TOPK = 2
    BLOCKS = TOPK * TOK // P + E - 1
    PER_EXPERT = TOK // P
    TABLE = E * PER_EXPERT + E
    SCALE = float(D) ** -0.5
    assert KD == 2 and TJ == 2 and NB == 2 * E and BLOCKS % 2 == 1 and SK <= P

    slot_table = nc.dram_tensor("slot_table", (TABLE * P, 2), I32).ap()
    tokens_dram = nc.dram_tensor("tokens_dram", (TOK, D), F32).ap()
    expert_rows = nc.dram_tensor("expert_rows", (TOPK * TOK + TABLE * P, D), F32).ap()

    x_v = x.rearrange("b (j p) d -> p b j d", p=P)
    out_v = out.rearrange("b (j p) d -> p b j d", p=P)
    ctx_v = ctx_in.rearrange("b s d -> s b d")
    w1_v = W1.rearrange("e (c p) d -> p e c d", p=P)
    w2_v = W2.rearrange("e (k p) f -> p e k f", p=P)
    tok_v = tokens_dram.rearrange("(b j p) d -> p b j d", p=P, j=TJ)
    first_v = expert_rows[0:TOK, :].rearrange("(b j p) d -> p b j d", p=P, j=TJ)
    second_v = expert_rows[TOK:2 * TOK, :].rearrange("(b j p) d -> p b j d", p=P, j=TJ)
    table_v = slot_table.rearrange("(t q) c -> t (q c)", q=P)

    with ExitStack() as stack:
        def sb(name, shape, dt=F32):
            return stack.enter_context(nc.sbuf_tensor(name, shape, dt))

        def sem(name):
            return stack.enter_context(nc.semaphore(name))

        def sem2(name):
            return [sem(f"{name}{i}") for i in range(2)]

        WE = KF * D
        w1hi = sb("w1hi", [P, E * WE], F16)
        w1lo = sb("w1lo", [P, E * WE], F16)
        w2hi = sb("w2hi", [P, E * WE], F16)
        w2lo = sb("w2lo", [P, E * WE], F16)
        x1 = sb("x1", [P, NB, TJ, D])
        ident = sb("ident", [P, P])
        ones = sb("ones", [P, P])
        before = sb("before", [P, P], BF16)
        ones_bf = sb("ones_bf", [P, P], BF16)
        iota8 = sb("iota8", [P, E])
        slot0 = sb("slot0", [P, E])
        minus_half = sb("minus_half", [P, TJ])
        ids = sb("ids", [P, NT * TOPK, 2], I32)
        mt = sb("mt", [P, KD, D])
        wv_ext = sb("wv_ext", [P, KD, D + 1])
        wrt = sb("wrt", [P, KD, E])
        g_col = sb("g_col", [P, KD])
        ident_c = sb("ident_c", [P, P])
        bv_bc = sb("bv_bc", [P, D])
        br_bc = sb("br_bc", [P, E])
        b1t = sb("b1t", [P, E * KF])
        stage = [sb(f"stage{i}", [P, KF * D]) for i in range(2)]
        wqkv = stage[0][:, 0:3 * KD * D].rearrange("p (w k d) -> p w k d", w=3, k=KD)
        wr_in = stage[1][0:E, 0:D]
        b1_in = stage[1][0:E * KF, D:D + P]
        bqk = sb("bqk", [P, 2, KD])
        bq_rep = stage[1][:, 1024:1024 + KD * P].rearrange("p (k q) -> p k q", k=KD)
        c_col = sb("c_col", [P, 1])
        PADS = -(-TABLE // P)
        pad_rows = [sb_at.bitcast(I32).rearrange("p (q c) -> p q c", c=2)
                    for sb_at in (stage[0][:, 1536:1792], stage[0][:, 1792:2048], stage[1][:, 1536:1792])]
        ctx_sb = [sb(f"ctx_sb{i}", [P, D]) for i in range(2)]
        st1 = sb("st1", [P, TJ, 6])
        st2 = sb("st2", [P, TJ, 6])
        mv1 = [sb(f"mv1_{i}", [P, TJ, 2]) for i in range(2)]
        mv2 = [sb(f"mv2_{i}", [P, TJ, 2]) for i in range(2)]
        ve1, ve2, ve3, nmu1, nmu2, nmu3 = (sb(n, [P, TJ]) for n in ("ve1", "ve2", "ve3", "nmu1", "nmu2", "nmu3"))
        rn1 = sb("rn1", [P, 2, TJ])
        rn2 = sb("rn2", [P, NB, 2, TJ])
        xn = [sb(f"xn{i}", [P, TJ, D]) for i in range(2)]
        xn2 = [sb(f"xn2_{i}", [P, TJ, D]) for i in range(2)]
        xnt = sb("xnt", [P, KD, SQ])
        work = sb("work", [P, KD * SQ + 2 * KD * SK + 2 * D + 2 * SK + TJ * SK + TJ * P])
        cut = [0]

        def piece(rows, cols):
            cut[0] += cols
            return work[0:rows, cut[0] - cols:cut[0]]

        xn2t = piece(P, KD * SQ).rearrange("p (k q) -> p k q", k=KD)
        ctxt = piece(P, KD * SK).rearrange("p (k s) -> p k s", k=KD)
        kt = piece(P, KD * SK).rearrange("p (k s) -> p k s", k=KD)
        v_sb = [piece(SK, D) for i in range(2)]
        s_diag = [piece(SK, SK) for i in range(2)]
        top = sb("top", [P, TJ])
        neg = sb("neg", [P, TJ])
        probs = piece(P, TJ * SK).rearrange("p (j s) -> p j s", j=TJ)
        psum_p = sb("psum_p", [P, TJ])
        rinv = sb("rinv", [P, TJ])
        pt = piece(SK, TJ * P).rearrange("p (j q) -> p j q", j=TJ)
        lg = sb("lg", [P, TJ, E])
        mx = sb("mx", [P, TJ, E])
        ix = sb("ix", [P, TJ, E], U32)
        ixf = sb("ixf", [P, TJ, TOPK])
        oh = sb("oh", [P, TJ, TOPK, E])
        chosen = sb("chosen", [P, TJ, E], BF16)
        seen = sb("seen", [P, E], BF16)
        slot_e = sb("slot_e", [P, TJ, E])
        prod = sb("prod", [P, TJ, TOPK, E])
        slotf = sb("slotf", [P, TJ * TOPK])
        slots = [sb(f"slots{i}", [P, TJ * TOPK], I32) for i in range(2)]
        rows_now = [sb(f"rows_now{i}", [P, TJ * TOPK, 2], I32) for i in range(2)]
        vals = sb("vals", [P, NB, TJ, TOPK])
        gate = sb("gate", [P, NB, TJ, TOPK])
        gexp = stage[0][:, 900:900 + NT]
        gsum = stage[0][:, 950:950 + NT]
        cnt = sb("cnt", [P, E], I32)
        nblk_i = sb("nblk_i", [P, E], I32)
        nblk = sb("nblk", [P, E])
        endb = [sb(f"endb{i}", [P, E]) for i in range(4)]
        jota = sb("jota", [P, BLOCKS])
        passed = stage[0][:, 0:BLOCKS * E].rearrange("p (t e) -> p t e", e=E)
        skipped = stage[0][:, 1024:1024 + BLOCKS * E].rearrange("p (t e) -> p t e", e=E)
        eidf = stage[0][:, 600:600 + BLOCKS]
        firstf = stage[0][:, 700:700 + BLOCKS]
        rowf = stage[0][:, 800:800 + BLOCKS]
        eid = xn[1][:, 1, 0:BLOCKS].bitcast(I32)
        row = xn[1][:, 1, P:P + BLOCKS].bitcast(I32)
        idx_all = xn[0][:, 1, 0:2 * BLOCKS].bitcast(I32).rearrange("p (t c) -> p t c", c=2)
        gidx = [sb(f"gidx{i}", [P, 1], I32) for i in range(2)]
        sidx = [sb(f"sidx{i}", [P, 1], I32) for i in range(2)]
        b1s = [sb(f"b1s{i}", [P, KF]) for i in range(2)]
        b2_bc = work[:, 0:E * D]
        lnw_bc, lnb_bc = ctx_sb[0], ctx_sb[1]
        xg = [xn[i][:, 0, :] for i in range(2)]
        y_sb = [xn2[i][:, 0, :] for i in range(2)]
        xnt_q = xnt[:, :, :].rearrange("p k q -> p (k q)").bitcast(F16).rearrange("p (i k q) -> p i k q", i=4, k=KD)
        xhi = [xnt_q[:, i, :, :] for i in range(2)]
        xlo = [xnt_q[:, 2 + i, :, :] for i in range(2)]
        h32 = [stage[i][:, 0:KF * P] for i in range(2)]
        hhi = [stage[i][:, KF * P:KF * P * 3 // 2].bitcast(F16) for i in range(2)]
        hlo = [stage[i][:, KF * P * 3 // 2:KF * P * 2].bitcast(F16) for i in range(2)]
        first = w1hi[:, :].bitcast(F32).rearrange("p (b j d) -> p b j d", b=NB, j=TJ)
        second = w1lo[:, :].bitcast(F32).rearrange("p (b j d) -> p b j d", b=NB, j=TJ)
        w2hi_f = w2hi[:, :].bitcast(F32).rearrange("p (n d) -> p n d", d=D)
        z_sb = [w2hi_f[:, 2 * i:2 * i + 2, :] for i in range(2)]
        zn_sb = [w2hi_f[:, 4 + 2 * i:6 + 2 * i, :] for i in range(2)]
        xf_sb = [w2hi_f[:, 8 + 2 * i:10 + 2 * i, :] for i in range(2)]
        zw_sb = [w2hi_f[:, 12 + 2 * i:14 + 2 * i, :] for i in range(2)]
        o_sb = [w2hi_f[:, 16 + 2 * i:18 + 2 * i, :] for i in range(2)]
        st3 = sb("st3", [P, TJ, 6])
        mv3 = [sb(f"mv3_{i}", [P, TJ, 2]) for i in range(2)]
        rn3 = [sb(f"rn3_{i}", [P, 2, TJ]) for i in range(2)]

        bank = [stack.enter_context(nc.psum_tensor(f"bank{i}", [P, 512], F32)) for i in range(8)]
        b_x = bank[0][:, :].rearrange("p (k q) -> p k q", k=KD)
        b_ctxt = bank[1][:, 0:KD * SK].rearrange("p (k s) -> p k s", k=KD)
        b_kt = bank[1][:, 256:256 + KD * SK].rearrange("p (k s) -> p k s", k=KD)
        b_v = bank[2][0:SK, 0:D + 1]
        b_s = bank[3][:, 0:TJ * SK].rearrange("p (j s) -> p j s", j=TJ)
        b_pt = bank[3][0:SK, 256:512].rearrange("p (j q) -> p j q", j=TJ)
        b_o = bank[4][:, :].rearrange("p (j d) -> p j d", j=TJ)
        b_lg = bank[5][:, 0:TJ * E].rearrange("p (j e) -> p j e", j=TJ)
        b_rank = bank[5][:, 64:64 + TJ * E].rearrange("p (j e) -> p j e", j=TJ)
        b_w = [bank[6][:, :], bank[7][:, :]]
        f_h = [[bank[0], bank[1]], [bank[2], bank[3]]]
        f_x = bank[4][:, 0:KD * P].rearrange("p (k q) -> p k q", k=KD)
        f_y = [bank[5][:, 0:D], bank[6][:, 0:D]]

        consts_pool = sem("consts_pool")
        pool_self = sem("pool_self")
        proj_w_loaded = sem("proj_w_loaded")
        small_loaded = sem("small_loaded")
        late_loaded = sem("late_loaded")
        table_blank = sem("table_blank")
        bq_spread = sem("bq_spread")
        setup_mm = sem("setup_mm")
        setup_ev = sem("setup_ev")
        x_loaded = sem2("x_loaded")
        ctx_loaded = sem2("ctx_loaded")
        w_loaded = sem2("w_loaded")
        stats1 = sem("stats1")
        stats2 = sem("stats2")
        dve_self = sem("dve_self")
        xn_ready = sem("xn_ready")
        rn1_ready = sem("rn1_ready")
        rn2_ready = sem("rn2_ready")
        xn2_ready = sem("xn2_ready")
        xn2_stored = sem2("xn2_stored")
        ctxt_mm = sem("ctxt_mm")
        ctxt_ready = sem("ctxt_ready")
        k_mm = sem("k_mm")
        kt_ready = sem("kt_ready")
        v_mm = sem("v_mm")
        v_ready = sem("v_ready")
        xt_mm = sem("xt_mm")
        xnt_ready = sem("xnt_ready")
        s_mm = sem("s_mm")
        max_ready = sem("max_ready")
        exp_ready = sem("exp_ready")
        pt_mm = sem("pt_mm")
        pt_ready = sem("pt_ready")
        o_mm = sem("o_mm")
        x1_ready = sem("x1_ready")
        x2t_mm = sem("x2t_mm")
        xn2t_ready = sem("xn2t_ready")
        lg_mm = sem("lg_mm")
        chosen_ready = sem("chosen_ready")
        rank_mm = sem("rank_mm")
        slots_ready = sem("slots_ready")
        seen_ready = sem("seen_ready")
        rows_copied = sem("rows_copied")
        published = sem2("published")
        w_mm = sem("w_mm")
        whi_ready = sem("whi_ready")
        wlo_ready = sem("wlo_ready")
        count_mm = sem("count_mm")
        blocks_ready = sem("blocks_ready")
        gate_diff = sem("gate_diff")
        gate_exp = sem("gate_exp")
        idx_loaded = sem2("idx_loaded")
        gidx_ready = sem("gidx_ready")
        sidx_ready = sem("sidx_ready")
        b1_staged = sem("b1_staged")
        gathered = sem2("gathered")
        xg_mm = sem("xg_mm")
        xhi_ready = sem("xhi_ready")
        xlo_ready = sem("xlo_ready")
        h_mm = sem("h_mm")
        gelu_ready = sem("gelu_ready")
        hhi_ready = sem("hhi_ready")
        split_ready = sem("split_ready")
        y_mm = sem("y_mm")
        y_ready = sem("y_ready")
        scattered = sem2("scattered")
        rows_loaded = sem2("rows_loaded")
        xf_ready = sem("xf_ready")
        z_ready = sem("z_ready")
        stats3 = sem("stats3")
        rn3_ready = sem("rn3_ready")
        zn_ready = sem("zn_ready")
        zw_ready = sem("zw_ready")
        o_ready = sem("o_ready")
        stored = sem2("stored")

        norm_self = sem("norm_self")
        tally_dve = sem("tally_dve")
        tally_pool = sem("tally_pool")
        stats_self = sem("stats_self")
        max_self = sem("max_self")
        top_self = sem("top_self")
        slot_self = sem("slot_self")
        z_self = sem("z_self")
        affine_self = sem("affine_self")

        block = stack.enter_context(nc.Block())

        N_SMALL = 6
        PEEL = 6
        ROUTED = 64

        def steps(eng, step, last):
            def one(m, u):
                back = [(m, u), (m, 0) if u else (m - 1, 1), (m - 1, u), (m - 1, 0) if u else (m - 2, 1)]
                t = 2 * m + u
                if isinstance(t, int):
                    back = [b if 0 <= t - d < NB else None for d, b in enumerate(back)]
                step(*back)
            for t in range(PEEL):
                one(t // 2, t % 2)
            with eng.Fori(PEEL // 2, NB // 2) as m:
                one(m, 0)
                one(m, 1)
            for t in range(NB, NB + last):
                one(t // 2, t % 2)

        @block.sync
        def _(sp):
            for w, src in enumerate((Wq, Wk, Wv)):
                sp.dma_start(wqkv[:, w, :, :], src.rearrange("(k p) d -> p k d", p=P)).then_inc(proj_w_loaded, 16)
            with nc.allow_non_contiguous_dma(reason="two short bias columns"):
                sp.dma_start(bqk[:, 0, :], bq.rearrange("(k p) -> p k", p=P)).then_inc(small_loaded, 16)
                sp.dma_start(bqk[:, 1, :], bk.rearrange("(k p) -> p k", p=P)).then_inc(small_loaded, 16)
            sp.dma_start(wr_in, Wr).then_inc(small_loaded, 16)
            sp.dma_start(b1_in, b1.rearrange("e (c p) -> (e c) p", p=P)).then_inc(small_loaded, 16)
            sp.dma_start(bv_bc[:, :], bv.partition_broadcast(P)).then_inc(small_loaded, 16)
            sp.dma_start(br_bc[:, :], br.partition_broadcast(P)).then_inc(small_loaded, 16)
            sp.wait_ge(consts_pool, 1)
            for i in range(PADS):
                n = min(P, TABLE - i * P)
                sp.dma_start(table_v[i * P:i * P + n, :], pad_rows[i][0:n].rearrange("p q c -> p (q c)")).then_inc(table_blank, 16)

            def load(project, attend, route, publish):
                if project is None:
                    return
                m, p = project
                b = 2 * m + p
                at_least(sp, x_loaded[p], 16 * m)
                sp.dma_start(x1[:, bass.ds(b, 1), :, :].rearrange("p a j d -> p (a j) d"), x_v[:, bass.ds(b, 1), :, :].rearrange("p a j d -> p (a j) d")).then_inc(x_loaded[p], 16)
                at_least(sp, ctxt_mm, b - 1)
                sp.dma_start(ctx_sb[p][0:SK, :], ctx_v[:, bass.ds(b, 1), :].rearrange("p a d -> p (a d)")).then_inc(ctx_loaded[p], 16)
                at_least(sp, w_mm, 4 * (b - 1))
                if isinstance(m, int) and m == 0:
                    sp.wait_ge(setup_mm, 5)
                    sp.wait_ge(table_blank, 16 * PADS)
                src = w2_v if p else w1_v
                sp.dma_start(stage[p][:, :].rearrange("p (c d) -> p c d", c=KD if p else KF),
                             src[:, bass.ds(m, 1), :, :].rearrange("p a c d -> p (a c) d")).then_inc(w_loaded[p], 16)

            steps(sp, load, 0)

            for p in range(2):
                sp.wait_ge(published[p], ROUTED * NB // 2)
            sp.wait_ge(blocks_ready, 1)

            def load_rows(m, p):
                j = 2 * m + p
                at_least(sp, idx_loaded[p], 16 * m)
                r = sp.value_load(row[0:1, bass.ds(j, 1)], min_val=0, max_val=TABLE - 1)
                sp.dma_start(idx_all[:, bass.ds(j, 1), :].rearrange("p a c -> p (a c)"),
                             slot_table[bass.ds(r * P, P), :]).then_inc(idx_loaded[p], 16)

            sp.dma_start(b2_bc, b2.rearrange("e d -> (e d)").partition_broadcast(P)).then_inc(late_loaded, 16)
            sp.dma_start(lnw_bc[:, :], ln_w.partition_broadcast(P)).then_inc(late_loaded, 16)
            sp.dma_start(lnb_bc[:, :], ln_b.partition_broadcast(P)).then_inc(late_loaded, 16)
            for p in range(2):
                load_rows(0, p)
            with sp.Fori(1, BLOCKS // 2) as m:
                load_rows(m, 0)
                load_rows(m, 1)
            load_rows(BLOCKS // 2, 0)

            sp.wait_ge(scattered[0], 16 * (BLOCKS // 2 + 1))
            sp.wait_ge(scattered[1], 16 * (BLOCKS // 2))

            def load_pair(m, p):
                b = 2 * m + p
                at_least(sp, rows_loaded[p], 32 * m)
                for dst, src in ((first, first_v), (second, second_v)):
                    sp.dma_start(dst[:, bass.ds(b, 1), :, :].rearrange("p a j d -> p (a j) d"),
                                 src[:, bass.ds(b, 1), :, :].rearrange("p a j d -> p (a j) d")).then_inc(rows_loaded[p], 16)

            def store(m, p):
                b = 2 * m + p
                sp.wait_ge(o_ready, b + 1)
                sp.dma_start(out_v[:, bass.ds(b, 1), :, :].rearrange("p a j d -> p (a j) d"), o_sb[p]).then_inc(stored[p], 16)

            for m in range(2):
                for p in range(2):
                    load_pair(m, p)
            with sp.Fori(0, NB // 2 - 2) as m:
                for p in range(2):
                    load_pair(m + 2, p)
                    store(m, p)
            for m in range(NB // 2 - 2, NB // 2):
                for p in range(2):
                    store(m, p)
            for p in range(2):
                sp.wait_ge(stored[p], 16 * NB // 2)

        @block.gpsimd
        def _(pool):
            for i in range(PADS):
                nc.gpsimd.iota(pad_rows[i][:, :, 0], [[1, P]], base=0, channel_multiplier=0)
                ins = nc.gpsimd.iota(pad_rows[i][:, :, 1], [[1, P]], base=TOPK * TOK + i * P * P, channel_multiplier=P)
            ins.then_inc(consts_pool, 1)
            nc.gpsimd.memset(ident[:, :], 0.0)
            nc.gpsimd.memset(before[:, :], 1.0)
            nc.gpsimd.memset(ones[:, :], 1.0)
            nc.gpsimd.memset(ones_bf[:, :], 1.0)
            nc.gpsimd.memset(seen[:, :], 0.0)
            nc.gpsimd.memset(minus_half[:, :], -0.5).then_inc(pool_self, 1)
            pool.wait_ge(pool_self, 1)
            nc.gpsimd.affine_select(out=ident[:, :], in_=ident[:, :], compare_op=ALU.not_equal, fill=1.0, base=0,
                                    pattern=[[-1, P]], channel_multiplier=1)
            nc.gpsimd.affine_select(out=before[:, :], in_=before[:, :], compare_op=ALU.is_gt, fill=0.0, base=0,
                                    pattern=[[1, P]], channel_multiplier=-1)
            nc.gpsimd.iota(iota8[:, :], [[1, E]], base=0, channel_multiplier=0, allow_small_or_imprecise_dtypes=True)
            nc.gpsimd.iota(slot0[:, :], [[TOK, E]], base=0, channel_multiplier=0, allow_small_or_imprecise_dtypes=True)
            nc.gpsimd.iota(jota[:, :], [[1, BLOCKS]], base=0, channel_multiplier=0, allow_small_or_imprecise_dtypes=True)
            nc.gpsimd.iota(ids[:, :, 0], [[P, NT], [0, TOPK]], base=0, channel_multiplier=1)
            nc.gpsimd.iota(ids[:, :, 1], [[P, NT], [TOK, TOPK]], base=0, channel_multiplier=1).then_inc(consts_pool, 1)

            tick = [1]

            def then_self(ins):
                tick[0] += 1
                ins.then_inc(pool_self, 1)
                pool.wait_ge(pool_self, tick[0])

            def norm(count, mv, nmu, ve, scale, shift, eps, ready):
                nc.gpsimd.tensor_scalar(nmu[:, :], mv[:, :, 0], -1.0, None, ALU.mult)
                nc.gpsimd.tensor_scalar(ve[:, :], mv[:, :, 1], eps, None, ALU.add).then_inc(norm_self, 1)
                pool.wait_ge(norm_self, 2 * count + 1)
                nc.gpsimd.tensor_tensor(scale, ve[:, :], minus_half[:, :], ALU.pow).then_inc(norm_self, 1)
                pool.wait_ge(norm_self, 2 * count + 2)
                nc.gpsimd.tensor_tensor(shift, nmu[:, :], scale, ALU.mult).then_inc(ready, 1)

            def step(project, attend, route, publish):
                if project is not None:
                    m, p = project
                    b = 2 * m + p
                    used = b + (b - 2 if not isinstance(b, int) or b >= 2 else 0)
                    at_least(pool, xn_ready, b)
                    alone(pool, stats1, b + 1, tally_pool)
                    norm(used, mv1[p], nmu1, ve1, rn1[:, 0, :], rn1[:, 1, :], EPS_LN, rn1_ready)
                if route is not None:
                    m, p = route
                    b = 2 * m + p
                    used = 2 * b + 3 if not isinstance(b, int) or b + 3 <= NB else NB + b
                    alone(pool, stats2, b + 1, tally_pool)
                    rb = rn2[:, bass.ds(b, 1), :, :].rearrange("p a r j -> p (a r) j")
                    norm(used, mv2[p], nmu2, ve2, rb[:, 0, :], rb[:, 1, :], EPS_LN, rn2_ready)
                if publish is not None:
                    m, p = publish
                    b = 2 * m + p
                    n = TJ * TOPK
                    if isinstance(b, int) and b == 0:
                        pool.wait_ge(table_blank, 16 * PADS)
                    at_least(pool, published[p], ROUTED * m)
                    nc.gpsimd.tensor_copy(rows_now[p][:, :, :], ids[:, bass.ds(b * n, n), :]).then_inc(rows_copied, 1)
                    pool.wait_ge(rows_copied, b + 1)
                    alone(pool, slots_ready, b + 1, tally_pool)
                    for a in range(n):
                        nc.gpsimd.indirect_dma_start(
                            out=slot_table, out_offset=bass.IndirectOffsetOnAxis(ap=slots[p][:, a:a + 1], axis=0),
                            in_=rows_now[p][:, a, :], in_offset=None).then_inc(published[p], 16)

            steps(pool, step, 3)

            def fetch(m, p):
                j = 2 * m + p
                e = pool.value_load(eid[0:1, bass.ds(j, 1)], min_val=0, max_val=E - 1)
                pool.wait_ge(idx_loaded[p], 16 * (m + 1))
                at_least(pool, gathered[p], 16 * m)
                nc.gpsimd.tensor_copy(gidx[p][:, :], idx_all[:, bass.ds(j, 1), 0]).then_inc(gidx_ready, 1)
                pool.wait_ge(gidx_ready, j + 1)
                alone(pool, xg_mm, j - 1, tally_pool)
                nc.gpsimd.indirect_dma_start(
                    out=xg[p], out_offset=None, in_=tokens_dram,
                    in_offset=bass.IndirectOffsetOnAxis(ap=gidx[p][:, 0:1], axis=0)).then_inc(gathered[p], 16)
                at_least(pool, gelu_ready, 2 * (j - 1))
                nc.gpsimd.tensor_copy(b1s[p][:, :], b1t[:, bass.ds(e * KF, KF)]).then_inc(b1_staged, 1)

            def give(m, p):
                j = 2 * m + p
                at_least(pool, scattered[p], 16 * m)
                nc.gpsimd.tensor_copy(sidx[p][:, :], idx_all[:, bass.ds(j, 1), 1]).then_inc(sidx_ready, 1)
                pool.wait_ge(sidx_ready, j + 1)
                alone(pool, y_ready, j + 1, tally_pool)
                nc.gpsimd.indirect_dma_start(
                    out=expert_rows, out_offset=bass.IndirectOffsetOnAxis(ap=sidx[p][:, 0:1], axis=0),
                    in_=y_sb[p], in_offset=None).then_inc(scattered[p], 16)

            pool.wait_ge(blocks_ready, 1)
            pool.wait_ge(setup_ev, 5)
            for p in range(2):
                pool.wait_ge(xn2_stored[p], 16 * NB // 2)
            fetch(0, 0)
            fetch(0, 1)
            for p in range(2):
                fetch(1, p)
                give(0, p)
            with pool.Fori(1, BLOCKS // 2 - 1) as m:
                for p in range(2):
                    fetch(m + 1, p)
                    give(m, p)
            m = BLOCKS // 2 - 1
            fetch(m + 1, 0)
            give(m, 0)
            give(m, 1)
            give(m + 1, 0)

            def finish(m, p):
                b = 2 * m + p
                at_least(pool, zn_ready, b - 1)
                alone(pool, rn3_ready, b, tally_pool)
                alone(pool, stats3, b + 1, tally_pool)
                norm(2 * NB + b, mv3[p], nmu3, ve3, rn3[p][:, 0, :], rn3[p][:, 1, :], EPS_FFN, rn3_ready)

            def add_up(m, p):
                b = 2 * m + p
                pool.wait_ge(zw_ready, b + 1)
                at_least(pool, stored[p], 16 * m)
                nc.gpsimd.tensor_tensor(o_sb[p], zw_sb[p], x1[:, bass.ds(b, 1), :, :].rearrange("p a j d -> p (a j) d"),
                                        ALU.add).then_inc(o_ready, 1)

            finish(0, 0)
            finish(0, 1)
            add_up(0, 0)
            finish(1, 0)
            add_up(0, 1)
            with pool.Fori(1, NB // 2 - 1) as m:
                finish(m, 1)
                add_up(m, 0)
                finish(m + 1, 0)
                add_up(m, 1)
            m = NB // 2 - 1
            finish(m, 1)
            add_up(m, 0)
            add_up(m, 1)

        @block.tensor
        def _(pe):
            pe.wait_ge(consts_pool, 2)
            pe.wait_ge(proj_w_loaded, 48)
            wq, wk, wv = (wqkv[:, i, :, :] for i in range(3))
            for c in range(KD):
                for k in range(KD):
                    ins = nc.tensor.matmul(bank[c][:, 0:D], wk[:, k, c * P:(c + 1) * P], wq[:, k, :],
                                           start=(k == 0), stop=(k == KD - 1))
            ins.then_inc(setup_mm, 1)
            for k in range(KD):
                for c in range(KD):
                    ins = nc.tensor.transpose(bank[2 + c][:, k * P:(k + 1) * P], wv[:, k, c * P:(c + 1) * P], ident[:, :])
            ins.then_inc(setup_mm, 1)
            pe.wait_ge(small_loaded, 16 * N_SMALL)
            for c in range(KD):
                nc.tensor.transpose(bank[4][:, c * E:(c + 1) * E], wr_in[:, c * P:(c + 1) * P], ident[0:E, 0:E])
            nc.tensor.transpose(bank[4][:, 64:64 + E * KF], b1_in, ident[0:E * KF, 0:E * KF]).then_inc(setup_mm, 1)
            pe.wait_ge(bq_spread, 1)
            for c in range(KD):
                for k in range(KD):
                    nc.tensor.matmul(bank[5][:, c:c + 1], wk[:, k, c * P:(c + 1) * P], bqk[:, 0, k:k + 1],
                                     start=(k == 0), stop=(k == KD - 1))
            for c in range(KD):
                for k in range(KD):
                    nc.tensor.matmul(bank[5][:, 2 + c:3 + c], wq[:, k, c * P:(c + 1) * P], bqk[:, 1, k:k + 1],
                                     start=(k == 0), stop=(k == KD - 1))
            for k in range(KD):
                ins = nc.tensor.matmul(bank[5][:, 4:5], bq_rep[:, k, :], bqk[:, 1, k:k + 1],
                                       start=(k == 0), stop=(k == KD - 1))
            ins.then_inc(setup_mm, 2)
            pe.wait_ge(setup_ev, 5)

            def split_group(m, p, g):
                b = 2 * m + p
                if g == 0:
                    pe.wait_ge(w_loaded[p], 16 * (m + 1))
                n = 4 * b + g
                at_least(pe, wlo_ready, n - 1)
                for q in range(4):
                    c, k = 2 * g + q // 2, q % 2
                    col = k * FF + c * P if p else c * D + k * P
                    ins = nc.tensor.transpose(b_w[g % 2][:, q * P:(q + 1) * P], stage[p][:, col:col + P], ident[:, :])
                ins.then_inc(w_mm, 1)

            def step(project, attend, route, publish):
                if project is not None:
                    m, p = project
                    b = 2 * m + p
                    pe.wait_ge(ctx_loaded[p], 16 * (m + 1))
                    at_least(pe, kt_ready, b)
                    for k in range(KD):
                        ins = nc.tensor.transpose(b_ctxt[:, k, :], ctx_sb[p][0:SK, k * P:(k + 1) * P], ident[0:SK, 0:SK])
                    ins.then_inc(ctxt_mm, 1)
                if attend is not None:
                    ma, pa = attend
                    a = 2 * ma + pa
                    pe.wait_ge(xnt_ready, a + 1)
                    pe.wait_ge(kt_ready, a + 1)
                    pe.wait_ge(v_ready, a + 1)
                    at_least(pe, pt_ready, a)
                    for j in range(TJ):
                        for k in range(KD):
                            nc.tensor.matmul(b_s[:, j, :], xnt[:, k, j * P:(j + 1) * P], kt[:, k, :],
                                             start=(k == 0), stop=False)
                        ins = nc.tensor.matmul(b_s[:, j, :], ones[0:SK, :], s_diag[pa], start=False, stop=True)
                    ins.then_inc(s_mm, 1)
                if project is not None:
                    split_group(m, p, 0)
                    pe.wait_ge(xn_ready, b + 1)
                    at_least(pe, xn2t_ready, b - 2)
                    for k in range(KD):
                        for j in range(TJ):
                            ins = nc.tensor.transpose(b_x[:, k, j * P:(j + 1) * P], xn[p][:, j, k * P:(k + 1) * P], ident[:, :])
                    ins.then_inc(xt_mm, 1)
                    pe.wait_ge(ctxt_ready, b + 1)
                    for c in range(KD):
                        for k in range(KD):
                            ins = nc.tensor.matmul(b_kt[:, c, :], mt[:, k, c * P:(c + 1) * P], ctxt[:, k, :],
                                                   start=(k == 0), stop=(k == KD - 1))
                    ins.then_inc(k_mm, 1)
                    at_least(pe, v_ready, b)
                    for k in range(KD):
                        ins = nc.tensor.matmul(b_v, ctxt[:, k, :], wv_ext[:, k, :], start=(k == 0), stop=(k == KD - 1))
                    ins.then_inc(v_mm, 1)
                    split_group(m, p, 1)
                if attend is not None:
                    pe.wait_ge(exp_ready, a + 1)
                    for j in range(TJ):
                        ins = nc.tensor.transpose(b_pt[:, j, :], probs[:, j, :], ident[:, :])
                    ins.then_inc(pt_mm, 1)
                if route is not None:
                    mr, pr = route
                    r = 2 * mr + pr
                    pe.wait_ge(xn2_ready, r + 1)
                    pe.wait_ge(xnt_ready, min(r + 3, NB) if isinstance(r, int) else r + 3)
                    for k in range(KD):
                        for j in range(TJ):
                            ins = nc.tensor.transpose(b_x[:, k, j * P:(j + 1) * P], xn2[pr][:, j, k * P:(k + 1) * P], ident[:, :])
                    ins.then_inc(x2t_mm, 1)
                if project is not None:
                    split_group(m, p, 2)
                if attend is not None:
                    pe.wait_ge(pt_ready, a + 1)
                    at_least(pe, x1_ready, a)
                    for j in range(TJ):
                        ins = nc.tensor.matmul(b_o[:, j, :], pt[:, j, :], v_sb[pa], start=True, stop=True)
                    ins.then_inc(o_mm, 1)
                if route is not None:
                    pe.wait_ge(xn2t_ready, r + 1)
                    at_least(pe, slots_ready, r)
                    for j in range(TJ):
                        for k in range(KD):
                            ins = nc.tensor.matmul(b_lg[:, j, :], xn2t[:, k, j * P:(j + 1) * P], wrt[:, k, :],
                                                   start=(k == 0), stop=(k == KD - 1))
                    ins.then_inc(lg_mm, 1)
                if project is not None:
                    split_group(m, p, 3)
                if route is not None:
                    pe.wait_ge(chosen_ready, r + 1)
                    at_least(pe, seen_ready, r)
                    nc.tensor.matmul(b_rank[:, 0, :], before[:, :], chosen[:, 0, :], start=True, stop=False)
                    nc.tensor.matmul(b_rank[:, 0, :], ones_bf[:, :], seen[:, :], start=False, stop=True)
                    nc.tensor.matmul(b_rank[:, 1, :], before[:, :], chosen[:, 1, :], start=True, stop=False)
                    nc.tensor.matmul(b_rank[:, 1, :], ones_bf[:, :], chosen[:, 0, :], start=False, stop=False)
                    nc.tensor.matmul(b_rank[:, 1, :], ones_bf[:, :], seen[:, :], start=False, stop=True).then_inc(rank_mm, 1)

            steps(pe, step, 2)

            pe.wait_ge(seen_ready, NB)
            pe.wait_ge(slots_ready, NB)
            nc.tensor.matmul(bank[5][:, 0:E], ones_bf[:, :], seen[:, :], start=True, stop=True).then_inc(count_mm, 1)
            pe.wait_ge(xn2t_ready, NB)
            pe.wait_ge(wlo_ready, 4 * NB)
            pe.wait_ge(blocks_ready, 1)

            def turn(m, p):
                j = 2 * m + p
                pe.wait_ge(gathered[p], 16 * (m + 1))
                at_least(pe, xlo_ready, j)
                for k in range(KD):
                    ins = nc.tensor.transpose(f_x[:, k, :], xn[p][:, 0, k * P:(k + 1) * P], ident[:, :])
                ins.then_inc(xg_mm, 1)

            def up(m, p):
                j = 2 * m + p
                e = pe.value_load(eid[0:1, bass.ds(j, 1)], min_val=0, max_val=E - 1)
                pe.wait_ge(xlo_ready, j + 1)
                for c in range(KF):
                    dst = f_h[p][c // 4][:, (c % 4) * P:(c % 4 + 1) * P]
                    if c % 4 == 0:
                        at_least(pe, gelu_ready, 2 * (j - 2) + c // 4 + 1)
                    for k in range(KD):
                        col = bass.ds(e * WE + (c * D + k * P), P)
                        nc.tensor.matmul(dst, w1hi[:, col], xhi[p][:, k, :], start=(k == 0), stop=False)
                        nc.tensor.matmul(dst, w1hi[:, col], xlo[p][:, k, :], start=False, stop=False)
                        ins = nc.tensor.matmul(dst, w1lo[:, col], xhi[p][:, k, :], start=False, stop=(k == KD - 1))
                    if c % 4 == 3:
                        ins.then_inc(h_mm, 1)

            def down(m, p):
                j = 2 * m + p
                e = pe.value_load(eid[0:1, bass.ds(j, 1)], min_val=0, max_val=E - 1)
                at_least(pe, y_ready, j - 1)
                for c in range(KF):
                    if c % 4 == 0:
                        pe.wait_ge(split_ready, 2 * j + c // 4 + 1)
                    col = bass.ds(e * WE + c * D, D)
                    h = slice(c * P, (c + 1) * P)
                    nc.tensor.matmul(f_y[p], hhi[p][:, h], w2hi[:, col], start=(c == 0), stop=False)
                    nc.tensor.matmul(f_y[p], hhi[p][:, h], w2lo[:, col], start=False, stop=False)
                    ins = nc.tensor.matmul(f_y[p], hlo[p][:, h], w2hi[:, col], start=False, stop=(c == KF - 1))
                ins.then_inc(y_mm, 1)

            turn(0, 0)
            up(0, 0)
            turn(0, 1)
            for m in range(2):
                up(m, 1)
                turn(m + 1, 0)
                down(m, 0)
                up(m + 1, 0)
                turn(m + 1, 1)
                down(m, 1)
            with pe.Fori(2, BLOCKS // 2 - 1) as m:
                up(m, 1)
                turn(m + 1, 0)
                down(m, 0)
                up(m + 1, 0)
                turn(m + 1, 1)
                down(m, 1)
            m = BLOCKS // 2 - 1
            up(m, 1)
            turn(m + 1, 0)
            down(m, 0)
            up(m + 1, 0)
            down(m, 1)
            down(m + 1, 0)

        @block.scalar
        def _(act):
            act.wait_ge(setup_mm, 2)
            for c in range(KD):
                nc.scalar.copy(mt[:, c, :], bank[c][:, 0:D])
                ins = nc.scalar.copy(wv_ext[:, c, 0:D], bank[2 + c][:, 0:D])
            ins.then_inc(setup_ev, 1)
            act.wait_ge(setup_mm, 3)
            nc.scalar.copy(wrt[:, :, :], bank[4][:, 0:KD * E].rearrange("p (k e) -> p k e", k=KD))
            nc.scalar.copy(b1t[:, :], bank[4][:, 64:64 + E * KF]).then_inc(setup_ev, 1)
            act.wait_ge(setup_mm, 5)
            nc.scalar.copy(wv_ext[:, :, D], bank[5][:, 0:2])
            nc.scalar.copy(g_col[:, :], bank[5][:, 2:4])
            nc.scalar.copy(c_col[:, :], bank[5][:, 4:5]).then_inc(setup_ev, 1)
            act.wait_ge(setup_ev, 3)
            nc.scalar.activation(ident_c[:, :], ident[:, :], ACT.Identity, scale=c_col[:, 0:1]).then_inc(setup_ev, 2)
            act.wait_ge(setup_ev, 5)

            def high_part(m, p, g):
                b = 2 * m + p
                act.wait_ge(w_mm, 4 * b + g + 1)
                dst = w2hi if p else w1hi
                nc.scalar.activation(dst[:, bass.ds(m * WE + g * 512, 512)], b_w[g % 2], ACT.Copy,
                                     scale=W_SCALE).then_inc(whi_ready, 1)

            def step(project, attend, route, publish):
                if route is not None:
                    mr, pr = route
                    r = 2 * mr + pr
                    act.wait_ge(rn2_ready, r + 1)
                    at_least(act, x2t_mm, r - 1)
                    at_least(act, xn2_stored[pr], 16 * mr)
                    rb = rn2[:, bass.ds(r, 1), :, :].rearrange("p a r j -> p (a r) j")
                    for j in range(TJ):
                        ins = nc.scalar.activation(xn2[pr][:, j, :], x1[:, bass.ds(r, 1), j, :].rearrange("p a d -> p (a d)"),
                                                   ACT.Identity, bias=rb[:, 1, j:j + 1], scale=rb[:, 0, j:j + 1])
                    ins.then_inc(xn2_ready, 1)
                if project is not None:
                    m, p = project
                    b = 2 * m + p
                    act.wait_ge(rn1_ready, b + 1)
                    at_least(act, xt_mm, b - 1)
                    for j in range(TJ):
                        ins = nc.scalar.activation(xn[p][:, j, :], x1[:, bass.ds(b, 1), j, :].rearrange("p a d -> p (a d)"),
                                                   ACT.Identity, bias=rn1[:, 1, j:j + 1], scale=rn1[:, 0, j:j + 1])
                    ins.then_inc(xn_ready, 1)
                    act.wait_ge(ctxt_mm, b + 1)
                    nc.scalar.copy(ctxt[:, :, :], b_ctxt).then_inc(ctxt_ready, 1)
                if attend is not None:
                    ma, pa = attend
                    a = 2 * ma + pa
                    act.wait_ge(max_ready, a + 1)
                    for j in range(TJ):
                        ins = nc.scalar.activation(probs[:, j, :], b_s[:, j, :], ACT.Exp, bias=neg[:, j:j + 1],
                                                   scale=SCALE, accum_out=psum_p[:, j:j + 1])
                    ins.then_inc(exp_ready, 1)
                if project is not None:
                    high_part(m, p, 0)
                    act.wait_ge(xt_mm, b + 1)
                    nc.scalar.copy(xnt[:, :, :], b_x).then_inc(xnt_ready, 1)
                    act.wait_ge(k_mm, b + 1)
                    for c in range(KD):
                        ins = nc.scalar.activation(kt[:, c, :], b_kt[:, c, :], ACT.Identity, bias=g_col[:, c:c + 1])
                    ins.then_inc(kt_ready, 1)
                    high_part(m, p, 1)
                if attend is not None:
                    act.wait_ge(pt_mm, a + 1)
                    nc.scalar.copy(pt[:, :, :], b_pt).then_inc(pt_ready, 1)
                if route is not None:
                    act.wait_ge(x2t_mm, r + 1)
                    nc.scalar.copy(xn2t[:, :, :], b_x).then_inc(xn2t_ready, 1)
                    act.wait_ge(xn2_ready, r + 1)
                    act.dma_start(tok_v[:, bass.ds(r, 1), :, :].rearrange("p a j d -> p (a j) d"), xn2[pr][:, :, :]).then_inc(xn2_stored[pr], 16)
                if project is not None:
                    high_part(m, p, 2)
                    high_part(m, p, 3)

            steps(act, step, 2)

            act.wait_ge(gate_diff, 1)
            nc.scalar.activation(gexp, gexp, ACT.Exp).then_inc(gate_exp, 1)

            def x_high(m, p):
                j = 2 * m + p
                act.wait_ge(xg_mm, j + 1)
                at_least(act, h_mm, 2 * (j - 1))
                nc.scalar.copy(xhi[p][:, :, :], f_x).then_inc(xhi_ready, 1)

            def gelu(m, p, half):
                j = 2 * m + p
                act.wait_ge(h_mm, 2 * j + half + 1)
                if half == 0:
                    act.wait_ge(b1_staged, j + 1)
                at_least(act, split_ready, 2 * (j - 2) + half + 1)
                for c in range(4 * half, 4 * half + 4):
                    ins = nc.scalar.activation(h32[p][:, c * P:(c + 1) * P], f_h[p][half][:, (c % 4) * P:(c % 4 + 1) * P],
                                               ACT.Gelu, bias=b1s[p][:, c:c + 1], scale=1.0 / W_SCALE)
                ins.then_inc(gelu_ready, 1)

            def ahead(m1, p1, m2, p2):
                gelu(m1, p1, 0)
                x_high(m2, p2)
                gelu(m1, p1, 1)

            x_high(0, 0)
            ahead(0, 0, 0, 1)
            for m in range(2):
                ahead(m, 1, m + 1, 0)
                ahead(m + 1, 0, m + 1, 1)
            with act.Fori(2, BLOCKS // 2 - 1) as m:
                ahead(m, 1, m + 1, 0)
                ahead(m + 1, 0, m + 1, 1)
            m = BLOCKS // 2 - 1
            ahead(m, 1, m + 1, 0)
            gelu(m + 1, 0, 0)
            gelu(m + 1, 0, 1)

            act.wait_ge(y_mm, BLOCKS)

            def again(m, p):
                b = 2 * m + p
                at_least(act, z_ready, b - 1)
                rb = rn2[:, bass.ds(b, 1), :, :].rearrange("p a r j -> p (a r) j")
                nc.scalar.activation(xf_sb[p][:, 0, :], x1[:, bass.ds(b, 1), 0, :].rearrange("p a d -> p (a d)"), ACT.Identity,
                                     bias=rb[:, 1, 0:1], scale=rb[:, 0, 0:1])
                nc.scalar.activation(xf_sb[p][:, 1, :], x1[:, bass.ds(b, 1), 1, :].rearrange("p a d -> p (a d)"), ACT.Identity,
                                     bias=rb[:, 1, 1:2], scale=rb[:, 0, 1:2]).then_inc(xf_ready, 1)

            def normal(m, p):
                b = 2 * m + p
                act.wait_ge(rn3_ready, b + 1)
                at_least(act, zw_ready, b - 1)
                for j in range(TJ):
                    ins = nc.scalar.activation(zn_sb[p][:, j, :], z_sb[p][:, j, :], ACT.Identity,
                                               bias=rn3[p][:, 1, j:j + 1], scale=rn3[p][:, 0, j:j + 1])
                ins.then_inc(zn_ready, 1)

            again(0, 0)
            again(0, 1)
            normal(0, 0)
            again(1, 0)
            normal(0, 1)
            again(1, 1)
            with act.Fori(1, NB // 2 - 1) as m:
                normal(m, 0)
                again(m + 1, 0)
                normal(m, 1)
                again(m + 1, 1)
            normal(NB // 2 - 1, 0)
            normal(NB // 2 - 1, 1)

        @block.vector
        def _(dve):
            tick = [0]

            def chain(ins):
                tick[0] += 1
                ins.then_inc(dve_self, 1)
                dve.wait_ge(dve_self, tick[0])

            dve.wait_ge(small_loaded, 16 * N_SMALL)
            nc.vector.tensor_copy(bq_rep, bqk[:, 0, :].unsqueeze(2).to_broadcast([P, KD, P])).then_inc(bq_spread, 1)

            dve.wait_ge(setup_ev, 5)

            def low_part(m, p, g):
                b = 2 * m + p
                dve.wait_ge(whi_ready, 4 * b + g + 1)
                hi, lo = (w2hi, w2lo) if p else (w1hi, w1lo)
                col = bass.ds(m * WE + g * 512, 512)
                nc.vector.scalar_tensor_tensor(out=lo[:, col], in0=b_w[g % 2], scalar=W_SCALE, in1=hi[:, col],
                                               op0=ALU.mult, op1=ALU.subtract).then_inc(wlo_ready, 1)

            def stats(b, st, mv, src, done, self_count):
                for j in range(TJ):
                    ins = nc.vector.bn_stats(st[:, j, :], src(j))
                ins.then_inc(stats_self, 1)
                alone(dve, stats_self, self_count + 1, tally_dve)
                for j in range(TJ):
                    ins = nc.vector.bn_aggr(mv[:, j, :], st[:, j, :])
                ins.then_inc(done, 1)

            def step(project, attend, route, publish):
                if project is not None:
                    m, p = project
                    b = 2 * m + p
                    at_least(dve, rn1_ready, b - 1)
                    alone(dve, x_loaded[p], 16 * (m + 1), tally_dve)
                    used = b + (b - 2 if not isinstance(b, int) or b >= 2 else 0)
                    stats(b, st1, mv1[p], lambda j: x1[:, bass.ds(b, 1), j, :].rearrange("p a d -> p (a d)"), stats1, used)
                if route is not None:
                    mr, pr = route
                    r = 2 * mr + pr
                    at_least(dve, rn2_ready, r - 1)
                    alone(dve, x1_ready, r + 1, tally_dve)
                    used = 2 * r + 3 if not isinstance(r, int) or r + 3 <= NB else NB + r
                    stats(r, st2, mv2[pr], lambda j: x1[:, bass.ds(r, 1), j, :].rearrange("p a d -> p (a d)"), stats2, used)
                if attend is not None:
                    ma, pa = attend
                    a = 2 * ma + pa
                    dve.wait_ge(s_mm, a + 1)
                    nc.vector.tensor_reduce(top[:, :], b_s, AX.X, ALU.max).then_inc(max_self, 1)
                    dve.wait_ge(max_self, 2 * a + 1)
                    nc.vector.tensor_scalar(neg[:, :], top[:, :], -SCALE, None, ALU.mult).then_inc(max_ready, 1)
                if project is not None:
                    low_part(m, p, 0)
                    dve.wait_ge(v_mm, b + 1)
                    nc.vector.tensor_tensor(v_sb[p], b_v[:, 0:D], bv_bc[0:SK, :], ALU.add)
                    nc.vector.scalar_tensor_tensor(out=s_diag[p], in0=ident[0:SK, 0:SK], scalar=b_v[:, D:D + 1],
                                                   in1=ident_c[0:SK, 0:SK], op0=ALU.mult, op1=ALU.add).then_inc(v_ready, 1)
                    low_part(m, p, 1)
                if attend is not None:
                    dve.wait_ge(exp_ready, a + 1)
                    nc.vector.reciprocal(rinv[:, :], psum_p[:, :]).then_inc(max_self, 1)
                if route is not None:
                    dve.wait_ge(lg_mm, r + 1)
                    nc.vector.tensor_tensor(lg[:, :, :], b_lg, br_bc[:, :].unsqueeze(1).to_broadcast([P, TJ, E]), ALU.add).then_inc(top_self, 1)
                    alone(dve, top_self, 5 * r + 1, tally_dve)
                    for j in range(TJ):
                        ins = nc.vector.max(mx[:, j, :], lg[:, j, :])
                    ins.then_inc(top_self, 1)
                    alone(dve, top_self, 5 * r + 2, tally_dve)
                    for j in range(TJ):
                        ins = nc.vector.max_index(ix[:, j, :], mx[:, j, :], lg[:, j, :])
                    ins.then_inc(top_self, 1)
                    nc.vector.tensor_copy(vals[:, bass.ds(r, 1), :, :].rearrange("p a j k -> p (a j) k"), mx[:, :, 0:TOPK])
                    dve.wait_ge(top_self, 5 * r + 3)
                    nc.vector.tensor_copy(ixf[:, :, :], ix[:, :, 0:TOPK]).then_inc(top_self, 1)
                    dve.wait_ge(top_self, 5 * r + 4)
                    nc.vector.tensor_tensor(oh[:, :, :, :].rearrange("p j k e -> p (j k) e"),
                                            iota8[:, :].unsqueeze(1).to_broadcast([P, TJ * TOPK, E]),
                                            ixf[:, :, :].rearrange("p j k -> p (j k)").unsqueeze(2).to_broadcast([P, TJ * TOPK, E]),
                                            ALU.is_equal).then_inc(top_self, 1)
                    dve.wait_ge(top_self, 5 * r + 5)
                    nc.vector.tensor_tensor(chosen[:, :, :], oh[:, :, 0, :], oh[:, :, 1, :], ALU.add).then_inc(chosen_ready, 1)
                if project is not None:
                    low_part(m, p, 2)
                if attend is not None:
                    dve.wait_ge(o_mm, a + 1)
                    dve.wait_ge(max_self, 2 * a + 2)
                    for j in range(TJ):
                        xs = x1[:, bass.ds(a, 1), j, :].rearrange("p a d -> p (a d)")
                        ins = nc.vector.scalar_tensor_tensor(out=xs, in0=b_o[:, j, :], scalar=rinv[:, j:j + 1], in1=xs,
                                                             op0=ALU.mult, op1=ALU.add)
                    ins.then_inc(x1_ready, 1)
                if project is not None:
                    low_part(m, p, 3)
                if route is not None:
                    dve.wait_ge(rank_mm, r + 1)
                    nc.vector.tensor_tensor(slot_e[:, :, :], b_rank, slot0[:, :].unsqueeze(1).to_broadcast([P, TJ, E]), ALU.add).then_inc(slot_self, 1)
                    dve.wait_ge(chosen_ready, r + 1)
                    nc.vector.tensor_tensor(seen[:, :], seen[:, :], chosen[:, 0, :], ALU.add).then_inc(slot_self, 1)
                    dve.wait_ge(slot_self, 5 * r + 2)
                    nc.vector.tensor_tensor(seen[:, :], seen[:, :], chosen[:, 1, :], ALU.add).then_inc(seen_ready, 1)
                    for j in range(TJ):
                        ins = nc.vector.tensor_tensor(prod[:, j, :, :], oh[:, j, :, :],
                                                      slot_e[:, j, :].unsqueeze(1).to_broadcast([P, TOPK, E]), ALU.mult)
                        ins.then_inc(slot_self, 1)
                    dve.wait_ge(slot_self, 5 * r + 4)
                    nc.vector.tensor_reduce(slotf[:, :], prod[:, :, :, :].rearrange("p j k e -> p (j k) e"), AX.X, ALU.add).then_inc(slot_self, 1)
                    at_least(dve, published[pr], ROUTED * mr)
                    dve.wait_ge(slot_self, 5 * r + 5)
                    nc.vector.tensor_copy(slots[pr][:, :], slotf[:, :]).then_inc(slots_ready, 1)

            steps(dve, step, 2)

            dve.wait_ge(count_mm, 1)
            chain(nc.vector.tensor_scalar(cnt[:, :], bank[5][:, 0:E], float(P - 1), None, ALU.add))
            chain(nc.vector.tensor_scalar(nblk_i[:, :], cnt[:, :], P.bit_length() - 1, None, ALU.arith_shift_right))
            chain(nc.vector.tensor_copy(nblk[:, :], nblk_i[:, :]))
            chain(nc.vector.tensor_copy(endb[0][:, :], nblk[:, :]))
            for s, d in enumerate((1, 2, 4)):
                nc.vector.tensor_copy(endb[s + 1][:, 0:d], endb[s][:, 0:d])
                chain(nc.vector.tensor_tensor(endb[s + 1][:, d:E], endb[s][:, d:E], endb[s][:, 0:E - d], ALU.add))
            ends = endb[3][:, :].unsqueeze(1).to_broadcast([P, BLOCKS, E])
            chain(nc.vector.tensor_tensor(passed, ends, jota[:, :].unsqueeze(2).to_broadcast([P, BLOCKS, E]), ALU.is_le))
            nc.vector.tensor_reduce(eidf, passed[:, :, 0:E - 1], AX.X, ALU.add)
            chain(nc.vector.tensor_tensor(skipped[:, :, 0:E - 1], passed[:, :, 0:E - 1],
                                          nblk[:, 0:E - 1].unsqueeze(1).to_broadcast([P, BLOCKS, E - 1]), ALU.mult))
            nc.vector.tensor_copy(eid, eidf)
            chain(nc.vector.tensor_reduce(firstf, skipped[:, :, 0:E - 1], AX.X, ALU.add))
            chain(nc.vector.scalar_tensor_tensor(out=rowf, in0=eidf, scalar=float(PER_EXPERT), in1=jota[:, :],
                                                 op0=ALU.mult, op1=ALU.add))
            chain(nc.vector.tensor_tensor(firstf, rowf, firstf, ALU.subtract))
            nc.vector.tensor_copy(row, firstf).then_inc(blocks_ready, 1)
            v2 = vals[:, :, :, :].rearrange("p b j k -> p (b j) k")
            g2 = gate[:, :, :, :].rearrange("p b j k -> p (b j) k")
            nc.vector.tensor_tensor(gexp, v2[:, :, 1], v2[:, :, 0], ALU.subtract).then_inc(gate_diff, 1)
            dve.wait_ge(gate_exp, 1)
            chain(nc.vector.tensor_scalar(gsum, gexp, 1.0, None, ALU.add))
            chain(nc.vector.reciprocal(g2[:, :, 0], gsum))
            nc.vector.tensor_tensor(g2[:, :, 1], gexp, g2[:, :, 0], ALU.mult)

            def x_low(m, p):
                j = 2 * m + p
                dve.wait_ge(xhi_ready, j + 1)
                nc.vector.tensor_tensor(xlo[p][:, :, :], f_x, xhi[p][:, :, :], ALU.subtract).then_inc(xlo_ready, 1)

            def split(m, p, half):
                j = 2 * m + p
                s = slice(half * 512, half * 512 + 512)
                dve.wait_ge(gelu_ready, 2 * j + half + 1)
                at_least(dve, y_mm, j - 1)
                nc.vector.tensor_copy(hhi[p][:, s], h32[p][:, s]).then_inc(hhi_ready, 1)
                dve.wait_ge(hhi_ready, 2 * j + half + 1)
                nc.vector.tensor_tensor(hlo[p][:, s], h32[p][:, s], hhi[p][:, s], ALU.subtract).then_inc(split_ready, 1)

            def y_out(m, p):
                j = 2 * m + p
                e = dve.value_load(eid[0:1, bass.ds(j, 1)], min_val=0, max_val=E - 1)
                dve.wait_ge(y_mm, j + 1)
                at_least(dve, scattered[p], 16 * m)
                nc.vector.scalar_tensor_tensor(out=y_sb[p], in0=f_y[p], scalar=1.0 / W_SCALE,
                                               in1=b2_bc[:, bass.ds(e * D, D)], op0=ALU.mult, op1=ALU.add).then_inc(y_ready, 1)

            def ahead(m1, p1, m2, p2):
                split(m1, p1, 0)
                x_low(m2, p2)
                split(m1, p1, 1)

            dve.wait_ge(late_loaded, 48)
            x_low(0, 0)
            ahead(0, 0, 0, 1)
            for m in range(2):
                ahead(m, 1, m + 1, 0)
                y_out(m, 0)
                ahead(m + 1, 0, m + 1, 1)
                y_out(m, 1)
            with dve.Fori(2, BLOCKS // 2 - 1) as m:
                ahead(m, 1, m + 1, 0)
                y_out(m, 0)
                ahead(m + 1, 0, m + 1, 1)
                y_out(m, 1)
            m = BLOCKS // 2 - 1
            ahead(m, 1, m + 1, 0)
            y_out(m, 0)
            split(m + 1, 0, 0)
            split(m + 1, 0, 1)
            y_out(m, 1)
            y_out(m + 1, 0)

            def weigh(m, p):
                b = 2 * m + p
                dve.wait_ge(rows_loaded[p], 32 * (m + 1))
                dve.wait_ge(xf_ready, b + 1)
                at_least(dve, zn_ready, b - 1)
                for k, (rows, add) in enumerate(((first, xf_sb[p]), (second, z_sb[p]))):
                    for j in range(TJ):
                        ins = nc.vector.scalar_tensor_tensor(
                            out=z_sb[p][:, j, :], in0=rows[:, bass.ds(b, 1), j, :].rearrange("p a d -> p (a d)"),
                            scalar=gate[:, bass.ds(b, 1), j, k], in1=add[:, j, :], op0=ALU.mult, op1=ALU.add)
                    ins.then_inc(z_self, 1)
                    dve.wait_ge(z_self, 2 * b + k + 1)
                alone(dve, rn3_ready, b - 1, tally_dve)
                for j in range(TJ):
                    ins = nc.vector.bn_stats(st3[:, j, :], z_sb[p][:, j, :])
                ins.then_inc(z_ready, 1)
                alone(dve, z_ready, b + 1, tally_dve)
                for j in range(TJ):
                    ins = nc.vector.bn_aggr(mv3[p][:, j, :], st3[:, j, :])
                ins.then_inc(stats3, 1)

            def affine(m, p):
                b = 2 * m + p
                dve.wait_ge(zn_ready, b + 1)
                at_least(dve, o_ready, b - 1)
                nc.vector.tensor_tensor(zn_sb[p], zn_sb[p], lnw_bc[:, :].unsqueeze(1).to_broadcast([P, TJ, D]),
                                        ALU.mult).then_inc(affine_self, 1)
                dve.wait_ge(affine_self, b + 1)
                nc.vector.tensor_tensor(zw_sb[p], zn_sb[p], lnb_bc[:, :].unsqueeze(1).to_broadcast([P, TJ, D]),
                                        ALU.add).then_inc(zw_ready, 1)

            weigh(0, 0)
            weigh(0, 1)
            affine(0, 0)
            weigh(1, 0)
            affine(0, 1)
            with dve.Fori(1, NB // 2 - 1) as m:
                weigh(m, 1)
                affine(m, 0)
                weigh(m + 1, 0)
                affine(m, 1)
            m = NB // 2 - 1
            weigh(m, 1)
            affine(m, 0)
            affine(m, 1)


_INS = ['x', 'ctx_1024', 'L0_xattn_Wq', 'L0_xattn_bq', 'L0_xattn_Wk', 'L0_xattn_bk', 'L0_xattn_Wv', 'L0_xattn_bv',
        'L0_ffn_Wr', 'L0_ffn_br', 'L0_ffn_W1', 'L0_ffn_b1', 'L0_ffn_W2', 'L0_ffn_b2', 'L0_ffn_ln_w', 'L0_ffn_ln_b']
_OUTS = [((16, 256, 256), 'float32')]


def kernel(**inputs):
    import numpy as _np
    import concourse.bacc as _bacc
    from concourse import mybir as _mybir
    from concourse.bass_utils import run_bass_kernel_spmd as _run

    nc = _bacc.Bacc("TRN2", target_bir_lowering=False, num_devices=1)
    arrays, args = {}, []
    for name in _INS:
        a = _np.ascontiguousarray(inputs[name])
        arrays[f"in_{name}_dram"] = a
        args.append(nc.dram_tensor(f"in_{name}_dram", a.shape, _mybir.dt.from_np(a.dtype), kind="ExternalInput").ap())
    for i, (shape, dtype) in enumerate(_OUTS):
        dt = _mybir.dt.from_np(_np.dtype(dtype))
        args.append(nc.dram_tensor(f"out_{i}_dram", shape, dt, kind="ExternalOutput").ap())
    build(nc, *args)
    r = _run(nc, [arrays], core_ids=[0])
    got = tuple(r.results[0][f"out_{i}_dram"] for i in range(len(_OUTS)))
    return got[0]
```

```python
from contextlib import ExitStack

import concourse.bass as bass
from concourse import mybir

F32 = mybir.dt.float32
F16 = mybir.dt.float16
BF16 = mybir.dt.bfloat16
I32 = mybir.dt.int32
U32 = mybir.dt.uint32
ALU = mybir.AluOpType
ACT = mybir.ActivationFunctionType
AX = mybir.AxisListType

P = 128
EPS_LN = 1e-5
EPS_FFN = 1e-12
W_SCALE = 64.0


def at_least(eng, sem, n):
    if not (isinstance(n, int) and n <= 0):
        eng.wait_ge(sem, n)


def alone(eng, sem, n, tally):
    if not (isinstance(n, int) and n <= 0):
        eng.wait_ge(sem, n)
        eng.sem_inc(tally, 1)


def build(nc, x, ctx_in, Wq, bq, Wk, bk, Wv, bv, Wr, br, W1, b1, W2, b2, ln_w, ln_b, out):
    NB, SQ, D = x.shape
    SK = ctx_in.shape[1]
    E, FF, _ = W1.shape
    KD = D // P
    KF = FF // P
    TJ = SQ // P
    NT = NB * TJ
    TOK = NB * SQ
    TOPK = 2
    TB = 2
    BT = TB * P
    BLOCKS = TOPK * TOK // BT + E - 1
    PER_EXPERT = TOK // BT
    TABLE = E * PER_EXPERT + E
    UNITS = TABLE * TB
    SCALE = float(D) ** -0.5
    assert KD == 2 and TJ == 2 and NB == 2 * E and BLOCKS % 2 == 1 and SK <= P

    slot_table = nc.dram_tensor("slot_table", (UNITS * P, 2), I32).ap()
    tokens_dram = nc.dram_tensor("tokens_dram", (TOK, D), F32).ap()
    expert_rows = nc.dram_tensor("expert_rows", (TOPK * TOK + UNITS * P, D), F32).ap()

    x_v = x.rearrange("b (j p) d -> p b j d", p=P)
    out_v = out.rearrange("b (j p) d -> p b j d", p=P)
    ctx_v = ctx_in.rearrange("b s d -> s b d")
    w1_v = W1.rearrange("e (c p) d -> p e c d", p=P)
    w2_v = W2.rearrange("e (k p) f -> p e k f", p=P)
    tok_v = tokens_dram.rearrange("(b j p) d -> p b j d", p=P, j=TJ)
    first_v = expert_rows[0:TOK, :].rearrange("(b j p) d -> p b j d", p=P, j=TJ)
    second_v = expert_rows[TOK:2 * TOK, :].rearrange("(b j p) d -> p b j d", p=P, j=TJ)
    table_v = slot_table.rearrange("(t q) c -> t (q c)", q=P)

    with ExitStack() as stack:
        def sb(name, shape, dt=F32):
            return stack.enter_context(nc.sbuf_tensor(name, shape, dt))

        def sem(name):
            return stack.enter_context(nc.semaphore(name))

        def sem2(name):
            return [sem(f"{name}{i}") for i in range(2)]

        WE = KF * D
        w1hi = sb("w1hi", [P, E * WE], F16)
        w1lo = sb("w1lo", [P, E * WE], F16)
        w2hi = sb("w2hi", [P, E * WE], F16)
        w2lo = sb("w2lo", [P, E * WE], F16)
        x1 = sb("x1", [P, NB, TJ, D])
        ident = sb("ident", [P, P])
        ones = sb("ones", [P, P])
        before = sb("before", [P, P], BF16)
        ones_bf = sb("ones_bf", [P, P], BF16)
        iota8 = sb("iota8", [P, E])
        slot0 = sb("slot0", [P, E])
        minus_half = sb("minus_half", [P, 2, TJ])
        ids = sb("ids", [P, NT * TOPK, 2], I32)
        mt = sb("mt", [P, KD, D])
        wv_ext = sb("wv_ext", [P, KD, D + 1])
        wrt = sb("wrt", [P, KD, E])
        g_col = sb("g_col", [P, KD])
        ident_c = sb("ident_c", [P, P])
        bv_bc = sb("bv_bc", [P, D])
        br_bc = sb("br_bc", [P, E])
        b1t = sb("b1t", [P, E * KF])
        stage = [sb(f"stage{i}", [P, KF * D]) for i in range(2)]
        wqkv = stage[0][:, 0:3 * KD * D].rearrange("p (w k d) -> p w k d", w=3, k=KD)
        wr_in = stage[1][0:E, 0:D]
        b1_in = stage[1][0:E * KF, D:D + P]
        bqk = sb("bqk", [P, 2, KD])
        bq_rep = stage[1][:, 1024:1024 + KD * P].rearrange("p (k q) -> p k q", k=KD)
        c_col = sb("c_col", [P, 1])
        PADS = -(-UNITS // P)
        pad_rows = [sb_at.bitcast(I32).rearrange("p (q c) -> p q c", c=2)
                    for sb_at in (stage[0][:, 1536:1792], stage[0][:, 1792:2048], stage[1][:, 1536:1792])]
        ctx_sb = [sb(f"ctx_sb{i}", [P, D]) for i in range(2)]
        st = [sb(f"st{i}", [P, 2, TJ, 6]) for i in range(2)]
        mv = [sb(f"mv{i}", [P, 2, TJ, 2]) for i in range(2)]
        ve = [sb(f"ve{i}", [P, 2, TJ]) for i in range(2)]
        nmu = [sb(f"nmu{i}", [P, 2, TJ]) for i in range(2)]
        rn = [sb(f"rn{i}", [P, 2, 2, TJ]) for i in range(2)]
        xn = [sb(f"xn{i}", [P, TJ, D]) for i in range(2)]
        xn2 = [sb(f"xn2_{i}", [P, TJ, D]) for i in range(2)]
        xnt = sb("xnt", [P, KD, SQ])
        work = sb("work", [P, KD * SQ + 2 * KD * SK + 2 * D + 2 * SK + TJ * SK + TJ * P])
        cut = [0]

        def piece(rows, cols):
            cut[0] += cols
            return work[0:rows, cut[0] - cols:cut[0]]

        xn2t = piece(P, KD * SQ).rearrange("p (k q) -> p k q", k=KD)
        ctxt = piece(P, KD * SK).rearrange("p (k s) -> p k s", k=KD)
        kt = piece(P, KD * SK).rearrange("p (k s) -> p k s", k=KD)
        v_sb = [piece(SK, D) for i in range(2)]
        s_diag = [piece(SK, SK) for i in range(2)]
        top = sb("top", [P, TJ])
        neg = sb("neg", [P, TJ])
        probs = piece(P, TJ * SK).rearrange("p (j s) -> p j s", j=TJ)
        psum_p = sb("psum_p", [P, TJ])
        rinv = sb("rinv", [P, TJ])
        pt = piece(SK, TJ * P).rearrange("p (j q) -> p j q", j=TJ)
        lg = sb("lg", [P, TJ, E])
        mx = sb("mx", [P, TJ, E])
        ix = sb("ix", [P, TJ, E], U32)
        ixf = sb("ixf", [P, TJ, TOPK])
        oh = sb("oh", [P, TJ, TOPK, E])
        chosen = sb("chosen", [P, TJ, E], BF16)
        seen = sb("seen", [P, E], BF16)
        slot_e = sb("slot_e", [P, TJ, E])
        prod = sb("prod", [P, TJ, TOPK, E])
        slotf = sb("slotf", [P, TJ * TOPK])
        slots = [sb(f"slots{i}", [P, TJ * TOPK], I32) for i in range(2)]
        rows_now = [sb(f"rows_now{i}", [P, TJ * TOPK, 2], I32) for i in range(2)]
        vals = sb("vals", [P, NB, TJ, TOPK])
        gate = sb("gate", [P, NB, TJ, TOPK])
        gexp = stage[0][:, 900:900 + NT]
        gsum = stage[0][:, 950:950 + NT]
        jota = sb("jota", [P, BLOCKS])
        passed = stage[0][:, 0:BLOCKS * E].rearrange("p (t e) -> p t e", e=E)
        skipped = stage[0][:, 1024:1024 + BLOCKS * E].rearrange("p (t e) -> p t e", e=E)
        endb = [stage[0][:, 320 + E * i:320 + E * (i + 1)] for i in range(4)]
        cnt, nblk_i = (stage[0][:, 400 + E * i:400 + E * (i + 1)].bitcast(I32) for i in range(2))
        nblk = stage[0][:, 400 + 2 * E:400 + 3 * E]
        eidf = stage[0][:, 600:600 + BLOCKS]
        firstf = stage[0][:, 700:700 + BLOCKS]
        rowf = stage[0][:, 800:800 + BLOCKS]
        eid = sb("eid", [P, BLOCKS], I32)
        woff = sb("woff", [1, BLOCKS], I32)
        row = sb("row", [1, BLOCKS], I32)
        idx_all = work[:, E * D:E * D + 2 * TB * BLOCKS].bitcast(I32).rearrange("p (t j c) -> p t j c", j=TB, c=2)
        gidx = [sb(f"gidx{i}", [P, TB], I32) for i in range(2)]
        sidx = [sb(f"sidx{i}", [P, TB], I32) for i in range(2)]
        b1s = [sb(f"b1s{i}", [P, KF]) for i in range(2)]
        b2_bc = work[:, 0:E * D]
        lnw_bc, lnb_bc = ctx_sb[0], ctx_sb[1]
        xg, y_sb = xn, xn2
        xparts = xnt[:, :, :].rearrange("p k q -> p (k q)").bitcast(F16).rearrange("p (i k q) -> p i k q", i=2, k=KD)
        xhi, xlo = xparts[:, 0, :, :], xparts[:, 1, :, :]
        h32 = stage[0][:, :]
        hhi = stage[1][:, 0:KF * P].bitcast(F16)
        hlo = stage[1][:, KF * P:2 * KF * P].bitcast(F16)
        def by_batch(t):
            return t[:, :].bitcast(F32).rearrange("p (b j d) -> p b j d", b=NB, j=TJ)

        residual, first, second = by_batch(w1lo), by_batch(w1hi), by_batch(w2lo)
        w2hi_f = w2hi[:, :].bitcast(F32).rearrange("p (n d) -> p n d", d=D)
        z_sb = [w2hi_f[:, 2 * i:2 * i + 2, :] for i in range(2)]
        zn_sb = [w2hi_f[:, 4 + 2 * i:6 + 2 * i, :] for i in range(2)]
        zw_sb = [w2hi_f[:, 8 + 2 * i:10 + 2 * i, :] for i in range(2)]
        o_sb = [w2hi_f[:, 12 + 2 * i:14 + 2 * i, :] for i in range(2)]
        st3 = [w2hi_f[:, 18 + i, 0:TJ * 6].rearrange("p (j s) -> p j s", j=TJ) for i in range(2)]
        mv3 = [w2hi_f[:, 21 + i, 0:TJ * 2].rearrange("p (j s) -> p j s", j=TJ) for i in range(2)]
        rn3 = [w2hi_f[:, 23 + i, 0:2 * TJ].rearrange("p (r j) -> p r j", r=2) for i in range(2)]

        bank = [stack.enter_context(nc.psum_tensor(f"bank{i}", [P, 512], F32)) for i in range(8)]
        b_x = bank[0][:, :].rearrange("p (k q) -> p k q", k=KD)
        b_ctxt = bank[1][:, 0:KD * SK].rearrange("p (k s) -> p k s", k=KD)
        b_kt = bank[1][:, 256:256 + KD * SK].rearrange("p (k s) -> p k s", k=KD)
        b_v = bank[2][0:SK, 0:D + 1]
        b_s = bank[3][:, 0:TJ * SK].rearrange("p (j s) -> p j s", j=TJ)
        b_pt = bank[3][0:SK, 256:512].rearrange("p (j q) -> p j q", j=TJ)
        b_o = bank[4][:, :].rearrange("p (j d) -> p j d", j=TJ)
        b_lg = bank[5][:, 0:TJ * E].rearrange("p (j e) -> p j e", j=TJ)
        b_rank = bank[5][:, 64:64 + TJ * E].rearrange("p (j e) -> p j e", j=TJ)
        b_w = [bank[6][:, :], bank[7][:, :]]
        f_h = bank[0:4]
        f_x = bank[4][:, :].rearrange("p (k q) -> p k q", k=KD)
        f_y = [bank[5 + t][:, 0:D] for t in range(TB)]
        HB = len(f_h)

        consts_pool = sem("consts_pool")
        pool_self = sem("pool_self")
        proj_w_loaded = sem("proj_w_loaded")
        small_loaded = sem("small_loaded")
        late_loaded = sem("late_loaded")
        shift_loaded = sem("shift_loaded")
        shift_added = sem("shift_added")
        table_blank = sem("table_blank")
        bq_spread = sem("bq_spread")
        setup_mm = sem("setup_mm")
        setup_ev = sem("setup_ev")
        x_loaded = sem2("x_loaded")
        ctx_loaded = sem2("ctx_loaded")
        w_loaded = sem2("w_loaded")
        dve_self = sem("dve_self")
        xn_ready = sem("xn_ready")
        stats_ready = sem("stats_ready")
        rn_ready = sem("rn_ready")
        xn2_ready = sem("xn2_ready")
        xn2_stored = sem2("xn2_stored")
        ctxt_mm = sem("ctxt_mm")
        ctxt_ready = sem("ctxt_ready")
        k_mm = sem("k_mm")
        kt_ready = sem("kt_ready")
        v_mm = sem("v_mm")
        v_ready = sem("v_ready")
        xt_mm = sem("xt_mm")
        xnt_ready = sem("xnt_ready")
        s_mm = sem("s_mm")
        max_ready = sem("max_ready")
        exp_ready = sem("exp_ready")
        pt_mm = sem("pt_mm")
        pt_ready = sem("pt_ready")
        o_mm = sem("o_mm")
        x1_ready = sem("x1_ready")
        x2t_mm = sem("x2t_mm")
        xn2t_ready = sem("xn2t_ready")
        lg_mm = sem("lg_mm")
        chosen_ready = sem("chosen_ready")
        rank_mm = sem("rank_mm")
        slots_ready = sem("slots_ready")
        seen_ready = sem("seen_ready")
        rows_copied = sem("rows_copied")
        published = sem2("published")
        w_mm = sem("w_mm")
        whi_ready = sem("whi_ready")
        wlo_ready = sem("wlo_ready")
        count_mm = sem("count_mm")
        blocks_ready = sem("blocks_ready")
        gate_diff = sem("gate_diff")
        gate_exp = sem("gate_exp")
        idx_loaded = sem2("idx_loaded")
        gidx_ready = sem("gidx_ready")
        sidx_ready = sem("sidx_ready")
        b1_staged = sem("b1_staged")
        gathered = sem2("gathered")
        xg_mm = sem("xg_mm")
        xhi_ready = sem("xhi_ready")
        xlo_ready = sem("xlo_ready")
        h_mm = sem("h_mm")
        gelu_ready = sem("gelu_ready")
        hhi_ready = sem("hhi_ready")
        split_ready = sem("split_ready")
        y_mm = sem("y_mm")
        y_ready = sem("y_ready")
        scattered = sem2("scattered")
        rows_loaded = sem2("rows_loaded")
        z_ready = sem("z_ready")
        stats3 = sem("stats3")
        rn3_ready = sem("rn3_ready")
        zn_ready = sem("zn_ready")
        zw_ready = sem("zw_ready")
        o_ready = sem("o_ready")
        stored = sem2("stored")

        norm_self = sem("norm_self")
        tally_dve = sem("tally_dve")
        tally_pool = sem("tally_pool")
        stats_self = sem("stats_self")
        max_self = sem("max_self")
        top_self = sem("top_self")
        slot_self = sem("slot_self")
        z_self = sem("z_self")

        block = stack.enter_context(nc.Block())

        N_SMALL = 6
        PEEL = 8
        ROUTED = 64

        def steps(eng, step, last):
            def one(m, u):
                back = []
                for d in range(6):
                    t = 2 * m + u
                    inside = not isinstance(t, int) or 0 <= t - d < NB
                    back.append((m - (d + 1 - u) // 2, (u + d) % 2) if inside else None)
                step(2 * m + u, u, *back)
            for t in range(PEEL):
                one(t // 2, t % 2)
            with eng.Fori(PEEL // 2, NB // 2) as m:
                one(m, 0)
                one(m, 1)
            for t in range(NB, NB + last):
                one(t // 2, t % 2)

        @block.sync
        def _(sp):
            for w, src in enumerate((Wq, Wk, Wv)):
                sp.dma_start(wqkv[:, w, :, :], src.rearrange("(k p) d -> p k d", p=P)).then_inc(proj_w_loaded, 16)
            with nc.allow_non_contiguous_dma(reason="two short bias columns"):
                sp.dma_start(bqk[:, 0, :], bq.rearrange("(k p) -> p k", p=P)).then_inc(small_loaded, 16)
                sp.dma_start(bqk[:, 1, :], bk.rearrange("(k p) -> p k", p=P)).then_inc(small_loaded, 16)
            sp.dma_start(wr_in, Wr).then_inc(small_loaded, 16)
            sp.dma_start(b1_in, b1.rearrange("e (c p) -> (e c) p", p=P)).then_inc(small_loaded, 16)
            sp.dma_start(bv_bc[:, :], bv.partition_broadcast(P)).then_inc(small_loaded, 16)
            sp.dma_start(br_bc[:, :], br.partition_broadcast(P)).then_inc(small_loaded, 16)
            sp.wait_ge(consts_pool, 1)
            for i in range(PADS):
                n = min(P, UNITS - i * P)
                sp.dma_start(table_v[i * P:i * P + n, :], pad_rows[i][0:n].rearrange("p q c -> p (q c)")).then_inc(table_blank, 16)

            def load(t, u, measure, *later):
                m, p = measure
                b = 2 * m + p
                at_least(sp, x_loaded[p], 16 * m)
                sp.dma_start(x1[:, bass.ds(b, 1), :, :].rearrange("p a j d -> p (a j) d"), x_v[:, bass.ds(b, 1), :, :].rearrange("p a j d -> p (a j) d")).then_inc(x_loaded[p], 16)
                at_least(sp, ctxt_mm, b - 1)
                sp.dma_start(ctx_sb[p][0:SK, :], ctx_v[:, bass.ds(b, 1), :].rearrange("p a d -> p (a d)")).then_inc(ctx_loaded[p], 16)
                at_least(sp, w_mm, 4 * (b - 1))
                if isinstance(m, int) and m == 0:
                    sp.wait_ge(setup_mm, 5)
                    sp.wait_ge(table_blank, 16 * PADS)
                src = w2_v if p else w1_v
                sp.dma_start(stage[p][:, :].rearrange("p (c d) -> p c d", c=KD if p else KF),
                             src[:, bass.ds(m, 1), :, :].rearrange("p a c d -> p (a c) d")).then_inc(w_loaded[p], 16)

            steps(sp, load, 0)

            sp.wait_ge(ctxt_mm, NB)
            sp.dma_start(lnb_bc[:, :], ln_b.partition_broadcast(P)).then_inc(shift_loaded, 16)
            for p in range(2):
                sp.wait_ge(published[p], ROUTED * NB // 2)
            sp.wait_ge(blocks_ready, 1)

            def load_rows(m, p):
                j = 2 * m + p
                at_least(sp, idx_loaded[p], 16 * m)
                r = sp.value_load(row[0:1, bass.ds(j, 1)], min_val=0, max_val=TABLE - 1)
                sp.dma_start(idx_all[:, bass.ds(j, 1), :, :].rearrange("p a j c -> p (a j c)"),
                             slot_table[bass.ds(r * BT, BT), :].rearrange("(p j) c -> p (j c)", j=TB)).then_inc(idx_loaded[p], 16)

            for p in range(2):
                load_rows(0, p)
            sp.dma_start(b2_bc, b2.rearrange("e d -> (e d)").partition_broadcast(P)).then_inc(late_loaded, 16)
            sp.dma_start(lnw_bc[:, :], ln_w.partition_broadcast(P)).then_inc(late_loaded, 16)
            with sp.Fori(1, BLOCKS // 2) as m:
                load_rows(m, 0)
                load_rows(m, 1)
            load_rows(BLOCKS // 2, 0)

            sp.wait_ge(h_mm, HB * BLOCKS)

            def load_batch(m, p, dst, src):
                sp.dma_start(dst[:, bass.ds(2 * m + p, 1), :, :].rearrange("p a j d -> p (a j) d"),
                             src[:, bass.ds(2 * m + p, 1), :, :].rearrange("p a j d -> p (a j) d")).then_inc(rows_loaded[p], 16)

            for p in range(2):
                load_batch(0, p, residual, tok_v)
            sp.wait_ge(y_mm, HB * BLOCKS)
            sp.wait_ge(scattered[0], 16 * TB * (BLOCKS // 2 + 1))
            sp.wait_ge(scattered[1], 16 * TB * (BLOCKS // 2))

            def load_three(m, p):
                at_least(sp, rows_loaded[p], 48 * m)
                if not (isinstance(m, int) and m == 0):
                    load_batch(m, p, residual, tok_v)
                load_batch(m, p, first, first_v)
                load_batch(m, p, second, second_v)

            def store(m, p):
                b = 2 * m + p
                sp.wait_ge(o_ready, b + 1)
                sp.dma_start(out_v[:, bass.ds(b, 1), :, :].rearrange("p a j d -> p (a j) d"), o_sb[p]).then_inc(stored[p], 16)

            for m in range(2):
                for p in range(2):
                    load_three(m, p)
            with sp.Fori(0, NB // 2 - 2) as m:
                for p in range(2):
                    load_three(m + 2, p)
                    store(m, p)
            for m in range(NB // 2 - 2, NB // 2):
                for p in range(2):
                    store(m, p)
            for p in range(2):
                sp.wait_ge(stored[p], 16 * NB // 2)

        @block.gpsimd
        def _(pool):
            for i in range(PADS):
                nc.gpsimd.iota(pad_rows[i][:, :, 0], [[1, P]], base=0, channel_multiplier=0)
                ins = nc.gpsimd.iota(pad_rows[i][:, :, 1], [[1, P]], base=TOPK * TOK + i * P * P, channel_multiplier=P)
            ins.then_inc(consts_pool, 1)
            nc.gpsimd.memset(ident[:, :], 0.0)
            nc.gpsimd.memset(before[:, :], 1.0)
            nc.gpsimd.memset(ones[:, :], 1.0)
            nc.gpsimd.memset(ones_bf[:, :], 1.0)
            nc.gpsimd.memset(seen[:, :], 0.0)
            nc.gpsimd.memset(minus_half[:, :, :], -0.5).then_inc(pool_self, 1)
            pool.wait_ge(pool_self, 1)
            nc.gpsimd.affine_select(out=ident[:, :], in_=ident[:, :], compare_op=ALU.not_equal, fill=1.0, base=0,
                                    pattern=[[-1, P]], channel_multiplier=1)
            nc.gpsimd.affine_select(out=before[:, :], in_=before[:, :], compare_op=ALU.is_gt, fill=0.0, base=0,
                                    pattern=[[1, P]], channel_multiplier=-1)
            nc.gpsimd.iota(iota8[:, :], [[1, E]], base=0, channel_multiplier=0, allow_small_or_imprecise_dtypes=True)
            nc.gpsimd.iota(slot0[:, :], [[TOK, E]], base=0, channel_multiplier=0, allow_small_or_imprecise_dtypes=True)
            nc.gpsimd.iota(jota[:, :], [[1, BLOCKS]], base=0, channel_multiplier=0, allow_small_or_imprecise_dtypes=True)
            nc.gpsimd.iota(ids[:, :, 0], [[P, NT], [0, TOPK]], base=0, channel_multiplier=1)
            nc.gpsimd.iota(ids[:, :, 1], [[P, NT], [TOK, TOPK]], base=0, channel_multiplier=1).then_inc(consts_pool, 1)

            tick = [1]

            def then_self(ins):
                tick[0] += 1
                ins.then_inc(pool_self, 1)
                pool.wait_ge(pool_self, tick[0])

            def norm(count, mean, var, nmu, ve, half, scale, shift, eps, ready):
                nc.gpsimd.tensor_scalar(nmu, mean, -1.0, None, ALU.mult)
                nc.gpsimd.tensor_scalar(ve, var, eps, None, ALU.add).then_inc(norm_self, 1)
                pool.wait_ge(norm_self, 2 * count + 1)
                nc.gpsimd.tensor_tensor(scale, ve, half, ALU.pow).then_inc(norm_self, 1)
                pool.wait_ge(norm_self, 2 * count + 2)
                nc.gpsimd.tensor_tensor(shift, nmu, scale, ALU.mult).then_inc(ready, 1)

            def step(t, u, measure, project, attend, renorm, route, publish):
                if measure is not None or renorm is not None:
                    w = slice(0 if measure is not None else 1, 2 if renorm is not None else 1)
                    at_least(pool, xn_ready, min(t - 1, NB) if isinstance(t, int) else t - 1)
                    at_least(pool, xn2_ready, t - 4)
                    alone(pool, stats_ready, t + 1, tally_pool)
                    norm(t, mv[u][:, w, :, 0], mv[u][:, w, :, 1], nmu[u][:, w, :], ve[u][:, w, :], minus_half[:, w, :],
                         rn[u][:, w, 0, :], rn[u][:, w, 1, :], EPS_LN, rn_ready)
                if publish is not None:
                    m, p = publish
                    b = 2 * m + p
                    n = TJ * TOPK
                    if isinstance(b, int) and b == 0:
                        pool.wait_ge(table_blank, 16 * PADS)
                    at_least(pool, published[p], ROUTED * m)
                    nc.gpsimd.tensor_copy(rows_now[p][:, :, :], ids[:, bass.ds(b * n, n), :]).then_inc(rows_copied, 1)
                    pool.wait_ge(rows_copied, b + 1)
                    alone(pool, slots_ready, b + 1, tally_pool)
                    for a in range(n):
                        nc.gpsimd.indirect_dma_start(
                            out=slot_table, out_offset=bass.IndirectOffsetOnAxis(ap=slots[p][:, a:a + 1], axis=0),
                            in_=rows_now[p][:, a, :], in_offset=None).then_inc(published[p], 16)

            steps(pool, step, 5)

            def fetch(m, p):
                j = 2 * m + p
                e = pool.value_load(eid[0:1, bass.ds(j, 1)], min_val=0, max_val=E - 1)
                pool.wait_ge(idx_loaded[p], 16 * (m + 1))
                at_least(pool, gathered[p], 16 * TB * m)
                nc.gpsimd.tensor_copy(gidx[p][:, :], idx_all[:, bass.ds(j, 1), :, 0].rearrange("p a j -> p (a j)")).then_inc(gidx_ready, 1)
                pool.wait_ge(gidx_ready, j + 1)
                alone(pool, xg_mm, j - 1, tally_pool)
                for t in range(TB):
                    nc.gpsimd.indirect_dma_start(
                        out=xg[p][:, t, :], out_offset=None, in_=tokens_dram,
                        in_offset=bass.IndirectOffsetOnAxis(ap=gidx[p][:, t:t + 1], axis=0)).then_inc(gathered[p], 16)
                at_least(pool, gelu_ready, HB * (j - 1))
                nc.gpsimd.tensor_copy(b1s[p][:, :], b1t[:, bass.ds(e * KF, KF)]).then_inc(b1_staged, 1)

            def give(m, p):
                j = 2 * m + p
                at_least(pool, scattered[p], 16 * TB * m)
                nc.gpsimd.tensor_copy(sidx[p][:, :], idx_all[:, bass.ds(j, 1), :, 1].rearrange("p a j -> p (a j)")).then_inc(sidx_ready, 1)
                pool.wait_ge(sidx_ready, j + 1)
                alone(pool, y_ready, j + 1, tally_pool)
                for t in range(TB):
                    nc.gpsimd.indirect_dma_start(
                        out=expert_rows, out_offset=bass.IndirectOffsetOnAxis(ap=sidx[p][:, t:t + 1], axis=0),
                        in_=y_sb[p][:, t, :], in_offset=None).then_inc(scattered[p], 16)

            pool.wait_ge(blocks_ready, 1)
            pool.wait_ge(setup_ev, 5)
            for p in range(2):
                pool.wait_ge(xn2_stored[p], 16 * NB // 2)
            for n in range(3):
                fetch(n // 2, n % 2)
            fetch(1, 1)
            give(0, 0)
            fetch(2, 0)
            give(0, 1)
            with pool.Fori(1, BLOCKS // 2 - 1) as m:
                fetch(m + 1, 1)
                give(m, 0)
                fetch(m + 2, 0)
                give(m, 1)
            m = BLOCKS // 2 - 1
            give(m, 0)
            give(m, 1)
            give(m + 1, 0)

            def finish(m, p):
                b = 2 * m + p
                at_least(pool, zn_ready, b - 1)
                alone(pool, rn3_ready, b, tally_pool)
                alone(pool, stats3, b + 1, tally_pool)
                norm(NB + 3 + b, mv3[p][:, :, 0], mv3[p][:, :, 1], nmu[0][:, 0, :], ve[0][:, 0, :], minus_half[:, 0, :],
                     rn3[p][:, 0, :], rn3[p][:, 1, :], EPS_FFN, rn3_ready)

            def add_up(m, p):
                b = 2 * m + p
                pool.wait_ge(zw_ready, b + 1)
                if isinstance(b, int) and b == 0:
                    pool.wait_ge(shift_added, NB)
                at_least(pool, stored[p], 16 * m)
                nc.gpsimd.tensor_tensor(o_sb[p], zw_sb[p], x1[:, bass.ds(b, 1), :, :].rearrange("p a j d -> p (a j) d"),
                                        ALU.add).then_inc(o_ready, 1)

            finish(0, 0)
            finish(0, 1)
            add_up(0, 0)
            finish(1, 0)
            add_up(0, 1)
            with pool.Fori(1, NB // 2 - 1) as m:
                finish(m, 1)
                add_up(m, 0)
                finish(m + 1, 0)
                add_up(m, 1)
            m = NB // 2 - 1
            finish(m, 1)
            add_up(m, 0)
            add_up(m, 1)

        @block.tensor
        def _(pe):
            pe.wait_ge(consts_pool, 2)
            pe.wait_ge(proj_w_loaded, 48)
            wq, wk, wv = (wqkv[:, i, :, :] for i in range(3))
            for c in range(KD):
                for k in range(KD):
                    ins = nc.tensor.matmul(bank[c][:, 0:D], wk[:, k, c * P:(c + 1) * P], wq[:, k, :],
                                           start=(k == 0), stop=(k == KD - 1))
            ins.then_inc(setup_mm, 1)
            for k in range(KD):
                for c in range(KD):
                    ins = nc.tensor.transpose(bank[2 + c][:, k * P:(k + 1) * P], wv[:, k, c * P:(c + 1) * P], ident[:, :])
            ins.then_inc(setup_mm, 1)
            pe.wait_ge(small_loaded, 16 * N_SMALL)
            for c in range(KD):
                nc.tensor.transpose(bank[4][:, c * E:(c + 1) * E], wr_in[:, c * P:(c + 1) * P], ident[0:E, 0:E])
            nc.tensor.transpose(bank[4][:, 64:64 + E * KF], b1_in, ident[0:E * KF, 0:E * KF]).then_inc(setup_mm, 1)
            pe.wait_ge(bq_spread, 1)
            for c in range(KD):
                for k in range(KD):
                    nc.tensor.matmul(bank[5][:, c:c + 1], wk[:, k, c * P:(c + 1) * P], bqk[:, 0, k:k + 1],
                                     start=(k == 0), stop=(k == KD - 1))
            for c in range(KD):
                for k in range(KD):
                    nc.tensor.matmul(bank[5][:, 2 + c:3 + c], wq[:, k, c * P:(c + 1) * P], bqk[:, 1, k:k + 1],
                                     start=(k == 0), stop=(k == KD - 1))
            for k in range(KD):
                ins = nc.tensor.matmul(bank[5][:, 4:5], bq_rep[:, k, :], bqk[:, 1, k:k + 1],
                                       start=(k == 0), stop=(k == KD - 1))
            ins.then_inc(setup_mm, 2)
            pe.wait_ge(setup_ev, 5)

            def split_group(m, p, g):
                b = 2 * m + p
                if g == 0:
                    pe.wait_ge(w_loaded[p], 16 * (m + 1))
                n = 4 * b + g
                at_least(pe, wlo_ready, n - 1)
                for q in range(4):
                    c, k = 2 * g + q // 2, q % 2
                    col = k * FF + c * P if p else c * D + k * P
                    ins = nc.tensor.transpose(b_w[g % 2][:, q * P:(q + 1) * P], stage[p][:, col:col + P], ident[:, :])
                ins.then_inc(w_mm, 1)

            def turned(out, src, count):
                for k in range(KD):
                    for j in range(TJ):
                        ins = nc.tensor.transpose(out[:, k, j * P:(j + 1) * P], src[:, j, k * P:(k + 1) * P], ident[:, :])
                ins.then_inc(count, 1)

            def step(t, u, measure, project, attend, renorm, route, publish):
                if attend is not None:
                    ma, pa = attend
                    a = 2 * ma + pa
                    pe.wait_ge(xnt_ready, a + 1)
                    pe.wait_ge(kt_ready, a + 1)
                    pe.wait_ge(v_ready, a + 1)
                    at_least(pe, pt_ready, a)
                    for j in range(TJ):
                        for k in range(KD):
                            nc.tensor.matmul(b_s[:, j, :], xnt[:, k, j * P:(j + 1) * P], kt[:, k, :],
                                             start=(k == 0), stop=False)
                        ins = nc.tensor.matmul(b_s[:, j, :], ones[0:SK, :], s_diag[pa], start=False, stop=True)
                    ins.then_inc(s_mm, 1)
                if project is not None:
                    m, p = project
                    b = 2 * m + p
                    pe.wait_ge(ctx_loaded[p], 16 * (m + 1))
                    at_least(pe, kt_ready, b)
                    for k in range(KD):
                        ins = nc.tensor.transpose(b_ctxt[:, k, :], ctx_sb[p][0:SK, k * P:(k + 1) * P], ident[0:SK, 0:SK])
                    ins.then_inc(ctxt_mm, 1)
                if route is not None:
                    mr, pr = route
                    r = 2 * mr + pr
                    pe.wait_ge(xn2_ready, r + 1)
                    pe.wait_ge(xnt_ready, min(t - 1, NB) if isinstance(t, int) else t - 1)
                    turned(b_x, xn2[pr], x2t_mm)
                if project is not None:
                    split_group(m, p, 0)
                if publish is not None:
                    mk, pk = publish
                    pe.wait_ge(chosen_ready, 2 * mk + pk + 1)
                    at_least(pe, seen_ready, 2 * mk + pk)
                    nc.tensor.matmul(b_rank[:, 0, :], before[:, :], chosen[:, 0, :], start=True, stop=False)
                    nc.tensor.matmul(b_rank[:, 0, :], ones_bf[:, :], seen[:, :], start=False, stop=True)
                    nc.tensor.matmul(b_rank[:, 1, :], before[:, :], chosen[:, 1, :], start=True, stop=False)
                    nc.tensor.matmul(b_rank[:, 1, :], ones_bf[:, :], chosen[:, 0, :], start=False, stop=False)
                    nc.tensor.matmul(b_rank[:, 1, :], ones_bf[:, :], seen[:, :], start=False, stop=True).then_inc(rank_mm, 1)
                if project is not None:
                    pe.wait_ge(ctxt_ready, b + 1)
                    at_least(pe, v_ready, b)
                    for cols in (slice(0, D), slice(D, D + 1)):
                        for k in range(KD):
                            ins = nc.tensor.matmul(b_v[:, cols], ctxt[:, k, :], wv_ext[:, k, cols],
                                                   start=(k == 0), stop=(k == KD - 1))
                    ins.then_inc(v_mm, 1)
                    pe.wait_ge(xn_ready, b + 1)
                    at_least(pe, xn2t_ready, b - 2)
                    turned(b_x, xn[p], xt_mm)
                if project is not None:
                    for c in range(KD):
                        for k in range(KD):
                            ins = nc.tensor.matmul(b_kt[:, c, :], mt[:, k, c * P:(c + 1) * P], ctxt[:, k, :],
                                                   start=(k == 0), stop=(k == KD - 1))
                    ins.then_inc(k_mm, 1)
                if attend is not None:
                    pe.wait_ge(exp_ready, a + 1)
                    for j in range(TJ):
                        ins = nc.tensor.transpose(b_pt[:, j, :], probs[:, j, :], ident[:, :])
                    ins.then_inc(pt_mm, 1)
                if project is not None:
                    split_group(m, p, 1)
                if route is not None:
                    pe.wait_ge(xn2t_ready, r + 1)
                    at_least(pe, slot_self, 5 * r - 4)
                    for j in range(TJ):
                        for k in range(KD):
                            ins = nc.tensor.matmul(b_lg[:, j, :], xn2t[:, k, j * P:(j + 1) * P], wrt[:, k, :],
                                                   start=(k == 0), stop=(k == KD - 1))
                    ins.then_inc(lg_mm, 1)
                if attend is not None:
                    pe.wait_ge(pt_ready, a + 1)
                    at_least(pe, x1_ready, a)
                    for j in range(TJ):
                        ins = nc.tensor.matmul(b_o[:, j, :], pt[:, j, :], v_sb[pa], start=True, stop=True)
                    ins.then_inc(o_mm, 1)
                if project is not None:
                    split_group(m, p, 2)
                    split_group(m, p, 3)

            steps(pe, step, 5)

            pe.wait_ge(seen_ready, NB)
            pe.wait_ge(slots_ready, NB)
            nc.tensor.matmul(bank[5][:, 0:E], ones_bf[:, :], seen[:, :], start=True, stop=True).then_inc(count_mm, 1)
            pe.wait_ge(xn2t_ready, NB)
            pe.wait_ge(wlo_ready, 4 * NB)
            pe.wait_ge(blocks_ready, 1)

            def turn(m, p):
                j = 2 * m + p
                pe.wait_ge(gathered[p], 16 * TB * (m + 1))
                at_least(pe, xlo_ready, j)
                for k in range(KD):
                    for t in range(TB):
                        ins = nc.tensor.transpose(f_x[:, k, t * P:(t + 1) * P], xg[p][:, t, k * P:(k + 1) * P], ident[:, :])
                ins.then_inc(xg_mm, 1)

            def weights_at(m, p):
                return pe.value_load(woff[0:1, bass.ds(2 * m + p, 1)], min_val=0, max_val=(E - 1) * WE)

            def up(m, p, at, after):
                j = 2 * m + p
                pe.wait_ge(xlo_ready, j + 1)
                for c in range(KF):
                    q = c // 2
                    dst = f_h[q][:, (c % 2) * BT:(c % 2 + 1) * BT]
                    if c % 2 == 0:
                        at_least(pe, gelu_ready, HB * (j - 1) + q + 1)
                    if c == KF - 3:
                        later = weights_at(*after)
                    for k in range(KD):
                        col = bass.ds(at + (c * D + k * P), P)
                        nc.tensor.matmul(dst, w1hi[:, col], xhi[:, k, :], start=(k == 0), stop=False)
                        nc.tensor.matmul(dst, w1hi[:, col], xlo[:, k, :], start=False, stop=False)
                        ins = nc.tensor.matmul(dst, w1lo[:, col], xhi[:, k, :], start=False, stop=(k == KD - 1))
                    if c % 2 == 1:
                        ins.then_inc(h_mm, 1)
                return later

            def down(m, p, at, after=None, turned=None):
                j = 2 * m + p
                later = None
                at_least(pe, y_ready, j)
                for c in range(KF):
                    if c == KF // 2 and turned is not None:
                        turn(*turned)
                    if c % 2 == 0:
                        pe.wait_ge(split_ready, HB * j + c // 2 + 1)
                    if c == KF - 3 and after is not None:
                        later = weights_at(*after)
                    col = bass.ds(at + c * D, D)
                    for t in range(TB):
                        h = slice(c * BT + t * P, c * BT + (t + 1) * P)
                        nc.tensor.matmul(f_y[t], hhi[:, h], w2hi[:, col], start=(c == 0), stop=False)
                        nc.tensor.matmul(f_y[t], hhi[:, h], w2lo[:, col], start=False, stop=False)
                        ins = nc.tensor.matmul(f_y[t], hlo[:, h], w2hi[:, col], start=False, stop=(c == KF - 1))
                    if c % 2 == 1:
                        ins.then_inc(y_mm, 1)
                return later

            def pair(m):
                at = up(m, 1, weights_at(m, 1), (m, 0))
                at = down(m, 0, at, (m + 1, 0), turned=(m + 1, 0))
                at = up(m + 1, 0, at, (m, 1))
                down(m, 1, at, turned=(m + 1, 1))

            LAST = BLOCKS // 2 - 1
            turn(0, 0)
            up(0, 0, weights_at(0, 0), (0, 1))
            turn(0, 1)
            pair(0)
            with pe.Fori(1, LAST) as m:
                pair(m)
            at = up(LAST, 1, weights_at(LAST, 1), (LAST, 0))
            at = down(LAST, 0, at, (LAST + 1, 0), turned=(LAST + 1, 0))
            at = up(LAST + 1, 0, at, (LAST, 1))
            down(LAST, 1, at)
            down(LAST + 1, 0, weights_at(LAST + 1, 0))

        @block.scalar
        def _(act):
            act.wait_ge(setup_mm, 2)
            for c in range(KD):
                nc.scalar.copy(mt[:, c, :], bank[c][:, 0:D])
                ins = nc.scalar.copy(wv_ext[:, c, 0:D], bank[2 + c][:, 0:D])
            ins.then_inc(setup_ev, 1)
            act.wait_ge(setup_mm, 3)
            nc.scalar.copy(wrt[:, :, :], bank[4][:, 0:KD * E].rearrange("p (k e) -> p k e", k=KD))
            nc.scalar.copy(b1t[:, :], bank[4][:, 64:64 + E * KF]).then_inc(setup_ev, 1)
            act.wait_ge(setup_mm, 5)
            nc.scalar.copy(wv_ext[:, :, D], bank[5][:, 0:2])
            nc.scalar.copy(g_col[:, :], bank[5][:, 2:4])
            nc.scalar.copy(c_col[:, :], bank[5][:, 4:5]).then_inc(setup_ev, 1)
            act.wait_ge(setup_ev, 3)
            nc.scalar.activation(ident_c[:, :], ident[:, :], ACT.Identity, scale=c_col[:, 0:1]).then_inc(setup_ev, 2)
            act.wait_ge(setup_ev, 5)

            def high_part(m, p, g):
                b = 2 * m + p
                act.wait_ge(w_mm, 4 * b + g + 1)
                dst = w2hi if p else w1hi
                nc.scalar.activation(dst[:, bass.ds(m * WE + g * 512, 512)], b_w[g % 2], ACT.Copy,
                                     scale=W_SCALE).then_inc(whi_ready, 1)

            def normalised(out, batch, u, which, done):
                for j in range(TJ):
                    ins = nc.scalar.activation(out[:, j, :], x1[:, bass.ds(batch, 1), j, :].rearrange("p a d -> p (a d)"),
                                               ACT.Identity, bias=rn[u][:, which, 1, j:j + 1], scale=rn[u][:, which, 0, j:j + 1])
                ins.then_inc(done, 1)

            def step(t, u, measure, project, attend, renorm, route, publish):
                if project is not None:
                    m, p = project
                    b = 2 * m + p
                    act.wait_ge(ctxt_mm, b + 1)
                    nc.scalar.copy(ctxt[:, :, :], b_ctxt).then_inc(ctxt_ready, 1)
                if route is not None:
                    mr, pr = route
                    r = 2 * mr + pr
                    act.wait_ge(x2t_mm, r + 1)
                    at_least(act, lg_mm, r)
                    nc.scalar.copy(xn2t[:, :, :], b_x).then_inc(xn2t_ready, 1)
                if attend is not None:
                    ma, pa = attend
                    a = 2 * ma + pa
                    act.wait_ge(max_ready, a + 1)
                    for j in range(TJ):
                        ins = nc.scalar.activation(probs[:, j, :], b_s[:, j, :], ACT.Exp, bias=neg[:, j:j + 1],
                                                   scale=SCALE, accum_out=psum_p[:, j:j + 1])
                    ins.then_inc(exp_ready, 1)
                if project is not None:
                    high_part(m, p, 0)
                    act.wait_ge(xt_mm, b + 1)
                    nc.scalar.copy(xnt[:, :, :], b_x).then_inc(xnt_ready, 1)
                if project is not None:
                    act.wait_ge(k_mm, b + 1)
                    for c in range(KD):
                        ins = nc.scalar.activation(kt[:, c, :], b_kt[:, c, :], ACT.Identity, bias=g_col[:, c:c + 1])
                    ins.then_inc(kt_ready, 1)
                if attend is not None:
                    act.wait_ge(pt_mm, a + 1)
                    nc.scalar.copy(pt[:, :, :], b_pt).then_inc(pt_ready, 1)
                if project is not None:
                    high_part(m, p, 1)
                if measure is not None:
                    mn, pn = measure
                    act.wait_ge(rn_ready, t + 1)
                    at_least(act, xt_mm, t - 1)
                    normalised(xn[pn], 2 * mn + pn, u, 0, xn_ready)
                if project is not None:
                    high_part(m, p, 2)
                if renorm is not None:
                    ms, ps = renorm
                    n = 2 * ms + ps
                    act.wait_ge(rn_ready, t + 1)
                    at_least(act, x2t_mm, n - 1)
                    at_least(act, xn2_stored[ps], 16 * ms)
                    normalised(xn2[ps], n, u, 1, xn2_ready)
                if project is not None:
                    high_part(m, p, 3)
                if renorm is not None:
                    act.wait_ge(xn2_ready, n + 1)
                    act.dma_start(tok_v[:, bass.ds(n, 1), :, :].rearrange("p a j d -> p (a j) d"), xn2[ps][:, :, :]).then_inc(xn2_stored[ps], 16)

            steps(act, step, 4)

            act.wait_ge(gate_diff, 1)
            nc.scalar.activation(gexp, gexp, ACT.Exp).then_inc(gate_exp, 1)
            nc.scalar.activation(c_col[:, :], c_col[:, :], ACT.Gelu)

            def x_high(m, p):
                j = 2 * m + p
                act.wait_ge(xg_mm, j + 1)
                at_least(act, h_mm, HB * j)
                nc.scalar.copy(xhi, f_x).then_inc(xhi_ready, 1)

            def gelu(m, p, q):
                j = 2 * m + p
                act.wait_ge(h_mm, HB * j + q + 1)
                if q == 0:
                    act.wait_ge(b1_staged, j + 1)
                at_least(act, split_ready, HB * (j - 1) + q + 1)
                for c in (2 * q, 2 * q + 1):
                    ins = nc.scalar.activation(h32[:, c * BT:(c + 1) * BT], f_h[q][:, (c % 2) * BT:(c % 2 + 1) * BT],
                                               ACT.Gelu, bias=b1s[p][:, c:c + 1], scale=1.0 / W_SCALE)
                ins.then_inc(gelu_ready, 1)

            def ahead(m1, p1, m2, p2):
                for q in range(HB):
                    gelu(m1, p1, q)
                x_high(m2, p2)

            x_high(0, 0)
            ahead(0, 0, 0, 1)
            ahead(0, 1, 1, 0)
            ahead(1, 0, 1, 1)
            with act.Fori(1, BLOCKS // 2 - 1) as m:
                ahead(m, 1, m + 1, 0)
                ahead(m + 1, 0, m + 1, 1)
            m = BLOCKS // 2 - 1
            ahead(m, 1, m + 1, 0)
            for q in range(HB):
                gelu(m + 1, 0, q)

            def normal(m, p):
                b = 2 * m + p
                act.wait_ge(rn3_ready, b + 1)
                at_least(act, zw_ready, b - 1)
                for j in range(TJ):
                    ins = nc.scalar.activation(zn_sb[p][:, j, :], z_sb[p][:, j, :], ACT.Identity,
                                               bias=rn3[p][:, 1, j:j + 1], scale=rn3[p][:, 0, j:j + 1])
                ins.then_inc(zn_ready, 1)

            normal(0, 0)
            normal(0, 1)
            with act.Fori(1, NB // 2) as m:
                normal(m, 0)
                normal(m, 1)

        @block.vector
        def _(dve):
            tick = [0]

            def chain(ins):
                tick[0] += 1
                ins.then_inc(dve_self, 1)
                dve.wait_ge(dve_self, tick[0])

            dve.wait_ge(small_loaded, 16 * N_SMALL)
            nc.vector.tensor_copy(bq_rep, bqk[:, 0, :].unsqueeze(2).to_broadcast([P, KD, P])).then_inc(bq_spread, 1)

            dve.wait_ge(setup_ev, 5)

            def low_part(m, p, g):
                b = 2 * m + p
                dve.wait_ge(whi_ready, 4 * b + g + 1)
                hi, lo = (w2hi, w2lo) if p else (w1hi, w1lo)
                col = bass.ds(m * WE + g * 512, 512)
                nc.vector.scalar_tensor_tensor(out=lo[:, col], in0=b_w[g % 2], scalar=W_SCALE, in1=hi[:, col],
                                               op0=ALU.mult, op1=ALU.subtract).then_inc(wlo_ready, 1)

            def rows_of(batch, j):
                return x1[:, bass.ds(batch, 1), j, :].rearrange("p a d -> p (a d)")

            def step(t, u, measure, project, attend, renorm, route, publish):
                m, p = project or (0, 0)
                ma, pa = attend or (0, 0)
                mr, pr = route or (0, 0)
                mk, pk = publish or (0, 0)
                b, a, r, k = 2 * m + p, 2 * ma + pa, 2 * mr + pr, 2 * mk + pk
                if attend is not None:
                    dve.wait_ge(s_mm, a + 1)
                    nc.vector.tensor_reduce(top[:, :], b_s, AX.X, ALU.max).then_inc(max_self, 1)
                if publish is not None:
                    dve.wait_ge(rank_mm, k + 1)
                    nc.vector.tensor_tensor(slot_e[:, :, :], b_rank, slot0[:, :].unsqueeze(1).to_broadcast([P, TJ, E]), ALU.add).then_inc(slot_self, 1)
                    dve.wait_ge(chosen_ready, k + 1)
                    nc.vector.tensor_tensor(seen[:, :], seen[:, :], chosen[:, 0, :], ALU.add).then_inc(slot_self, 1)
                if attend is not None:
                    dve.wait_ge(max_self, 2 * a + 1)
                    nc.vector.tensor_scalar(neg[:, :], top[:, :], -SCALE, None, ALU.mult).then_inc(max_ready, 1)
                measured = [(w, 2 * z[0] + z[1]) for w, z in enumerate((measure, renorm)) if z is not None]
                if measured:
                    at_least(dve, rn_ready, t - 1)
                    if measure is not None:
                        alone(dve, x_loaded[measure[1]], 16 * (measure[0] + 1), tally_dve)
                    if renorm is not None:
                        alone(dve, x1_ready, t - 2, tally_dve)
                    for w, n in measured:
                        for j in range(TJ):
                            ins = nc.vector.bn_stats(st[u][:, w, j, :], rows_of(n, j))
                    ins.then_inc(stats_self, 1)
                if publish is not None:
                    dve.wait_ge(slot_self, 5 * k + 2)
                    nc.vector.tensor_tensor(seen[:, :], seen[:, :], chosen[:, 1, :], ALU.add).then_inc(seen_ready, 1)
                    for j in range(TJ):
                        ins = nc.vector.tensor_tensor(prod[:, j, :, :], oh[:, j, :, :],
                                                      slot_e[:, j, :].unsqueeze(1).to_broadcast([P, TOPK, E]), ALU.mult)
                        ins.then_inc(slot_self, 1)
                if measured:
                    alone(dve, stats_self, t + 1, tally_dve)
                    for w, n in measured:
                        for j in range(TJ):
                            ins = nc.vector.bn_aggr(mv[u][:, w, j, :], st[u][:, w, j, :])
                    ins.then_inc(stats_ready, 1)
                if publish is not None:
                    dve.wait_ge(slot_self, 5 * k + 4)
                    nc.vector.tensor_reduce(slotf[:, :], prod[:, :, :, :].rearrange("p j k e -> p (j k) e"), AX.X, ALU.add).then_inc(slot_self, 1)
                if project is not None:
                    low_part(m, p, 0)
                if publish is not None:
                    at_least(dve, published[pk], ROUTED * mk)
                    dve.wait_ge(slot_self, 5 * k + 5)
                    nc.vector.tensor_copy(slots[pk][:, :], slotf[:, :]).then_inc(slots_ready, 1)
                if project is not None:
                    dve.wait_ge(v_mm, b + 1)
                    nc.vector.tensor_tensor(v_sb[p], b_v[:, 0:D], bv_bc[0:SK, :], ALU.add)
                    nc.vector.scalar_tensor_tensor(out=s_diag[p], in0=ident[0:SK, 0:SK], scalar=b_v[:, D:D + 1],
                                                   in1=ident_c[0:SK, 0:SK], op0=ALU.mult, op1=ALU.add).then_inc(v_ready, 1)
                if attend is not None:
                    dve.wait_ge(exp_ready, a + 1)
                    nc.vector.reciprocal(rinv[:, :], psum_p[:, :]).then_inc(max_self, 1)
                if route is not None:
                    dve.wait_ge(lg_mm, r + 1)
                    nc.vector.tensor_tensor(lg[:, :, :], b_lg, br_bc[:, :].unsqueeze(1).to_broadcast([P, TJ, E]), ALU.add).then_inc(top_self, 1)
                if project is not None:
                    low_part(m, p, 1)
                if route is not None:
                    alone(dve, top_self, 5 * r + 1, tally_dve)
                    for j in range(TJ):
                        ins = nc.vector.max(mx[:, j, :], lg[:, j, :])
                    ins.then_inc(top_self, 1)
                if attend is not None:
                    dve.wait_ge(o_mm, a + 1)
                    dve.wait_ge(max_self, 2 * a + 2)
                    for j in range(TJ):
                        ins = nc.vector.scalar_tensor_tensor(out=rows_of(a, j), in0=b_o[:, j, :], scalar=rinv[:, j:j + 1],
                                                             in1=rows_of(a, j), op0=ALU.mult, op1=ALU.add)
                    ins.then_inc(x1_ready, 1)
                if route is not None:
                    alone(dve, top_self, 5 * r + 2, tally_dve)
                    for j in range(TJ):
                        ins = nc.vector.max_index(ix[:, j, :], mx[:, j, :], lg[:, j, :])
                    ins.then_inc(top_self, 1)
                    nc.vector.tensor_copy(vals[:, bass.ds(r, 1), :, :].rearrange("p a j k -> p (a j) k"), mx[:, :, 0:TOPK])
                    dve.wait_ge(top_self, 5 * r + 3)
                    nc.vector.tensor_copy(ixf[:, :, :], ix[:, :, 0:TOPK]).then_inc(top_self, 1)
                if project is not None:
                    low_part(m, p, 2)
                if route is not None:
                    dve.wait_ge(top_self, 5 * r + 4)
                    nc.vector.tensor_tensor(oh[:, :, :, :].rearrange("p j k e -> p (j k) e"),
                                            iota8[:, :].unsqueeze(1).to_broadcast([P, TJ * TOPK, E]),
                                            ixf[:, :, :].rearrange("p j k -> p (j k)").unsqueeze(2).to_broadcast([P, TJ * TOPK, E]),
                                            ALU.is_equal).then_inc(top_self, 1)
                if route is not None:
                    dve.wait_ge(top_self, 5 * r + 5)
                    nc.vector.tensor_tensor(chosen[:, :, :], oh[:, :, 0, :], oh[:, :, 1, :], ALU.add).then_inc(chosen_ready, 1)
                if project is not None:
                    low_part(m, p, 3)

            steps(dve, step, 5)

            dve.wait_ge(count_mm, 1)
            chain(nc.vector.tensor_scalar(cnt, bank[5][:, 0:E], float(BT - 1), None, ALU.add))
            chain(nc.vector.tensor_scalar(nblk_i, cnt, BT.bit_length() - 1, None, ALU.arith_shift_right))
            chain(nc.vector.tensor_copy(nblk, nblk_i))
            chain(nc.vector.tensor_copy(endb[0], nblk))
            for s, d in enumerate((1, 2, 4)):
                nc.vector.tensor_copy(endb[s + 1][:, 0:d], endb[s][:, 0:d])
                chain(nc.vector.tensor_tensor(endb[s + 1][:, d:E], endb[s][:, d:E], endb[s][:, 0:E - d], ALU.add))
            ends = endb[3].unsqueeze(1).to_broadcast([P, BLOCKS, E])
            chain(nc.vector.tensor_tensor(passed, ends, jota[:, :].unsqueeze(2).to_broadcast([P, BLOCKS, E]), ALU.is_le))
            nc.vector.tensor_reduce(eidf, passed[:, :, 0:E - 1], AX.X, ALU.add)
            chain(nc.vector.tensor_tensor(skipped[:, :, 0:E - 1], passed[:, :, 0:E - 1],
                                          nblk[:, 0:E - 1].unsqueeze(1).to_broadcast([P, BLOCKS, E - 1]), ALU.mult))
            nc.vector.tensor_copy(eid[:, :], eidf)
            nc.vector.tensor_scalar(woff[:, :], eidf[0:1, :], float(WE), None, ALU.mult)
            chain(nc.vector.tensor_reduce(firstf, skipped[:, :, 0:E - 1], AX.X, ALU.add))
            chain(nc.vector.scalar_tensor_tensor(out=rowf, in0=eidf, scalar=float(PER_EXPERT), in1=jota[:, :],
                                                 op0=ALU.mult, op1=ALU.add))
            chain(nc.vector.tensor_tensor(firstf, rowf, firstf, ALU.subtract))
            nc.vector.tensor_copy(row[:, :], firstf[0:1, :]).then_inc(blocks_ready, 1)
            v2 = vals[:, :, :, :].rearrange("p b j k -> p (b j) k")
            g2 = gate[:, :, :, :].rearrange("p b j k -> p (b j) k")
            nc.vector.tensor_tensor(gexp, v2[:, :, 1], v2[:, :, 0], ALU.subtract).then_inc(gate_diff, 1)
            dve.wait_ge(gate_exp, 1)
            chain(nc.vector.tensor_scalar(gsum, gexp, 1.0, None, ALU.add))
            chain(nc.vector.reciprocal(g2[:, :, 0], gsum))
            nc.vector.tensor_tensor(g2[:, :, 1], gexp, g2[:, :, 0], ALU.mult)

            dve.wait_ge(shift_loaded, 16)
            dve.wait_ge(xn2_ready, NB)
            with dve.Fori(0, NB) as b:
                xb = x1[:, bass.ds(b, 1), :, :].rearrange("p a j d -> p (a j) d")
                nc.vector.tensor_tensor(xb, xb, lnb_bc[:, :].unsqueeze(1).to_broadcast([P, TJ, D]), ALU.add).then_inc(shift_added, 1)

            def x_low(m, p):
                j = 2 * m + p
                dve.wait_ge(xhi_ready, j + 1)
                nc.vector.tensor_tensor(xlo, f_x, xhi, ALU.subtract).then_inc(xlo_ready, 1)

            def split(m, p, parts=range(HB)):
                j = 2 * m + p
                for q in parts:
                    s = slice(q * 2 * BT, (q + 1) * 2 * BT)
                    dve.wait_ge(gelu_ready, HB * j + q + 1)
                    at_least(dve, y_mm, HB * (j - 1) + q + 1)
                    nc.vector.tensor_copy(hhi[:, s], h32[:, s]).then_inc(hhi_ready, 1)
                    dve.wait_ge(hhi_ready, HB * j + q + 1)
                    nc.vector.tensor_tensor(hlo[:, s], h32[:, s], hhi[:, s], ALU.subtract).then_inc(split_ready, 1)

            def y_out(m, p):
                j = 2 * m + p
                e = dve.value_load(eid[0:1, bass.ds(j, 1)], min_val=0, max_val=E - 1)
                dve.wait_ge(y_mm, HB * (j + 1))
                at_least(dve, scattered[p], 16 * TB * m)
                for t in range(TB):
                    ins = nc.vector.scalar_tensor_tensor(out=y_sb[p][:, t, :], in0=f_y[t], scalar=1.0 / W_SCALE,
                                                         in1=b2_bc[:, bass.ds(e * D, D)], op0=ALU.mult, op1=ALU.add)
                ins.then_inc(y_ready, 1)

            def ahead(m1, p1, m2, p2):
                split(m1, p1, range(HB // 2))
                x_low(m2, p2)
                split(m1, p1, range(HB // 2, HB))

            x_low(0, 0)
            x_low(0, 1)
            split(0, 0)
            ahead(0, 1, 1, 0)
            dve.wait_ge(late_loaded, 32)
            y_out(0, 0)
            ahead(1, 0, 1, 1)
            y_out(0, 1)
            with dve.Fori(1, BLOCKS // 2 - 1) as m:
                ahead(m, 1, m + 1, 0)
                y_out(m, 0)
                ahead(m + 1, 0, m + 1, 1)
                y_out(m, 1)
            m = BLOCKS // 2 - 1
            ahead(m, 1, m + 1, 0)
            y_out(m, 0)
            split(m + 1, 0)
            y_out(m, 1)
            y_out(m + 1, 0)

            def weigh(m, p):
                b = 2 * m + p
                dve.wait_ge(rows_loaded[p], 48 * (m + 1))
                at_least(dve, zn_ready, b - 1)
                for k, (rows, add) in enumerate(((first, residual[:, bass.ds(b, 1), :, :].rearrange("p a j d -> p (a j) d")), (second, z_sb[p]))):
                    for j in range(TJ):
                        ins = nc.vector.scalar_tensor_tensor(
                            out=z_sb[p][:, j, :], in0=rows[:, bass.ds(b, 1), j, :].rearrange("p a d -> p (a d)"),
                            scalar=gate[:, bass.ds(b, 1), j, k], in1=add[:, j, :], op0=ALU.mult, op1=ALU.add)
                        ins.then_inc(z_self, 1)
                    if k == 0:
                        dve.wait_ge(z_self, 4 * b + 2)
                alone(dve, rn3_ready, b - 1, tally_dve)
                dve.wait_ge(z_self, 4 * b + 4)
                for j in range(TJ):
                    ins = nc.vector.bn_stats(st3[p][:, j, :], z_sb[p][:, j, :])
                ins.then_inc(z_ready, 1)

            def measure_z(m, p):
                alone(dve, z_ready, 2 * m + p + 1, tally_dve)
                for j in range(TJ):
                    ins = nc.vector.bn_aggr(mv3[p][:, j, :], st3[p][:, j, :])
                ins.then_inc(stats3, 1)

            def affine(m, p):
                b = 2 * m + p
                dve.wait_ge(zn_ready, b + 1)
                at_least(dve, o_ready, b - 1)
                nc.vector.tensor_tensor(zw_sb[p], zn_sb[p], lnw_bc[:, :].unsqueeze(1).to_broadcast([P, TJ, D]),
                                        ALU.mult).then_inc(zw_ready, 1)

            weigh(0, 0)
            measure_z(0, 0)
            weigh(0, 1)
            measure_z(0, 1)
            weigh(1, 0)
            affine(0, 0)
            measure_z(1, 0)
            weigh(1, 1)
            affine(0, 1)
            measure_z(1, 1)
            with dve.Fori(2, NB // 2) as m:
                for p in range(2):
                    weigh(m, p)
                    affine(m - 1, p)
                    measure_z(m, p)
            affine(NB // 2 - 1, 0)
            affine(NB // 2 - 1, 1)


_INS = ['x', 'ctx_1024', 'L0_xattn_Wq', 'L0_xattn_bq', 'L0_xattn_Wk', 'L0_xattn_bk', 'L0_xattn_Wv', 'L0_xattn_bv',
        'L0_ffn_Wr', 'L0_ffn_br', 'L0_ffn_W1', 'L0_ffn_b1', 'L0_ffn_W2', 'L0_ffn_b2', 'L0_ffn_ln_w', 'L0_ffn_ln_b']
_OUTS = [((16, 256, 256), 'float32')]


def kernel(**inputs):
    import numpy as _np
    import concourse.bacc as _bacc
    from concourse import mybir as _mybir
    from concourse.bass_utils import run_bass_kernel_spmd as _run

    nc = _bacc.Bacc("TRN2", target_bir_lowering=False, num_devices=1)
    arrays, args = {}, []
    for name in _INS:
        a = _np.ascontiguousarray(inputs[name])
        arrays[f"in_{name}_dram"] = a
        args.append(nc.dram_tensor(f"in_{name}_dram", a.shape, _mybir.dt.from_np(a.dtype), kind="ExternalInput").ap())
    for i, (shape, dtype) in enumerate(_OUTS):
        dt = _mybir.dt.from_np(_np.dtype(dtype))
        args.append(nc.dram_tensor(f"out_{i}_dram", shape, dt, kind="ExternalOutput").ap())
    build(nc, *args)
    r = _run(nc, [arrays], core_ids=[0])
    got = tuple(r.results[0][f"out_{i}_dram"] for i in range(len(_OUTS)))
    return got[0]
```

```python
from contextlib import ExitStack

import concourse.bass as bass
from concourse import mybir

F32 = mybir.dt.float32
F16 = mybir.dt.float16
BF16 = mybir.dt.bfloat16
I32 = mybir.dt.int32
U32 = mybir.dt.uint32
ALU = mybir.AluOpType
ACT = mybir.ActivationFunctionType
AX = mybir.AxisListType

P = 128
EPS_LN = 1e-5
EPS_FFN = 1e-12
W_SCALE = 64.0


def at_least(eng, sem, n):
    if not (isinstance(n, int) and n <= 0):
        eng.wait_ge(sem, n)


def alone(eng, sem, n, tally):
    if not (isinstance(n, int) and n <= 0):
        eng.wait_ge(sem, n)
        eng.sem_inc(tally, 1)


def build(nc, x, ctx_in, Wq, bq, Wk, bk, Wv, bv, Wr, br, W1, b1, W2, b2, ln_w, ln_b, out):
    NB, SQ, D = x.shape
    SK = ctx_in.shape[1]
    E, FF, _ = W1.shape
    KD = D // P
    KF = FF // P
    TJ = SQ // P
    NT = NB * TJ
    TOK = NB * SQ
    TOPK = 2
    TB = 2
    BT = TB * P
    BLOCKS = TOPK * TOK // BT + E - 1
    PER_EXPERT = TOK // BT
    TABLE = E * PER_EXPERT + E
    UNITS = TABLE * TB
    SCALE = float(D) ** -0.5
    assert KD == 2 and TJ == 2 and NB == 2 * E and BLOCKS % 2 == 1 and SK <= P

    slot_table = nc.dram_tensor("slot_table", (UNITS * P, 2), I32).ap()
    tokens_dram = nc.dram_tensor("tokens_dram", (TOK, D), F32).ap()
    expert_rows = nc.dram_tensor("expert_rows", (TOPK * TOK + UNITS * P, D), F32).ap()

    x_v = x.rearrange("b (j p) d -> p b j d", p=P)
    out_v = out.rearrange("b (j p) d -> p b j d", p=P)
    ctx_v = ctx_in.rearrange("b s d -> s b d")
    w1_v = W1.rearrange("e (c p) d -> p e c d", p=P)
    w2_v = W2.rearrange("e (k p) f -> p e k f", p=P)
    tok_v = tokens_dram.rearrange("(b j p) d -> p b j d", p=P, j=TJ)
    first_v = expert_rows[0:TOK, :].rearrange("(b j p) d -> p b j d", p=P, j=TJ)
    second_v = expert_rows[TOK:2 * TOK, :].rearrange("(b j p) d -> p b j d", p=P, j=TJ)
    table_v = slot_table.rearrange("(t q) c -> t (q c)", q=P)

    with ExitStack() as stack:
        def sb(name, shape, dt=F32):
            return stack.enter_context(nc.sbuf_tensor(name, shape, dt))

        def sem(name):
            return stack.enter_context(nc.semaphore(name))

        def sem2(name):
            return [sem(f"{name}{i}") for i in range(2)]

        WE = KF * D
        w1hi = sb("w1hi", [P, E * WE], F16)
        w1lo = sb("w1lo", [P, E * WE], F16)
        w2hi = sb("w2hi", [P, E * WE], F16)
        w2lo = sb("w2lo", [P, E * WE], F16)
        x1 = sb("x1", [P, NB, TJ, D])
        ident = sb("ident", [P, P])
        ones = sb("ones", [P, P])
        before = sb("before", [P, P], BF16)
        ones_bf = sb("ones_bf", [P, P], BF16)
        iota8 = sb("iota8", [P, E])
        slot0 = sb("slot0", [P, E])
        minus_half = sb("minus_half", [P, 2, TJ])
        ids = sb("ids", [P, NT * TOPK, 2], I32)
        mt = sb("mt", [P, KD, D])
        wv_ext = sb("wv_ext", [P, KD, D + 1])
        wrt = sb("wrt", [P, KD, E])
        g_col = sb("g_col", [P, KD])
        ident_c = sb("ident_c", [P, P])
        bv_bc = sb("bv_bc", [P, D])
        br_bc = sb("br_bc", [P, E])
        b1t = sb("b1t", [P, E * KF])
        stage = [sb(f"stage{i}", [P, KF * D]) for i in range(2)]
        late_lo = w2lo[:, (E - 2) * WE:].bitcast(F32)
        late_hi = w2hi[:, (E - 2) * WE:].bitcast(F32)
        wqkv = late_lo[:, 0:3 * KD * D].rearrange("p (w k d) -> p w k d", w=3, k=KD)
        wr_in = late_hi[0:E, 0:D]
        b1_in = late_hi[0:E * KF, D:D + P]
        bqk = sb("bqk", [P, 2, KD])
        bq_rep = late_hi[:, 512:512 + KD * P].rearrange("p (k q) -> p k q", k=KD)
        c_col = sb("c_col", [P, 1])
        PADS = -(-UNITS // P)
        pad_rows = [late_hi[:, 1024 + 2 * P * i:1024 + 2 * P * (i + 1)].bitcast(I32).rearrange("p (q c) -> p q c", c=2)
                    for i in range(PADS)]
        ctx_sb = [sb(f"ctx_sb{i}", [P, D]) for i in range(2)]
        st = [sb(f"st{i}", [P, 2, TJ, 6]) for i in range(2)]
        mv = [sb(f"mv{i}", [P, 2, TJ, 2]) for i in range(2)]
        ve = [sb(f"ve{i}", [P, 2, TJ]) for i in range(2)]
        nmu = [sb(f"nmu{i}", [P, 2, TJ]) for i in range(2)]
        rn = [sb(f"rn{i}", [P, 2, 2, TJ]) for i in range(2)]
        rn2 = sb("rn2", [P, NB, 2, TJ])
        xn = [sb(f"xn{i}", [P, TJ, D]) for i in range(2)]
        xn2 = [sb(f"xn2_{i}", [P, TJ, D]) for i in range(2)]
        xnt = sb("xnt", [P, KD, SQ])
        work = sb("work", [P, KD * SQ + 2 * KD * SK + 2 * D + 2 * SK + TJ * SK + TJ * P])
        cut = [0]

        def piece(rows, cols):
            cut[0] += cols
            return work[0:rows, cut[0] - cols:cut[0]]

        xn2t = piece(P, KD * SQ).rearrange("p (k q) -> p k q", k=KD)
        ctxt = piece(P, KD * SK).rearrange("p (k s) -> p k s", k=KD)
        kt = piece(P, KD * SK).rearrange("p (k s) -> p k s", k=KD)
        v_sb = [piece(SK, D) for i in range(2)]
        s_diag = [piece(SK, SK) for i in range(2)]
        top = sb("top", [P, TJ])
        neg = sb("neg", [P, TJ])
        probs = piece(P, TJ * SK).rearrange("p (j s) -> p j s", j=TJ)
        psum_p = sb("psum_p", [P, TJ])
        rinv = sb("rinv", [P, TJ])
        pt = piece(SK, TJ * P).rearrange("p (j q) -> p j q", j=TJ)
        lg = sb("lg", [P, TJ, E])
        mx = sb("mx", [P, TJ, E])
        ix = sb("ix", [P, TJ, E], U32)
        ixf = sb("ixf", [P, TJ, TOPK])
        oh = sb("oh", [P, TJ, TOPK, E])
        chosen = sb("chosen", [P, TJ, E], BF16)
        seen = sb("seen", [P, E], BF16)
        slot_e = sb("slot_e", [P, TJ, E])
        prod = sb("prod", [P, TJ, TOPK, E])
        slotf = sb("slotf", [P, TJ * TOPK])
        slots = [sb(f"slots{i}", [P, TJ * TOPK], I32) for i in range(2)]
        rows_now = [sb(f"rows_now{i}", [P, TJ * TOPK, 2], I32) for i in range(2)]
        vals = sb("vals", [P, NB, TJ, TOPK])
        gate = sb("gate", [P, NB, TJ, TOPK])
        gexp = prod[:, :, :, :].rearrange("p j k e -> p (j k e)")[:, 0:NT]
        gsum = oh[:, :, :, :].rearrange("p j k e -> p (j k e)")[:, 0:NT]
        jota = sb("jota", [P, BLOCKS])
        passed = work[:, 0:BLOCKS * E].rearrange("p (t e) -> p t e", e=E)
        skipped = work[:, 1024:1024 + BLOCKS * E].rearrange("p (t e) -> p t e", e=E)
        endb = [work[:, 320 + E * i:320 + E * (i + 1)] for i in range(4)]
        cnt, nblk_i = (work[:, 400 + E * i:400 + E * (i + 1)].bitcast(I32) for i in range(2))
        nblk = work[:, 400 + 2 * E:400 + 3 * E]
        eidf = work[:, 600:600 + BLOCKS]
        firstf = work[:, 700:700 + BLOCKS]
        rowf = work[:, 800:800 + BLOCKS]
        eid = sb("eid", [P, BLOCKS], I32)
        woff = sb("woff", [1, BLOCKS], I32)
        row = sb("row", [1, BLOCKS], I32)
        idx_all = work[:, E * D:E * D + 2 * TB * BLOCKS].bitcast(I32).rearrange("p (t j c) -> p t j c", j=TB, c=2)
        gidx = [sb(f"gidx{i}", [P, TB], I32) for i in range(2)]
        sidx = [sb(f"sidx{i}", [P, TB], I32) for i in range(2)]
        b1s = [sb(f"b1s{i}", [P, KF]) for i in range(2)]
        b2_bc = work[:, 0:E * D]
        lnw_bc, lnb_bc = ctx_sb[0], ctx_sb[1]
        lnb_parts = ctx_sb[1][0:3, 0:D // 2].bitcast(BF16)
        lnb_split = [stage[1][0:3, D * i:D * i + D // 2].bitcast(BF16) for i in range(3)]
        lnb_rest = [stage[1][0:3, D * i:D * (i + 1)] for i in range(3, 7)]
        xg, y_sb = xn, xn2
        xparts = xnt[:, :, :].rearrange("p k q -> p (k q)").bitcast(F16).rearrange("p (i k q) -> p i k q", i=2, k=KD)
        xhi, xlo = xparts[:, 0, :, :], xparts[:, 1, :, :]
        h32 = stage[0][:, :]
        hhi = stage[1][:, 0:KF * P].bitcast(F16)
        hlo = stage[1][:, KF * P:2 * KF * P].bitcast(F16)
        def by_batch(t):
            return t[:, :].bitcast(F32).rearrange("p (b j d) -> p b j d", b=NB, j=TJ)

        first, second = by_batch(w1hi), by_batch(w2lo)
        w1lo_f = w1lo[:, :].bitcast(F32).rearrange("p (n d) -> p n d", d=D)
        z_sb = [w1lo_f[:, 2 * i:2 * i + 2, :] for i in range(2)]
        zn_sb = [w1lo_f[:, 4 + 2 * i:6 + 2 * i, :] for i in range(2)]
        zw_sb = [w1lo_f[:, 8 + 2 * i:10 + 2 * i, :] for i in range(2)]
        o_sb = [w1lo_f[:, 12 + 2 * i:14 + 2 * i, :] for i in range(2)]
        xf_sb = [w1lo_f[:, 26 + 2 * i:28 + 2 * i, :] for i in range(2)]
        st3 = [w1lo_f[:, 18 + i, 0:TJ * 6].rearrange("p (j s) -> p j s", j=TJ) for i in range(2)]
        mv3 = [w1lo_f[:, 21 + i, 0:TJ * 2].rearrange("p (j s) -> p j s", j=TJ) for i in range(2)]
        rn3 = [w1lo_f[:, 23 + i, 0:2 * TJ].rearrange("p (r j) -> p r j", r=2) for i in range(2)]

        bank = [stack.enter_context(nc.psum_tensor(f"bank{i}", [P, 512], F32)) for i in range(8)]
        b_x = bank[0][:, :].rearrange("p (k q) -> p k q", k=KD)
        b_ctxt = bank[1][:, 0:KD * SK].rearrange("p (k s) -> p k s", k=KD)
        b_kt = bank[1][:, 256:256 + KD * SK].rearrange("p (k s) -> p k s", k=KD)
        b_v = bank[2][0:SK, 0:D + 1]
        b_s = bank[3][:, 0:TJ * SK].rearrange("p (j s) -> p j s", j=TJ)
        b_pt = bank[3][0:SK, 256:512].rearrange("p (j q) -> p j q", j=TJ)
        b_o = bank[4][:, :].rearrange("p (j d) -> p j d", j=TJ)
        b_lg = bank[5][:, 0:TJ * E].rearrange("p (j e) -> p j e", j=TJ)
        b_rank = bank[5][:, 64:64 + TJ * E].rearrange("p (j e) -> p j e", j=TJ)
        b_w = [bank[6][:, :], bank[7][:, :]]
        f_h = bank[0:4]
        f_x = bank[4][:, :].rearrange("p (k q) -> p k q", k=KD)
        f_y = [bank[5 + t][:, 0:D] for t in range(TB)]
        b_out = [bank[i][:, :].rearrange("p (j d) -> p j d", j=TJ) for i in range(2)]
        HB = len(f_h)

        consts_pool = sem("consts_pool")
        pool_self = sem("pool_self")
        proj_w_loaded = sem("proj_w_loaded")
        small_loaded = sem("small_loaded")
        late_loaded = sem("late_loaded")
        shift_loaded = sem("shift_loaded")
        shift_split = sem("shift_split")
        table_blank = sem("table_blank")
        bq_spread = sem("bq_spread")
        setup_mm = sem("setup_mm")
        setup_ev = sem("setup_ev")
        x_loaded = sem2("x_loaded")
        ctx_loaded = sem2("ctx_loaded")
        w_loaded = sem2("w_loaded")
        dve_self = sem("dve_self")
        xn_ready = sem("xn_ready")
        stats_ready = sem("stats_ready")
        rn_ready = sem("rn_ready")
        rn2_kept = sem("rn2_kept")
        xn2_ready = sem("xn2_ready")
        xn2_stored = sem2("xn2_stored")
        ctxt_mm = sem("ctxt_mm")
        ctxt_ready = sem("ctxt_ready")
        k_mm = sem("k_mm")
        kt_ready = sem("kt_ready")
        v_mm = sem("v_mm")
        v_ready = sem("v_ready")
        xt_mm = sem("xt_mm")
        xnt_ready = sem("xnt_ready")
        s_mm = sem("s_mm")
        max_ready = sem("max_ready")
        exp_ready = sem("exp_ready")
        pt_mm = sem("pt_mm")
        pt_ready = sem("pt_ready")
        o_mm = sem("o_mm")
        x1_ready = sem("x1_ready")
        x2t_mm = sem("x2t_mm")
        xn2t_ready = sem("xn2t_ready")
        lg_mm = sem("lg_mm")
        chosen_ready = sem("chosen_ready")
        rank_mm = sem("rank_mm")
        slots_ready = sem("slots_ready")
        seen_ready = sem("seen_ready")
        rows_copied = sem("rows_copied")
        published = sem2("published")
        w_mm = sem("w_mm")
        whi_ready = sem("whi_ready")
        wlo_ready = sem("wlo_ready")
        count_mm = sem("count_mm")
        blocks_ready = sem("blocks_ready")
        gate_diff = sem("gate_diff")
        gate_exp = sem("gate_exp")
        idx_loaded = sem2("idx_loaded")
        gidx_ready = sem("gidx_ready")
        sidx_ready = sem("sidx_ready")
        b1_staged = sem("b1_staged")
        gathered = sem2("gathered")
        xg_mm = sem("xg_mm")
        xhi_ready = sem("xhi_ready")
        xlo_ready = sem("xlo_ready")
        h_mm = sem("h_mm")
        gelu_ready = sem("gelu_ready")
        hhi_ready = sem("hhi_ready")
        split_ready = sem("split_ready")
        y_mm = sem("y_mm")
        y_ready = sem("y_ready")
        scattered = sem2("scattered")
        rows_loaded = sem2("rows_loaded")
        xf_ready = sem("xf_ready")
        z_ready = sem("z_ready")
        out_mm = sem("out_mm")
        stats3 = sem("stats3")
        rn3_ready = sem("rn3_ready")
        zn_ready = sem("zn_ready")
        zw_ready = sem("zw_ready")
        o_ready = sem("o_ready")
        stored = sem2("stored")

        norm_self = sem("norm_self")
        tally_dve = sem("tally_dve")
        tally_pool = sem("tally_pool")
        stats_self = sem("stats_self")
        max_self = sem("max_self")
        top_self = sem("top_self")
        slot_self = sem("slot_self")
        z_self = sem("z_self")

        block = stack.enter_context(nc.Block())

        N_SMALL = 6
        PEEL = 8
        GROUPS = 3
        LATE = 4
        SLOTS = (1, 3)
        ROUTED = 64

        def group_of(t, project, i):
            if project is not None and i < GROUPS:
                m, p = project
                return GROUPS * (2 * m + p) + i, (i + p) % 2, p, p, m, i, i == 0
            if not isinstance(t, int) or t <= NB:
                return None
            if t > NB + 4:
                r = t - NB - 3
            elif i in SLOTS:
                r, i = divmod(2 * (t - NB - 1) + SLOTS.index(i), 4)
            else:
                return None
            return GROUPS * NB + 4 * r + i, i % 2, r % 2, r // 2, 4 * (r % 2) + i, GROUPS, i == 0

        def late_groups(do, first, end):
            for n in range(first, end):
                do(NB + 5 + n // 4, None, n % 4)

        def steps(eng, step, last):
            def one(m, u):
                back = []
                for d in range(6):
                    t = 2 * m + u
                    inside = not isinstance(t, int) or 0 <= t - d < NB
                    back.append((m - (d + 1 - u) // 2, (u + d) % 2) if inside else None)
                step(2 * m + u, u, *back)
            for t in range(PEEL):
                one(t // 2, t % 2)
            with eng.Fori(PEEL // 2, NB // 2) as m:
                one(m, 0)
                one(m, 1)
            for t in range(NB, NB + last):
                one(t // 2, t % 2)

        @block.sync
        def _(sp):
            def load_rows_in(m, p):
                b = 2 * m + p
                at_least(sp, x_loaded[p], 16 * m)
                sp.dma_start(x1[:, bass.ds(b, 1), :, :].rearrange("p a j d -> p (a j) d"), x_v[:, bass.ds(b, 1), :, :].rearrange("p a j d -> p (a j) d")).then_inc(x_loaded[p], 16)
                at_least(sp, ctxt_mm, b - 1)
                sp.dma_start(ctx_sb[p][0:SK, :], ctx_v[:, bass.ds(b, 1), :].rearrange("p a d -> p (a d)")).then_inc(ctx_loaded[p], 16)

            def load_weights(m, p):
                b = 2 * m + p
                at_least(sp, w_mm, GROUPS * (b - 1))
                if p:
                    dst = stage[1][:, :].rearrange("p (k f) -> p k f", k=KD)[:, :, 0:GROUPS * 2 * P]
                    src = w2_v[:, bass.ds(m, 1), :, 0:GROUPS * 2 * P]
                else:
                    dst = stage[0][:, 0:GROUPS * 2 * D].rearrange("p (c d) -> p c d", d=D)
                    src = w1_v[:, bass.ds(m, 1), 0:GROUPS * 2, :]
                sp.dma_start(dst, src.rearrange("p a c d -> p (a c) d")).then_inc(w_loaded[p], 16)

            def load_late(r):
                sp.wait_ge(w_mm, GROUPS * (NB - 1) if r == 0 else GROUPS * NB + 4 * (r - 1))
                e = slice(4 * (r % 2), 4 * (r % 2) + 4)
                if r < 2:
                    dst = stage[r % 2][:, :].rearrange("p (e c d) -> p e c d", e=4, d=D)
                    src = w1_v[:, e, GROUPS * 2:, :]
                else:
                    dst = stage[r % 2][:, :].rearrange("p (e k f) -> p e k f", e=4, k=KD)
                    src = w2_v[:, e, :, GROUPS * 2 * P:]
                for a in range(4):
                    ins = sp.dma_start(dst[:, a], src[:, a]).then_inc(w_loaded[r % 2], 16)

            for w, src in enumerate((Wq, Wk, Wv)):
                sp.dma_start(wqkv[:, w, :, :], src.rearrange("(k p) d -> p k d", p=P)).then_inc(proj_w_loaded, 16)
            with nc.allow_non_contiguous_dma(reason="two short bias columns"):
                sp.dma_start(bqk[:, 0, :], bq.rearrange("(k p) -> p k", p=P)).then_inc(small_loaded, 16)
                sp.dma_start(bqk[:, 1, :], bk.rearrange("(k p) -> p k", p=P)).then_inc(small_loaded, 16)
            sp.dma_start(wr_in, Wr).then_inc(small_loaded, 16)
            sp.dma_start(b1_in, b1.rearrange("e (c p) -> (e c) p", p=P)).then_inc(small_loaded, 16)
            sp.dma_start(bv_bc[:, :], bv.partition_broadcast(P)).then_inc(small_loaded, 16)
            sp.dma_start(br_bc[:, :], br.partition_broadcast(P)).then_inc(small_loaded, 16)
            load_rows_in(0, 0)
            load_weights(0, 0)
            load_rows_in(0, 1)
            sp.wait_ge(consts_pool, 1)
            for i in range(PADS):
                n = min(P, UNITS - i * P)
                sp.dma_start(table_v[i * P:i * P + n, :], pad_rows[i][0:n].rearrange("p q c -> p (q c)")).then_inc(table_blank, 16)

            load_weights(0, 1)

            def step(t, u, measure, project, attend, renorm, route, publish):
                ahead = measure is not None and not (isinstance(t, int) and t < 2)
                if ahead:
                    load_rows_in(*measure)
                if isinstance(t, int) and t in (NB, NB + 1, NB + 3):
                    load_late((NB, NB + 1, NB + 3).index(t))
                if route is not None:
                    mr, pr = route
                    r = 2 * mr + pr
                    sp.wait_ge(xn2_ready, r + 1)
                    sp.dma_start(tok_v[:, bass.ds(r, 1), :, :].rearrange("p a j d -> p (a j) d"), xn2[pr][:, :, :]).then_inc(xn2_stored[pr], 16)
                if ahead:
                    load_weights(*measure)

            steps(sp, step, 4)

            load_late(3)
            sp.wait_ge(ctxt_mm, NB)
            sp.dma_start(lnb_bc[:, :], ln_b.partition_broadcast(P)).then_inc(shift_loaded, 16)
            for p in range(2):
                sp.wait_ge(published[p], ROUTED * NB // 2)
            sp.wait_ge(blocks_ready, 1)

            def load_rows(m, p):
                j = 2 * m + p
                at_least(sp, idx_loaded[p], 16 * m)
                r = sp.value_load(row[0:1, bass.ds(j, 1)], min_val=0, max_val=TABLE - 1)
                sp.dma_start(idx_all[:, bass.ds(j, 1), :, :].rearrange("p a j c -> p (a j c)"),
                             slot_table[bass.ds(r * BT, BT), :].rearrange("(p j) c -> p (j c)", j=TB)).then_inc(idx_loaded[p], 16)

            for p in range(2):
                load_rows(0, p)
            for p in range(2):
                load_rows(1, p)
            for p in range(2):
                sp.wait_ge(gathered[p], 16 * TB)
            sp.dma_start(b2_bc, b2.rearrange("e d -> (e d)").partition_broadcast(P)).then_inc(late_loaded, 16)
            sp.dma_start(lnw_bc[:, :], ln_w.partition_broadcast(P)).then_inc(late_loaded, 16)
            with sp.Fori(2, BLOCKS // 2) as m:
                load_rows(m, 0)
                load_rows(m, 1)
            load_rows(BLOCKS // 2, 0)

            sp.wait_ge(y_mm, HB * BLOCKS)
            sp.wait_ge(scattered[0], 16 * TB * (BLOCKS // 2 + 1))
            sp.wait_ge(scattered[1], 16 * TB * (BLOCKS // 2))

            def load_pair(m, p):
                at_least(sp, rows_loaded[p], 32 * m)
                for dst, src in ((first, first_v), (second, second_v)):
                    sp.dma_start(dst[:, bass.ds(2 * m + p, 1), :, :].rearrange("p a j d -> p (a j) d"),
                                 src[:, bass.ds(2 * m + p, 1), :, :].rearrange("p a j d -> p (a j) d")).then_inc(rows_loaded[p], 16)

            for m in range(2):
                for p in range(2):
                    load_pair(m, p)
            with sp.Fori(2, NB // 2) as m:
                for p in range(2):
                    load_pair(m, p)
            for p in range(2):
                sp.wait_ge(stored[p], 16 * NB // 2)

        @block.gpsimd
        def _(pool):
            for i in range(PADS):
                nc.gpsimd.iota(pad_rows[i][:, :, 0], [[1, P]], base=0, channel_multiplier=0)
                ins = nc.gpsimd.iota(pad_rows[i][:, :, 1], [[1, P]], base=TOPK * TOK + i * P * P, channel_multiplier=P)
            ins.then_inc(consts_pool, 1)
            nc.gpsimd.memset(ident[:, :], 0.0)
            nc.gpsimd.memset(before[:, :], 1.0)
            nc.gpsimd.memset(ones[:, :], 1.0)
            nc.gpsimd.memset(ones_bf[:, :], 1.0)
            nc.gpsimd.memset(seen[:, :], 0.0)
            nc.gpsimd.memset(minus_half[:, :, :], -0.5).then_inc(pool_self, 1)
            pool.wait_ge(pool_self, 1)
            nc.gpsimd.affine_select(out=ident[:, :], in_=ident[:, :], compare_op=ALU.not_equal, fill=1.0, base=0,
                                    pattern=[[-1, P]], channel_multiplier=1)
            nc.gpsimd.affine_select(out=before[:, :], in_=before[:, :], compare_op=ALU.is_gt, fill=0.0, base=0,
                                    pattern=[[1, P]], channel_multiplier=-1)
            nc.gpsimd.iota(iota8[:, :], [[1, E]], base=0, channel_multiplier=0, allow_small_or_imprecise_dtypes=True)
            nc.gpsimd.iota(slot0[:, :], [[TOK, E]], base=0, channel_multiplier=0, allow_small_or_imprecise_dtypes=True)
            nc.gpsimd.iota(jota[:, :], [[1, BLOCKS]], base=0, channel_multiplier=0, allow_small_or_imprecise_dtypes=True)
            nc.gpsimd.iota(ids[:, :, 0], [[P, NT], [0, TOPK]], base=0, channel_multiplier=1)
            nc.gpsimd.iota(ids[:, :, 1], [[P, NT], [TOK, TOPK]], base=0, channel_multiplier=1).then_inc(consts_pool, 1)

            tick = [1]

            def then_self(ins):
                tick[0] += 1
                ins.then_inc(pool_self, 1)
                pool.wait_ge(pool_self, tick[0])

            def norm(count, mean, var, nmu, ve, half, scale, shift, eps, ready):
                nc.gpsimd.tensor_scalar(nmu, mean, -1.0, None, ALU.mult)
                nc.gpsimd.tensor_scalar(ve, var, eps, None, ALU.add).then_inc(norm_self, 1)
                pool.wait_ge(norm_self, 2 * count + 1)
                nc.gpsimd.tensor_tensor(scale, ve, half, ALU.pow).then_inc(norm_self, 1)
                pool.wait_ge(norm_self, 2 * count + 2)
                nc.gpsimd.tensor_tensor(shift, nmu, scale, ALU.mult).then_inc(ready, 1)

            def step(t, u, measure, project, attend, renorm, route, publish):
                if measure is not None or renorm is not None:
                    w = slice(0 if measure is not None else 1, 2 if renorm is not None else 1)
                    at_least(pool, xn_ready, min(t - 1, NB) if isinstance(t, int) else t - 1)
                    at_least(pool, xn2_ready, t - 4)
                    alone(pool, stats_ready, t + 1, tally_pool)
                    norm(t, mv[u][:, w, :, 0], mv[u][:, w, :, 1], nmu[u][:, w, :], ve[u][:, w, :], minus_half[:, w, :],
                         rn[u][:, w, 0, :], rn[u][:, w, 1, :], EPS_LN, rn_ready)
                if renorm is not None:
                    m, p = renorm
                    alone(pool, rn_ready, t + 1, tally_pool)
                    nc.gpsimd.tensor_copy(rn2[:, bass.ds(2 * m + p, 1), :, :].rearrange("p a r j -> p (a r) j"),
                                          rn[u][:, 1, :, :]).then_inc(rn2_kept, 1)
                if publish is not None:
                    m, p = publish
                    b = 2 * m + p
                    n = TJ * TOPK
                    if isinstance(b, int) and b == 0:
                        pool.wait_ge(table_blank, 16 * PADS)
                    at_least(pool, published[p], ROUTED * m)
                    nc.gpsimd.tensor_copy(rows_now[p][:, :, :], ids[:, bass.ds(b * n, n), :]).then_inc(rows_copied, 1)
                    pool.wait_ge(rows_copied, b + 1)
                    alone(pool, slots_ready, b + 1, tally_pool)
                    for a in range(n):
                        nc.gpsimd.indirect_dma_start(
                            out=slot_table, out_offset=bass.IndirectOffsetOnAxis(ap=slots[p][:, a:a + 1], axis=0),
                            in_=rows_now[p][:, a, :], in_offset=None).then_inc(published[p], 16)

            steps(pool, step, 5)

            def fetch(m, p):
                j = 2 * m + p
                e = pool.value_load(eid[0:1, bass.ds(j, 1)], min_val=0, max_val=E - 1)
                pool.wait_ge(idx_loaded[p], 16 * (m + 1))
                at_least(pool, gathered[p], 16 * TB * m)
                nc.gpsimd.tensor_copy(gidx[p][:, :], idx_all[:, bass.ds(j, 1), :, 0].rearrange("p a j -> p (a j)")).then_inc(gidx_ready, 1)
                pool.wait_ge(gidx_ready, j + 1)
                alone(pool, xg_mm, j - 1, tally_pool)
                for t in range(TB):
                    nc.gpsimd.indirect_dma_start(
                        out=xg[p][:, t, :], out_offset=None, in_=tokens_dram,
                        in_offset=bass.IndirectOffsetOnAxis(ap=gidx[p][:, t:t + 1], axis=0)).then_inc(gathered[p], 16)
                at_least(pool, gelu_ready, HB * (j - 1))
                nc.gpsimd.tensor_copy(b1s[p][:, :], b1t[:, bass.ds(e * KF, KF)]).then_inc(b1_staged, 1)

            def give(m, p):
                j = 2 * m + p
                at_least(pool, scattered[p], 16 * TB * m)
                nc.gpsimd.tensor_copy(sidx[p][:, :], idx_all[:, bass.ds(j, 1), :, 1].rearrange("p a j -> p (a j)")).then_inc(sidx_ready, 1)
                pool.wait_ge(sidx_ready, j + 1)
                alone(pool, y_ready, j + 1, tally_pool)
                for t in range(TB):
                    nc.gpsimd.indirect_dma_start(
                        out=expert_rows, out_offset=bass.IndirectOffsetOnAxis(ap=sidx[p][:, t:t + 1], axis=0),
                        in_=y_sb[p][:, t, :], in_offset=None).then_inc(scattered[p], 16)

            pool.wait_ge(blocks_ready, 1)
            pool.wait_ge(setup_ev, 5)
            for p in range(2):
                pool.wait_ge(xn2_stored[p], 16 * NB // 2)
            for n in range(3):
                fetch(n // 2, n % 2)
            fetch(1, 1)
            give(0, 0)
            fetch(2, 0)
            give(0, 1)
            with pool.Fori(1, BLOCKS // 2 - 1) as m:
                fetch(m + 1, 1)
                give(m, 0)
                fetch(m + 2, 0)
                give(m, 1)
            m = BLOCKS // 2 - 1
            give(m, 0)
            give(m, 1)
            give(m + 1, 0)

            def finish(m, p):
                b = 2 * m + p
                at_least(pool, zn_ready, b - 1)
                alone(pool, rn3_ready, b, tally_pool)
                alone(pool, stats3, b + 1, tally_pool)
                norm(NB + 3 + b, mv3[p][:, :, 0], mv3[p][:, :, 1], nmu[0][:, 0, :], ve[0][:, 0, :], minus_half[:, 0, :],
                     rn3[p][:, 0, :], rn3[p][:, 1, :], EPS_FFN, rn3_ready)

            def affine(m, p):
                b = 2 * m + p
                pool.wait_ge(zn_ready, b + 1)
                at_least(pool, o_ready, b - 1)
                nc.gpsimd.tensor_tensor(zw_sb[p], zn_sb[p], lnw_bc[:, :].unsqueeze(1).to_broadcast([P, TJ, D]),
                                        ALU.mult).then_inc(zw_ready, 1)

            finish(0, 0)
            finish(0, 1)
            affine(0, 0)
            finish(1, 0)
            affine(0, 1)
            finish(1, 1)
            affine(1, 0)
            with pool.Fori(2, NB // 2) as m:
                finish(m, 0)
                affine(m - 1, 1)
                finish(m, 1)
                affine(m, 0)
            affine(NB // 2 - 1, 1)

        @block.tensor
        def _(pe):
            pe.wait_ge(consts_pool, 2)
            pe.wait_ge(proj_w_loaded, 48)
            wq, wk, wv = (wqkv[:, i, :, :] for i in range(3))
            for c in range(KD):
                for k in range(KD):
                    ins = nc.tensor.matmul(bank[c][:, 0:D], wk[:, k, c * P:(c + 1) * P], wq[:, k, :],
                                           start=(k == 0), stop=(k == KD - 1))
            ins.then_inc(setup_mm, 1)
            for k in range(KD):
                for c in range(KD):
                    ins = nc.tensor.transpose(bank[2 + c][:, k * P:(k + 1) * P], wv[:, k, c * P:(c + 1) * P], ident[:, :])
            ins.then_inc(setup_mm, 1)
            pe.wait_ge(small_loaded, 16 * N_SMALL)
            for c in range(KD):
                nc.tensor.transpose(bank[4][:, c * E:(c + 1) * E], wr_in[:, c * P:(c + 1) * P], ident[0:E, 0:E])
            nc.tensor.transpose(bank[4][:, 64:64 + E * KF], b1_in, ident[0:E * KF, 0:E * KF]).then_inc(setup_mm, 1)
            pe.wait_ge(bq_spread, 1)
            for c in range(KD):
                for k in range(KD):
                    nc.tensor.matmul(bank[5][:, c:c + 1], wk[:, k, c * P:(c + 1) * P], bqk[:, 0, k:k + 1],
                                     start=(k == 0), stop=(k == KD - 1))
            for c in range(KD):
                for k in range(KD):
                    nc.tensor.matmul(bank[5][:, 2 + c:3 + c], wq[:, k, c * P:(c + 1) * P], bqk[:, 1, k:k + 1],
                                     start=(k == 0), stop=(k == KD - 1))
            for k in range(KD):
                ins = nc.tensor.matmul(bank[5][:, 4:5], bq_rep[:, k, :], bqk[:, 1, k:k + 1],
                                       start=(k == 0), stop=(k == KD - 1))
            ins.then_inc(setup_mm, 2)
            pe.wait_ge(setup_ev, 5)

            def transpose_group(t, project, i):
                if group_of(t, project, i) is None:
                    return
                n, w, p, second_w, e, g, starts = group_of(t, project, i)
                if starts:
                    pe.wait_ge(w_loaded[p], 16 * (e + 1) if project is not None else 16 * (E + 4 * (second_w + 1)))
                at_least(pe, wlo_ready, n - 1)
                for q in range(4):
                    c, k = q // 2, q % 2
                    if project is not None:
                        c += 2 * g
                        col = k * FF + c * P if second_w else c * D + k * P
                    else:
                        col = (e % 4) * 4 * P + (k * 2 * P + c * P if second_w else c * D + k * P)
                    ins = nc.tensor.transpose(b_w[w][:, q * P:(q + 1) * P], stage[p][:, col:col + P], ident[:, :])
                ins.then_inc(w_mm, 1)

            def turned(out, src, count):
                for k in range(KD):
                    for j in range(TJ):
                        ins = nc.tensor.transpose(out[:, k, j * P:(j + 1) * P], src[:, j, k * P:(k + 1) * P], ident[:, :])
                ins.then_inc(count, 1)

            def step(t, u, measure, project, attend, renorm, route, publish):
                if attend is not None:
                    ma, pa = attend
                    a = 2 * ma + pa
                    pe.wait_ge(xnt_ready, a + 1)
                    pe.wait_ge(kt_ready, a + 1)
                    pe.wait_ge(v_ready, a + 1)
                    at_least(pe, pt_ready, a)
                    for j in range(TJ):
                        for k in range(KD):
                            nc.tensor.matmul(b_s[:, j, :], xnt[:, k, j * P:(j + 1) * P], kt[:, k, :],
                                             start=(k == 0), stop=False)
                        ins = nc.tensor.matmul(b_s[:, j, :], ones[0:SK, :], s_diag[pa], start=False, stop=True)
                    ins.then_inc(s_mm, 1)
                if project is not None:
                    m, p = project
                    b = 2 * m + p
                    pe.wait_ge(ctx_loaded[p], 16 * (m + 1))
                    at_least(pe, kt_ready, b)
                    for k in range(KD):
                        ins = nc.tensor.transpose(b_ctxt[:, k, :], ctx_sb[p][0:SK, k * P:(k + 1) * P], ident[0:SK, 0:SK])
                    ins.then_inc(ctxt_mm, 1)
                transpose_group(t, project, 0)
                if route is not None:
                    mr, pr = route
                    r = 2 * mr + pr
                    pe.wait_ge(xn2_ready, r + 1)
                    pe.wait_ge(xnt_ready, min(t - 1, NB) if isinstance(t, int) else t - 1)
                    turned(b_x, xn2[pr], x2t_mm)
                if project is not None:
                    pe.wait_ge(ctxt_ready, b + 1)
                    at_least(pe, v_ready, b)
                    for cols in (slice(0, D), slice(D, D + 1)):
                        for k in range(KD):
                            ins = nc.tensor.matmul(b_v[:, cols], ctxt[:, k, :], wv_ext[:, k, cols],
                                                   start=(k == 0), stop=(k == KD - 1))
                    ins.then_inc(v_mm, 1)
                if publish is not None:
                    mk, pk = publish
                    pe.wait_ge(chosen_ready, 2 * mk + pk + 1)
                    at_least(pe, seen_ready, 2 * mk + pk)
                    nc.tensor.matmul(b_rank[:, 0, :], before[:, :], chosen[:, 0, :], start=True, stop=False)
                    nc.tensor.matmul(b_rank[:, 0, :], ones_bf[:, :], seen[:, :], start=False, stop=True)
                    nc.tensor.matmul(b_rank[:, 1, :], before[:, :], chosen[:, 1, :], start=True, stop=False)
                    nc.tensor.matmul(b_rank[:, 1, :], ones_bf[:, :], chosen[:, 0, :], start=False, stop=False)
                    nc.tensor.matmul(b_rank[:, 1, :], ones_bf[:, :], seen[:, :], start=False, stop=True).then_inc(rank_mm, 1)
                if project is not None:
                    pe.wait_ge(xn_ready, b + 1)
                    at_least(pe, xn2t_ready, b - 2)
                    turned(b_x, xn[p], xt_mm)
                if project is not None:
                    for c in range(KD):
                        for k in range(KD):
                            ins = nc.tensor.matmul(b_kt[:, c, :], mt[:, k, c * P:(c + 1) * P], ctxt[:, k, :],
                                                   start=(k == 0), stop=(k == KD - 1))
                    ins.then_inc(k_mm, 1)
                if attend is not None:
                    pe.wait_ge(exp_ready, a + 1)
                    for j in range(TJ):
                        ins = nc.tensor.transpose(b_pt[:, j, :], probs[:, j, :], ident[:, :])
                    ins.then_inc(pt_mm, 1)
                transpose_group(t, project, 1)
                if route is not None:
                    pe.wait_ge(xn2t_ready, r + 1)
                    at_least(pe, slot_self, 5 * r - 4)
                    for j in range(TJ):
                        for k in range(KD):
                            ins = nc.tensor.matmul(b_lg[:, j, :], xn2t[:, k, j * P:(j + 1) * P], wrt[:, k, :],
                                                   start=(k == 0), stop=(k == KD - 1))
                    ins.then_inc(lg_mm, 1)
                if attend is not None:
                    pe.wait_ge(pt_ready, a + 1)
                    at_least(pe, x1_ready, a)
                    for j in range(TJ):
                        ins = nc.tensor.matmul(b_o[:, j, :], pt[:, j, :], v_sb[pa], start=True, stop=True)
                    ins.then_inc(o_mm, 1)
                transpose_group(t, project, 2)
                transpose_group(t, project, 3)

            steps(pe, step, 5)

            pe.wait_ge(seen_ready, NB)
            pe.wait_ge(slots_ready, NB)
            nc.tensor.matmul(bank[5][:, 0:E], ones_bf[:, :], seen[:, :], start=True, stop=True).then_inc(count_mm, 1)
            late_groups(transpose_group, 0, 8)
            pe.wait_ge(blocks_ready, 1)

            def turn(m, p):
                j = 2 * m + p
                pe.wait_ge(gathered[p], 16 * TB * (m + 1))
                at_least(pe, xlo_ready, j)
                for k in range(KD):
                    for t in range(TB):
                        ins = nc.tensor.transpose(f_x[:, k, t * P:(t + 1) * P], xg[p][:, t, k * P:(k + 1) * P], ident[:, :])
                ins.then_inc(xg_mm, 1)

            def weights_at(m, p):
                return pe.value_load(woff[0:1, bass.ds(2 * m + p, 1)], min_val=0, max_val=(E - 1) * WE)

            def up(m, p, at, after):
                j = 2 * m + p
                pe.wait_ge(xlo_ready, j + 1)
                for c in range(KF):
                    q = c // 2
                    dst = f_h[q][:, (c % 2) * BT:(c % 2 + 1) * BT]
                    if c % 2 == 0:
                        at_least(pe, gelu_ready, HB * (j - 1) + q + 1)
                    if c == KF - 3:
                        later = weights_at(*after)
                    for k in range(KD):
                        col = bass.ds(at + (c * D + k * P), P)
                        nc.tensor.matmul(dst, w1hi[:, col], xhi[:, k, :], start=(k == 0), stop=False)
                        nc.tensor.matmul(dst, w1hi[:, col], xlo[:, k, :], start=False, stop=False)
                        ins = nc.tensor.matmul(dst, w1lo[:, col], xhi[:, k, :], start=False, stop=(k == KD - 1))
                    if c % 2 == 1:
                        ins.then_inc(h_mm, 1)
                return later

            def down(m, p, at, after=None, turned=None):
                j = 2 * m + p
                later = None
                at_least(pe, y_ready, j)
                for c in range(KF):
                    if c == KF // 2 and turned is not None:
                        turn(*turned)
                    if c % 2 == 0:
                        pe.wait_ge(split_ready, HB * j + c // 2 + 1)
                    if c == KF - 3 and after is not None:
                        later = weights_at(*after)
                    col = bass.ds(at + c * D, D)
                    for t in range(TB):
                        h = slice(c * BT + t * P, c * BT + (t + 1) * P)
                        nc.tensor.matmul(f_y[t], hhi[:, h], w2hi[:, col], start=(c == 0), stop=False)
                        nc.tensor.matmul(f_y[t], hhi[:, h], w2lo[:, col], start=False, stop=False)
                        ins = nc.tensor.matmul(f_y[t], hlo[:, h], w2hi[:, col], start=False, stop=(c == KF - 1))
                    if c % 2 == 1:
                        ins.then_inc(y_mm, 1)
                return later

            def pair(m):
                at = up(m, 1, weights_at(m, 1), (m, 0))
                at = down(m, 0, at, (m + 1, 0), turned=(m + 1, 0))
                at = up(m + 1, 0, at, (m, 1))
                down(m, 1, at, turned=(m + 1, 1))

            LAST = BLOCKS // 2 - 1
            turn(0, 0)
            pe.wait_ge(wlo_ready, GROUPS * NB + 4 * LATE)
            up(0, 0, weights_at(0, 0), (0, 1))
            turn(0, 1)
            pair(0)
            with pe.Fori(1, LAST) as m:
                pair(m)
            at = up(LAST, 1, weights_at(LAST, 1), (LAST, 0))
            at = down(LAST, 0, at, (LAST + 1, 0), turned=(LAST + 1, 0))
            at = up(LAST + 1, 0, at, (LAST, 1))
            down(LAST, 1, at)
            down(LAST + 1, 0, weights_at(LAST + 1, 0))

            pe.wait_ge(gelu_ready, HB * BLOCKS)
            pe.wait_ge(shift_split, 1)

            def sum_up(m, p):
                b = 2 * m + p
                at_least(pe, o_ready, b - 1)
                for j in range(TJ):
                    nc.tensor.matmul(b_out[p][:, j, :], ident[:, :], x1[:, bass.ds(b, 1), j, :].rearrange("p a d -> p (a d)"),
                                     start=True, stop=False)
                    ins = nc.tensor.matmul(b_out[p][:, j, :], ones_bf[0:3, :], lnb_parts, start=False, stop=True)
                ins.then_inc(out_mm, 1)

            sum_up(0, 0)
            sum_up(0, 1)
            with pe.Fori(1, NB // 2) as m:
                sum_up(m, 0)
                sum_up(m, 1)

        @block.scalar
        def _(act):
            act.wait_ge(setup_mm, 2)
            for c in range(KD):
                nc.scalar.copy(mt[:, c, :], bank[c][:, 0:D])
                ins = nc.scalar.copy(wv_ext[:, c, 0:D], bank[2 + c][:, 0:D])
            ins.then_inc(setup_ev, 1)
            act.wait_ge(setup_mm, 3)
            nc.scalar.copy(wrt[:, :, :], bank[4][:, 0:KD * E].rearrange("p (k e) -> p k e", k=KD))
            nc.scalar.copy(b1t[:, :], bank[4][:, 64:64 + E * KF]).then_inc(setup_ev, 1)
            act.wait_ge(setup_mm, 5)
            nc.scalar.copy(wv_ext[:, :, D], bank[5][:, 0:2])
            nc.scalar.copy(g_col[:, :], bank[5][:, 2:4])
            nc.scalar.copy(c_col[:, :], bank[5][:, 4:5]).then_inc(setup_ev, 1)
            act.wait_ge(setup_ev, 3)
            nc.scalar.activation(ident_c[:, :], ident[:, :], ACT.Identity, scale=c_col[:, 0:1]).then_inc(setup_ev, 2)
            act.wait_ge(setup_ev, 5)
            act.wait_ge(table_blank, 16 * PADS)

            def high_part(t, project, i):
                if group_of(t, project, i) is None:
                    return
                n, w, p, second_w, e, g, starts = group_of(t, project, i)
                act.wait_ge(w_mm, n + 1)
                dst = w2hi if second_w else w1hi
                nc.scalar.activation(dst[:, bass.ds(e * WE + g * 512, 512)], b_w[w], ACT.Copy,
                                     scale=W_SCALE).then_inc(whi_ready, 1)

            def normalised(out, batch, u, which, done):
                for j in range(TJ):
                    ins = nc.scalar.activation(out[:, j, :], x1[:, bass.ds(batch, 1), j, :].rearrange("p a d -> p (a d)"),
                                               ACT.Identity, bias=rn[u][:, which, 1, j:j + 1], scale=rn[u][:, which, 0, j:j + 1])
                ins.then_inc(done, 1)

            def step(t, u, measure, project, attend, renorm, route, publish):
                if project is not None:
                    m, p = project
                    b = 2 * m + p
                    act.wait_ge(ctxt_mm, b + 1)
                    nc.scalar.copy(ctxt[:, :, :], b_ctxt).then_inc(ctxt_ready, 1)
                if route is not None:
                    mr, pr = route
                    r = 2 * mr + pr
                    act.wait_ge(x2t_mm, r + 1)
                    at_least(act, lg_mm, r)
                    nc.scalar.copy(xn2t[:, :, :], b_x).then_inc(xn2t_ready, 1)
                if attend is not None:
                    ma, pa = attend
                    a = 2 * ma + pa
                    act.wait_ge(max_ready, a + 1)
                    for j in range(TJ):
                        ins = nc.scalar.activation(probs[:, j, :], b_s[:, j, :], ACT.Exp, bias=neg[:, j:j + 1],
                                                   scale=SCALE, accum_out=psum_p[:, j:j + 1])
                    ins.then_inc(exp_ready, 1)
                high_part(t, project, 0)
                if project is not None:
                    act.wait_ge(xt_mm, b + 1)
                    nc.scalar.copy(xnt[:, :, :], b_x).then_inc(xnt_ready, 1)
                if project is not None:
                    act.wait_ge(k_mm, b + 1)
                    for c in range(KD):
                        ins = nc.scalar.activation(kt[:, c, :], b_kt[:, c, :], ACT.Identity, bias=g_col[:, c:c + 1])
                    ins.then_inc(kt_ready, 1)
                if attend is not None:
                    act.wait_ge(pt_mm, a + 1)
                    nc.scalar.copy(pt[:, :, :], b_pt).then_inc(pt_ready, 1)
                high_part(t, project, 1)
                if measure is not None:
                    mn, pn = measure
                    act.wait_ge(rn_ready, t + 1)
                    at_least(act, xt_mm, t - 1)
                    normalised(xn[pn], 2 * mn + pn, u, 0, xn_ready)
                high_part(t, project, 2)
                if renorm is not None:
                    ms, ps = renorm
                    n = 2 * ms + ps
                    act.wait_ge(rn_ready, t + 1)
                    at_least(act, x2t_mm, n - 1)
                    at_least(act, xn2_stored[ps], 16 * ms)
                    normalised(xn2[ps], n, u, 1, xn2_ready)
                high_part(t, project, 3)

            steps(act, step, 5)

            late_groups(high_part, 0, 2)
            act.wait_ge(gate_diff, 1)
            nc.scalar.activation(gexp, gexp, ACT.Exp).then_inc(gate_exp, 1)
            nc.scalar.activation(c_col[:, :], c_col[:, :], ACT.Gelu)

            late_groups(high_part, 2, 8)

            def x_high(m, p):
                j = 2 * m + p
                act.wait_ge(xg_mm, j + 1)
                at_least(act, h_mm, HB * j)
                nc.scalar.copy(xhi, f_x).then_inc(xhi_ready, 1)

            def gelu(m, p, q):
                j = 2 * m + p
                act.wait_ge(h_mm, HB * j + q + 1)
                if q == 0:
                    act.wait_ge(b1_staged, j + 1)
                at_least(act, split_ready, HB * (j - 1) + q + 1)
                for c in (2 * q, 2 * q + 1):
                    ins = nc.scalar.activation(h32[:, c * BT:(c + 1) * BT], f_h[q][:, (c % 2) * BT:(c % 2 + 1) * BT],
                                               ACT.Gelu, bias=b1s[p][:, c:c + 1], scale=1.0 / W_SCALE)
                ins.then_inc(gelu_ready, 1)

            def ahead(m1, p1, m2, p2):
                for q in range(HB):
                    gelu(m1, p1, q)
                x_high(m2, p2)

            x_high(0, 0)
            ahead(0, 0, 0, 1)
            ahead(0, 1, 1, 0)
            ahead(1, 0, 1, 1)
            with act.Fori(1, BLOCKS // 2 - 1) as m:
                ahead(m, 1, m + 1, 0)
                ahead(m + 1, 0, m + 1, 1)
            m = BLOCKS // 2 - 1
            ahead(m, 1, m + 1, 0)
            for q in range(HB):
                gelu(m + 1, 0, q)

            act.wait_ge(h_mm, HB * BLOCKS)
            act.wait_ge(rn2_kept, NB)

            def again(m, p):
                b = 2 * m + p
                at_least(act, z_ready, b - 1)
                for j in range(TJ):
                    ins = nc.scalar.activation(xf_sb[p][:, j, :], x1[:, bass.ds(b, 1), j, :].rearrange("p a d -> p (a d)"), ACT.Identity,
                                               bias=rn2[:, bass.ds(b, 1), 1, j], scale=rn2[:, bass.ds(b, 1), 0, j])
                ins.then_inc(xf_ready, 1)

            def normal(m, p):
                b = 2 * m + p
                act.wait_ge(rn3_ready, b + 1)
                at_least(act, zw_ready, b - 1)
                for j in range(TJ):
                    ins = nc.scalar.activation(zn_sb[p][:, j, :], z_sb[p][:, j, :], ACT.Identity,
                                               bias=rn3[p][:, 1, j:j + 1], scale=rn3[p][:, 0, j:j + 1])
                ins.then_inc(zn_ready, 1)

            def store(m, p):
                b = 2 * m + p
                act.wait_ge(o_ready, b + 1)
                act.dma_start(out_v[:, bass.ds(b, 1), :, :].rearrange("p a j d -> p (a j) d"), o_sb[p]).then_inc(stored[p], 16)

            again(0, 0)
            again(0, 1)
            for m in range(2):
                for p in range(2):
                    again(m + 1, p)
                    normal(m, p)
                    if m > 0:
                        store(m - 1, p)
            with act.Fori(2, NB // 2 - 1) as m:
                for p in range(2):
                    again(m + 1, p)
                    normal(m, p)
                    store(m - 1, p)
            m = NB // 2 - 1
            for p in range(2):
                normal(m, p)
                store(m - 1, p)
            for p in range(2):
                store(m, p)

        @block.vector
        def _(dve):
            tick = [0]

            def chain(ins):
                tick[0] += 1
                ins.then_inc(dve_self, 1)
                dve.wait_ge(dve_self, tick[0])

            dve.wait_ge(small_loaded, 16 * N_SMALL)
            nc.vector.tensor_copy(bq_rep, bqk[:, 0, :].unsqueeze(2).to_broadcast([P, KD, P])).then_inc(bq_spread, 1)

            def low_part(t, project, i):
                if group_of(t, project, i) is None:
                    return
                n, w, p, second_w, e, g, starts = group_of(t, project, i)
                dve.wait_ge(whi_ready, n + 1)
                hi, lo = (w2hi, w2lo) if second_w else (w1hi, w1lo)
                col = bass.ds(e * WE + g * 512, 512)
                nc.vector.scalar_tensor_tensor(out=lo[:, col], in0=b_w[w], scalar=W_SCALE, in1=hi[:, col],
                                               op0=ALU.mult, op1=ALU.subtract).then_inc(wlo_ready, 1)

            def rows_of(batch, j):
                return x1[:, bass.ds(batch, 1), j, :].rearrange("p a d -> p (a d)")

            def step(t, u, measure, project, attend, renorm, route, publish):
                m, p = project or (0, 0)
                ma, pa = attend or (0, 0)
                mr, pr = route or (0, 0)
                mk, pk = publish or (0, 0)
                b, a, r, k = 2 * m + p, 2 * ma + pa, 2 * mr + pr, 2 * mk + pk
                if attend is not None:
                    dve.wait_ge(s_mm, a + 1)
                    nc.vector.tensor_reduce(top[:, :], b_s, AX.X, ALU.max).then_inc(max_self, 1)
                if attend is not None:
                    dve.wait_ge(max_self, 2 * a + 1)
                    nc.vector.tensor_scalar(neg[:, :], top[:, :], -SCALE, None, ALU.mult).then_inc(max_ready, 1)
                measured = [(w, 2 * z[0] + z[1]) for w, z in enumerate((measure, renorm)) if z is not None]
                if measured:
                    at_least(dve, rn_ready, t - 1)
                    if measure is not None:
                        alone(dve, x_loaded[measure[1]], 16 * (measure[0] + 1), tally_dve)
                    if renorm is not None:
                        alone(dve, x1_ready, t - 2, tally_dve)
                    for w, n in measured:
                        for j in range(TJ):
                            ins = nc.vector.bn_stats(st[u][:, w, j, :], rows_of(n, j))
                    ins.then_inc(stats_self, 1)
                if publish is not None:
                    dve.wait_ge(rank_mm, k + 1)
                    nc.vector.tensor_tensor(slot_e[:, :, :], b_rank, slot0[:, :].unsqueeze(1).to_broadcast([P, TJ, E]), ALU.add).then_inc(slot_self, 1)
                    dve.wait_ge(chosen_ready, k + 1)
                    nc.vector.tensor_tensor(seen[:, :], seen[:, :], chosen[:, 0, :], ALU.add).then_inc(slot_self, 1)
                if publish is not None:
                    dve.wait_ge(slot_self, 5 * k + 2)
                    nc.vector.tensor_tensor(seen[:, :], seen[:, :], chosen[:, 1, :], ALU.add).then_inc(seen_ready, 1)
                    for j in range(TJ):
                        ins = nc.vector.tensor_tensor(prod[:, j, :, :], oh[:, j, :, :],
                                                      slot_e[:, j, :].unsqueeze(1).to_broadcast([P, TOPK, E]), ALU.mult)
                        ins.then_inc(slot_self, 1)
                if measured:
                    alone(dve, stats_self, t + 1, tally_dve)
                    for w, n in measured:
                        for j in range(TJ):
                            ins = nc.vector.bn_aggr(mv[u][:, w, j, :], st[u][:, w, j, :])
                    ins.then_inc(stats_ready, 1)
                if publish is not None:
                    dve.wait_ge(slot_self, 5 * k + 4)
                    nc.vector.tensor_reduce(slotf[:, :], prod[:, :, :, :].rearrange("p j k e -> p (j k) e"), AX.X, ALU.add).then_inc(slot_self, 1)
                low_part(t, project, 0)
                if publish is not None:
                    at_least(dve, published[pk], ROUTED * mk)
                    dve.wait_ge(slot_self, 5 * k + 5)
                    nc.vector.tensor_copy(slots[pk][:, :], slotf[:, :]).then_inc(slots_ready, 1)
                if project is not None:
                    dve.wait_ge(v_mm, b + 1)
                    if isinstance(b, int) and b == 0:
                        dve.wait_ge(setup_ev, 5)
                    nc.vector.tensor_tensor(v_sb[p], b_v[:, 0:D], bv_bc[0:SK, :], ALU.add)
                    nc.vector.scalar_tensor_tensor(out=s_diag[p], in0=ident[0:SK, 0:SK], scalar=b_v[:, D:D + 1],
                                                   in1=ident_c[0:SK, 0:SK], op0=ALU.mult, op1=ALU.add).then_inc(v_ready, 1)
                if attend is not None:
                    dve.wait_ge(exp_ready, a + 1)
                    nc.vector.reciprocal(rinv[:, :], psum_p[:, :]).then_inc(max_self, 1)
                if route is not None:
                    dve.wait_ge(lg_mm, r + 1)
                    nc.vector.tensor_tensor(lg[:, :, :], b_lg, br_bc[:, :].unsqueeze(1).to_broadcast([P, TJ, E]), ALU.add).then_inc(top_self, 1)
                low_part(t, project, 1)
                if route is not None:
                    alone(dve, top_self, 5 * r + 1, tally_dve)
                    for j in range(TJ):
                        ins = nc.vector.max(mx[:, j, :], lg[:, j, :])
                    ins.then_inc(top_self, 1)
                if attend is not None:
                    dve.wait_ge(o_mm, a + 1)
                    dve.wait_ge(max_self, 2 * a + 2)
                    for j in range(TJ):
                        ins = nc.vector.scalar_tensor_tensor(out=rows_of(a, j), in0=b_o[:, j, :], scalar=rinv[:, j:j + 1],
                                                             in1=rows_of(a, j), op0=ALU.mult, op1=ALU.add)
                    ins.then_inc(x1_ready, 1)
                if route is not None:
                    alone(dve, top_self, 5 * r + 2, tally_dve)
                    for j in range(TJ):
                        ins = nc.vector.max_index(ix[:, j, :], mx[:, j, :], lg[:, j, :])
                    ins.then_inc(top_self, 1)
                    nc.vector.tensor_copy(vals[:, bass.ds(r, 1), :, :].rearrange("p a j k -> p (a j) k"), mx[:, :, 0:TOPK])
                    dve.wait_ge(top_self, 5 * r + 3)
                    nc.vector.tensor_copy(ixf[:, :, :], ix[:, :, 0:TOPK]).then_inc(top_self, 1)
                low_part(t, project, 2)
                if route is not None:
                    dve.wait_ge(top_self, 5 * r + 4)
                    nc.vector.tensor_tensor(oh[:, :, :, :].rearrange("p j k e -> p (j k) e"),
                                            iota8[:, :].unsqueeze(1).to_broadcast([P, TJ * TOPK, E]),
                                            ixf[:, :, :].rearrange("p j k -> p (j k)").unsqueeze(2).to_broadcast([P, TJ * TOPK, E]),
                                            ALU.is_equal).then_inc(top_self, 1)
                if route is not None:
                    dve.wait_ge(top_self, 5 * r + 5)
                    nc.vector.tensor_tensor(chosen[:, :, :], oh[:, :, 0, :], oh[:, :, 1, :], ALU.add).then_inc(chosen_ready, 1)
                low_part(t, project, 3)

            steps(dve, step, 5)

            dve.wait_ge(count_mm, 1)
            chain(nc.vector.tensor_scalar(cnt, bank[5][:, 0:E], float(BT - 1), None, ALU.add))
            chain(nc.vector.tensor_scalar(nblk_i, cnt, BT.bit_length() - 1, None, ALU.arith_shift_right))
            chain(nc.vector.tensor_copy(nblk, nblk_i))
            chain(nc.vector.tensor_copy(endb[0], nblk))
            for s, d in enumerate((1, 2, 4)):
                nc.vector.tensor_copy(endb[s + 1][:, 0:d], endb[s][:, 0:d])
                chain(nc.vector.tensor_tensor(endb[s + 1][:, d:E], endb[s][:, d:E], endb[s][:, 0:E - d], ALU.add))
            ends = endb[3].unsqueeze(1).to_broadcast([P, BLOCKS, E])
            chain(nc.vector.tensor_tensor(passed, ends, jota[:, :].unsqueeze(2).to_broadcast([P, BLOCKS, E]), ALU.is_le))
            nc.vector.tensor_reduce(eidf, passed[:, :, 0:E - 1], AX.X, ALU.add)
            chain(nc.vector.tensor_tensor(skipped[:, :, 0:E - 1], passed[:, :, 0:E - 1],
                                          nblk[:, 0:E - 1].unsqueeze(1).to_broadcast([P, BLOCKS, E - 1]), ALU.mult))
            nc.vector.tensor_copy(eid[:, :], eidf)
            nc.vector.tensor_scalar(woff[:, :], eidf[0:1, :], float(WE), None, ALU.mult)
            chain(nc.vector.tensor_reduce(firstf, skipped[:, :, 0:E - 1], AX.X, ALU.add))
            chain(nc.vector.scalar_tensor_tensor(out=rowf, in0=eidf, scalar=float(PER_EXPERT), in1=jota[:, :],
                                                 op0=ALU.mult, op1=ALU.add))
            chain(nc.vector.tensor_tensor(firstf, rowf, firstf, ALU.subtract))
            nc.vector.tensor_copy(row[:, :], firstf[0:1, :]).then_inc(blocks_ready, 1)
            v2 = vals[:, :, :, :].rearrange("p b j k -> p (b j) k")
            g2 = gate[:, :, :, :].rearrange("p b j k -> p (b j) k")
            nc.vector.tensor_tensor(gexp, v2[:, :, 1], v2[:, :, 0], ALU.subtract).then_inc(gate_diff, 1)
            dve.wait_ge(gate_exp, 1)
            chain(nc.vector.tensor_scalar(gsum, gexp, 1.0, None, ALU.add))
            chain(nc.vector.reciprocal(g2[:, :, 0], gsum))
            nc.vector.tensor_tensor(g2[:, :, 1], gexp, g2[:, :, 0], ALU.mult)

            late_groups(low_part, 0, 8)
            def x_low(m, p):
                j = 2 * m + p
                dve.wait_ge(xhi_ready, j + 1)
                nc.vector.tensor_tensor(xlo, f_x, xhi, ALU.subtract).then_inc(xlo_ready, 1)

            def split(m, p, parts=range(HB)):
                j = 2 * m + p
                for q in parts:
                    s = slice(q * 2 * BT, (q + 1) * 2 * BT)
                    dve.wait_ge(gelu_ready, HB * j + q + 1)
                    at_least(dve, y_mm, HB * (j - 1) + q + 1)
                    nc.vector.tensor_copy(hhi[:, s], h32[:, s]).then_inc(hhi_ready, 1)
                    dve.wait_ge(hhi_ready, HB * j + q + 1)
                    nc.vector.tensor_tensor(hlo[:, s], h32[:, s], hhi[:, s], ALU.subtract).then_inc(split_ready, 1)

            def y_out(m, p):
                j = 2 * m + p
                e = dve.value_load(eid[0:1, bass.ds(j, 1)], min_val=0, max_val=E - 1)
                dve.wait_ge(y_mm, HB * (j + 1))
                at_least(dve, scattered[p], 16 * TB * m)
                for t in range(TB):
                    ins = nc.vector.scalar_tensor_tensor(out=y_sb[p][:, t, :], in0=f_y[t], scalar=1.0 / W_SCALE,
                                                         in1=b2_bc[:, bass.ds(e * D, D)], op0=ALU.mult, op1=ALU.add)
                ins.then_inc(y_ready, 1)

            def ahead(m1, p1, m2, p2):
                split(m1, p1, range(HB // 2))
                x_low(m2, p2)
                split(m1, p1, range(HB // 2, HB))

            x_low(0, 0)
            dve.wait_ge(shift_loaded, 16)
            left = lnb_bc[0:3, :]
            for i in range(3):
                chain(nc.vector.tensor_copy(lnb_split[i], left))
                if i < 2:
                    chain(nc.vector.tensor_tensor(lnb_rest[i], left, lnb_split[i], ALU.subtract))
                    left = lnb_rest[i]
            chain(nc.vector.tensor_scalar(lnb_rest[2], lnb_split[0], ident[0:3, 0:1], None, ALU.mult))
            chain(nc.vector.scalar_tensor_tensor(out=lnb_rest[3], in0=lnb_split[1], scalar=ident[0:3, 1:2], in1=lnb_rest[2],
                                                 op0=ALU.mult, op1=ALU.add))
            nc.vector.scalar_tensor_tensor(out=lnb_parts, in0=lnb_split[2], scalar=ident[0:3, 2:3], in1=lnb_rest[3],
                                           op0=ALU.mult, op1=ALU.add).then_inc(shift_split, 1)
            x_low(0, 1)
            split(0, 0)
            ahead(0, 1, 1, 0)
            dve.wait_ge(late_loaded, 32)
            y_out(0, 0)
            ahead(1, 0, 1, 1)
            y_out(0, 1)
            with dve.Fori(1, BLOCKS // 2 - 1) as m:
                ahead(m, 1, m + 1, 0)
                y_out(m, 0)
                ahead(m + 1, 0, m + 1, 1)
                y_out(m, 1)
            m = BLOCKS // 2 - 1
            ahead(m, 1, m + 1, 0)
            y_out(m, 0)
            split(m + 1, 0)
            y_out(m, 1)
            y_out(m + 1, 0)

            def weigh(m, p):
                b = 2 * m + p
                dve.wait_ge(rows_loaded[p], 32 * (m + 1))
                dve.wait_ge(xf_ready, b + 1)
                at_least(dve, zn_ready, b - 1)
                for k, (rows, add) in enumerate(((first, xf_sb[p]), (second, z_sb[p]))):
                    for j in range(TJ):
                        ins = nc.vector.scalar_tensor_tensor(
                            out=z_sb[p][:, j, :], in0=rows[:, bass.ds(b, 1), j, :].rearrange("p a d -> p (a d)"),
                            scalar=gate[:, bass.ds(b, 1), j, k], in1=add[:, j, :], op0=ALU.mult, op1=ALU.add)
                        ins.then_inc(z_self, 1)
                    if k == 0:
                        dve.wait_ge(z_self, 4 * b + 2)
                alone(dve, rn3_ready, b - 1, tally_dve)
                dve.wait_ge(z_self, 4 * b + 4)
                for j in range(TJ):
                    ins = nc.vector.bn_stats(st3[p][:, j, :], z_sb[p][:, j, :])
                ins.then_inc(z_ready, 1)

            def measure_z(m, p):
                alone(dve, z_ready, 2 * m + p + 1, tally_dve)
                for j in range(TJ):
                    ins = nc.vector.bn_aggr(mv3[p][:, j, :], st3[p][:, j, :])
                ins.then_inc(stats3, 1)

            def finish(m, p):
                b = 2 * m + p
                dve.wait_ge(zw_ready, b + 1)
                dve.wait_ge(out_mm, b + 1)
                at_least(dve, stored[p], 16 * m)
                nc.vector.tensor_tensor(o_sb[p], b_out[p], zw_sb[p], ALU.add).then_inc(o_ready, 1)

            for m in range(2):
                for p in range(2):
                    weigh(m, p)
                    if m > 0:
                        finish(m - 1, p)
                    measure_z(m, p)
            with dve.Fori(2, NB // 2) as m:
                for p in range(2):
                    weigh(m, p)
                    finish(m - 1, p)
                    measure_z(m, p)
            for p in range(2):
                finish(NB // 2 - 1, p)


_INS = ['x', 'ctx_1024', 'L0_xattn_Wq', 'L0_xattn_bq', 'L0_xattn_Wk', 'L0_xattn_bk', 'L0_xattn_Wv', 'L0_xattn_bv',
        'L0_ffn_Wr', 'L0_ffn_br', 'L0_ffn_W1', 'L0_ffn_b1', 'L0_ffn_W2', 'L0_ffn_b2', 'L0_ffn_ln_w', 'L0_ffn_ln_b']
_OUTS = [((16, 256, 256), 'float32')]


def kernel(**inputs):
    import numpy as _np
    import concourse.bacc as _bacc
    from concourse import mybir as _mybir
    from concourse.bass_utils import run_bass_kernel_spmd as _run

    nc = _bacc.Bacc("TRN2", target_bir_lowering=False, num_devices=1)
    arrays, args = {}, []
    for name in _INS:
        a = _np.ascontiguousarray(inputs[name])
        arrays[f"in_{name}_dram"] = a
        args.append(nc.dram_tensor(f"in_{name}_dram", a.shape, _mybir.dt.from_np(a.dtype), kind="ExternalInput").ap())
    for i, (shape, dtype) in enumerate(_OUTS):
        dt = _mybir.dt.from_np(_np.dtype(dtype))
        args.append(nc.dram_tensor(f"out_{i}_dram", shape, dt, kind="ExternalOutput").ap())
    build(nc, *args)
    r = _run(nc, [arrays], core_ids=[0])
    got = tuple(r.results[0][f"out_{i}_dram"] for i in range(len(_OUTS)))
    return got[0]
```
